# Optimizing a Trainium2 kernel written in Bass

```python
import numpy as np
import jax
import jax.numpy as jnp

def _softmax(x, axis=-1):
    return jax.nn.softmax(x, axis=axis)

def _gelu(x):
    return jax.nn.gelu(x, approximate=True)

def _silu(x):
    return jax.nn.silu(x)

def _sigmoid(x):
    return jax.nn.sigmoid(x)

def _layernorm(x, axis=-1, eps=1e-05):
    m = jnp.mean(x, axis=axis, keepdims=True)
    v = jnp.var(x, axis=axis, keepdims=True)
    return (x - m) / jnp.sqrt(v + eps)

def _scatter_add(tgt, idx, src, axis=0):
    return tgt.at[idx].add(src)

def _segment_sum(src, seg, n):
    return jax.ops.segment_sum(src, seg, n)
kernel_name = 'mk_adaln_ffn_d1_seqx_r8_1999ba'

def setup_inputs(seed: int=0):
    np.random.seed(seed)
    _w = jnp.asarray

    def _rec_inputs():
        import jax
        import jax.numpy as jnp
        _rk = jax.random.key(seed)
        x = -5.13e-06 + 0.01765 * jax.random.normal(jax.random.fold_in(_rk, 1), (2, 512, 128), jnp.float32)
        _lenS = 512 - jax.random.randint(jax.random.fold_in(_rk, 7), (2,), 0, max(1, 512 // 4) + 1, jnp.int32)
        _lenS2 = 512 - jax.random.randint(jax.random.fold_in(_rk, 8), (2,), 0, max(1, 512 // 4) + 1, jnp.int32)
        cond_1024 = 0.0061147 + 1.02565 * jax.random.normal(jax.random.fold_in(_rk, 11), (2, 128), jnp.float32)
        return (x, cond_1024)
    x, cond_1024 = _rec_inputs()

    def _L0_cond_setup():
        import math
        import jax, jax.numpy as jnp
        import numpy as np
        EPS = 1e-07
        MAX_TANH_ARG = 1.0 - 1e-05

        def _norm(x):
            return jnp.sqrt(jnp.sum(x * x, axis=-1, keepdims=True)).clip(EPS)

        def logmap0(x):
            n = _norm(x)
            return jnp.arctanh(jnp.clip(n, EPS, MAX_TANH_ARG)) * x / n

        def expmap0(v):
            n = _norm(v)
            return jnp.tanh(n) * v / n

        def mobius_add(x, y):
            x2 = jnp.sum(x * x, -1, keepdims=True)
            y2 = jnp.sum(y * y, -1, keepdims=True)
            xy = jnp.sum(x * y, -1, keepdims=True)
            num = (1 + 2 * xy + y2) * x + (1 - x2) * y
            den = (1 + 2 * xy + x2 * y2).clip(EPS)
            return num / den

        def plin(x, w, b):
            return expmap0(logmap0(x) @ w + b)

        def layer_norm(x, eps=1e-06):
            m = x.mean(-1, keepdims=True)
            v = ((x - m) ** 2).mean(-1, keepdims=True)
            return (x - m) / jnp.sqrt(v + eps)

        def _beta(a, b):
            return math.exp(math.lgamma(a) + math.lgamma(b) - math.lgamma(a + b))
        D, H, FF = (128, 16, 512)
        HD = D // H
        BETA_N = _beta(D / 2, 0.5)
        BETA_H = _beta(HD / 2, 0.5)

        def _to_heads(p):
            B, S, _ = p.shape
            t = logmap0(p).reshape(B, S, H, HD) * (BETA_H / BETA_N)
            return expmap0(jnp.transpose(t, (0, 2, 1, 3)))

        def _from_heads(ph):
            B, _, S, _ = ph.shape
            t = logmap0(ph) * (BETA_N / BETA_H)
            t = jnp.transpose(t, (0, 2, 1, 3)).reshape(B, S, D)
            return expmap0(t)
        key = jax.random.key(seed)
        ks = jax.random.split(key, 20)
        B, S = (4, 128)
        x = expmap0(0.02 * jax.random.normal(ks[0], (B, S, D), jnp.float32))
        t_emb = jax.random.normal(ks[1], (B, 1, D), jnp.float32)
        g = lambda k, sh: 0.02 * jax.random.normal(k, sh, jnp.float32)
        return {'x': x, 't_emb': t_emb, 'w_q': g(ks[2], (D, D)), 'b_q': jnp.zeros((D,), jnp.float32), 'w_k': g(ks[3], (D, D)), 'b_k': jnp.zeros((D,), jnp.float32), 'w_v': g(ks[4], (D, D)), 'b_v': jnp.zeros((D,), jnp.float32), 'w_o': g(ks[5], (D, D)), 'b_o': jnp.zeros((D,), jnp.float32), 'w_f1': g(ks[6], (D, FF)), 'b_f1': jnp.zeros((FF,), jnp.float32), 'w_f2': g(ks[7], (FF, D)), 'b_f2': jnp.zeros((D,), jnp.float32), 'w_ada': g(ks[8], (D, 6 * D)), 'b_ada': jnp.zeros((6 * D,), jnp.float32)}
    _L0_cond_all = _L0_cond_setup()
    _L0_cond_in = {k: v for k, v in _L0_cond_all.items() if k in ('w_q', 'b_q', 'w_k', 'b_k', 'w_v', 'b_v', 'w_o', 'b_o', 'w_f1', 'b_f1', 'w_f2', 'b_f2', 'w_ada', 'b_ada')}
    del _L0_cond_all

    def _L0_ffn_setup():
        import jax, jax.numpy as jnp
        import numpy as np
        DIM = 128
        DEPTH = 2
        HEADS = 8
        DIM_HEAD = 64
        WINDOW = 64
        INNER = HEADS * DIM_HEAD
        HID = int(DIM * 4 * 2 / 3)
        B, N = (2, 1024)
        QK_SCALE = 8.0

        def shift_token(t):
            t1, t2 = jnp.split(t, 2, axis=-1)
            t2 = jnp.pad(t2, ((0, 0), (1, 0), (0, 0)))[:, :-1]
            return jnp.concatenate([t1, t2], axis=-1)

        def l2norm(t):
            return t / jnp.clip(jnp.linalg.norm(t, axis=-1, keepdims=True), 1e-12)

        def rotate_half(x):
            x1, x2 = jnp.split(x, 2, axis=-1)
            return jnp.concatenate([-x2, x1], axis=-1)

        def rotary_xpos(q, k):
            n = q.shape[-2]
            half_idx = jnp.arange(0, DIM_HEAD, 2, dtype=jnp.float32)
            inv_freq = 1.0 / 10000.0 ** (half_idx / DIM_HEAD)
            t = jnp.arange(n, dtype=jnp.float32)
            freqs = t[:, None] * inv_freq[None, :]
            freqs = jnp.concatenate([freqs, freqs], axis=-1)
            base = (half_idx + 0.4 * DIM_HEAD) / (1.4 * DIM_HEAD)
            power = (t - n // 2) / float(WINDOW // 2)
            scale = base[None, :] ** power[:, None]
            scale = jnp.concatenate([scale, scale], axis=-1)
            cos, sin = (jnp.cos(freqs), jnp.sin(freqs))
            q = q * cos * scale + rotate_half(q) * sin * scale
            k = k * cos / scale + rotate_half(k) * sin / scale
            return (q, k)

        def local_attention(q, k, v):
            b, h, n, d = q.shape
            w = n // WINDOW
            bq = q.reshape(b, h, w, WINDOW, d) * QK_SCALE
            bk = k.reshape(b, h, w, WINDOW, d)
            bv = v.reshape(b, h, w, WINDOW, d)

            def look_around(t):
                p = jnp.pad(t, ((0, 0), (0, 0), (1, 0), (0, 0), (0, 0)))
                return jnp.concatenate([p[:, :, :w], p[:, :, 1:]], axis=3)
            bk, bv = (look_around(bk), look_around(bv))
            bt = jnp.arange(n).reshape(w, WINDOW)
            btp = jnp.pad(bt, ((1, 0), (0, 0)), constant_values=-1)
            btk = jnp.concatenate([btp[:w], btp[1:]], axis=1)
            sim = jnp.einsum('bhwid,bhwjd->bhwij', bq, bk)
            i = bt[:, :, None]
            j = btk[:, None, :]
            mask = (i < j) | (i > j + WINDOW) | (j == -1)
            sim = jnp.where(mask, -jnp.finfo(sim.dtype).max, sim)
            attn = jax.nn.softmax(sim, axis=-1)
            out = jnp.einsum('bhwij,bhwjd->bhwid', attn, bv)
            return out.reshape(b, h, n, d)

        def _layer(x, wqkv, qs, ksc, wo, lg, lb, w1, b1, w2, b2):
            b, n, _ = x.shape
            h = shift_token(x)
            qkv = h @ wqkv
            q, k, v = jnp.split(qkv, 3, axis=-1)
            to_heads = lambda t: t.reshape(b, n, HEADS, DIM_HEAD).transpose(0, 2, 1, 3)
            q, k, v = (to_heads(q), to_heads(k), to_heads(v))
            q = l2norm(q) * qs
            k = l2norm(k) * ksc
            q, k = rotary_xpos(q, k)
            o = local_attention(q, k, v)
            o = o.transpose(0, 2, 1, 3).reshape(b, n, INNER)
            x = x + o @ wo
            h = shift_token(x)
            mu = h.mean(-1, keepdims=True)
            var = h.var(-1, keepdims=True)
            h = (h - mu) / jnp.sqrt(var + 1e-05) * lg + lb
            h = h @ w1 + b1
            a, g = jnp.split(h, 2, axis=-1)
            h = a * jax.nn.gelu(g, approximate=False)
            x = x + h @ w2 + b2
            return x
        key = jax.random.key(seed)
        ks = jax.random.split(key, 6)
        return {'x': jax.random.normal(ks[0], (B, N, DIM), jnp.float32), 'wqkv': jax.random.normal(ks[1], (DEPTH, DIM, 3 * INNER), jnp.float32) * 0.02, 'q_scale': jnp.ones((DEPTH, DIM_HEAD), jnp.float32), 'k_scale': jnp.ones((DEPTH, DIM_HEAD), jnp.float32), 'wo': jax.random.normal(ks[2], (DEPTH, INNER, DIM), jnp.float32) * 0.02, 'ln_g': jnp.ones((DEPTH, DIM), jnp.float32), 'ln_b': jnp.zeros((DEPTH, DIM), jnp.float32), 'w1': jax.random.normal(ks[3], (DEPTH, DIM, 2 * HID), jnp.float32) * 0.02, 'b1': jnp.zeros((DEPTH, 2 * HID), jnp.float32), 'w2': jax.random.normal(ks[4], (DEPTH, HID, DIM), jnp.float32) * 0.02, 'b2': jnp.zeros((DEPTH, DIM), jnp.float32)}
    _L0_ffn_all = _L0_ffn_setup()
    _L0_ffn_in = {k: v for k, v in _L0_ffn_all.items() if k in ('wqkv', 'q_scale', 'k_scale', 'wo', 'ln_g', 'ln_b', 'w1', 'b1', 'w2', 'b2')}
    del _L0_ffn_all
    return {'x': x, 'cond_1024': cond_1024, 'L0_cond_w_q': _L0_cond_in['w_q'], 'L0_cond_b_q': _L0_cond_in['b_q'], 'L0_cond_w_k': _L0_cond_in['w_k'], 'L0_cond_b_k': _L0_cond_in['b_k'], 'L0_cond_w_v': _L0_cond_in['w_v'], 'L0_cond_b_v': _L0_cond_in['b_v'], 'L0_cond_w_o': _L0_cond_in['w_o'], 'L0_cond_b_o': _L0_cond_in['b_o'], 'L0_cond_w_f1': _L0_cond_in['w_f1'], 'L0_cond_b_f1': _L0_cond_in['b_f1'], 'L0_cond_w_f2': _L0_cond_in['w_f2'], 'L0_cond_b_f2': _L0_cond_in['b_f2'], 'L0_cond_w_ada': _L0_cond_in['w_ada'], 'L0_cond_b_ada': _L0_cond_in['b_ada'], 'L0_ffn_wqkv': _L0_ffn_in['wqkv'], 'L0_ffn_q_scale': _L0_ffn_in['q_scale'], 'L0_ffn_k_scale': _L0_ffn_in['k_scale'], 'L0_ffn_wo': _L0_ffn_in['wo'], 'L0_ffn_ln_g': _L0_ffn_in['ln_g'], 'L0_ffn_ln_b': _L0_ffn_in['ln_b'], 'L0_ffn_w1': _L0_ffn_in['w1'], 'L0_ffn_b1': _L0_ffn_in['b1'], 'L0_ffn_w2': _L0_ffn_in['w2'], 'L0_ffn_b2': _L0_ffn_in['b2']}

def reference(x, cond_1024, L0_cond_w_q, L0_cond_b_q, L0_cond_w_k, L0_cond_b_k, L0_cond_w_v, L0_cond_b_v, L0_cond_w_o, L0_cond_b_o, L0_cond_w_f1, L0_cond_b_f1, L0_cond_w_f2, L0_cond_b_f2, L0_cond_w_ada, L0_cond_b_ada, L0_ffn_wqkv, L0_ffn_q_scale, L0_ffn_k_scale, L0_ffn_wo, L0_ffn_ln_g, L0_ffn_ln_b, L0_ffn_w1, L0_ffn_b1, L0_ffn_w2, L0_ffn_b2):
    import jax
    import jax.numpy as jnp

    def _L0_cond_ref(x, t_emb, w_q, b_q, w_k, b_k, w_v, b_v, w_o, b_o, w_f1, b_f1, w_f2, b_f2, w_ada, b_ada):
        import math
        import jax, jax.numpy as jnp
        import numpy as np
        EPS = 1e-07
        MAX_TANH_ARG = 1.0 - 1e-05

        def _norm(x):
            return jnp.sqrt(jnp.sum(x * x, axis=-1, keepdims=True)).clip(EPS)

        def logmap0(x):
            n = _norm(x)
            return jnp.arctanh(jnp.clip(n, EPS, MAX_TANH_ARG)) * x / n

        def expmap0(v):
            n = _norm(v)
            return jnp.tanh(n) * v / n

        def mobius_add(x, y):
            x2 = jnp.sum(x * x, -1, keepdims=True)
            y2 = jnp.sum(y * y, -1, keepdims=True)
            xy = jnp.sum(x * y, -1, keepdims=True)
            num = (1 + 2 * xy + y2) * x + (1 - x2) * y
            den = (1 + 2 * xy + x2 * y2).clip(EPS)
            return num / den

        def plin(x, w, b):
            return expmap0(logmap0(x) @ w + b)

        def layer_norm(x, eps=1e-06):
            m = x.mean(-1, keepdims=True)
            v = ((x - m) ** 2).mean(-1, keepdims=True)
            return (x - m) / jnp.sqrt(v + eps)

        def _beta(a, b):
            return math.exp(math.lgamma(a) + math.lgamma(b) - math.lgamma(a + b))
        D, H, FF = (128, 16, 512)
        HD = D // H
        BETA_N = _beta(D / 2, 0.5)
        BETA_H = _beta(HD / 2, 0.5)

        def _to_heads(p):
            B, S, _ = p.shape
            t = logmap0(p).reshape(B, S, H, HD) * (BETA_H / BETA_N)
            return expmap0(jnp.transpose(t, (0, 2, 1, 3)))

        def _from_heads(ph):
            B, _, S, _ = ph.shape
            t = logmap0(ph) * (BETA_N / BETA_H)
            t = jnp.transpose(t, (0, 2, 1, 3)).reshape(B, S, D)
            return expmap0(t)
        ada = t_emb @ w_ada + b_ada
        sh_msa, sc_msa, g_msa, sh_mlp, sc_mlp, g_mlp = jnp.split(ada, 6, axis=-1)
        residual = x
        xn = layer_norm(logmap0(x))
        xm = expmap0(xn * (1 + sc_msa) + sh_msa)
        q = _to_heads(plin(xm, w_q, b_q))
        k = _to_heads(plin(xm, w_k, b_k))
        v = _to_heads(plin(xm, w_v, b_v))
        qt, kt, vt = (logmap0(q), logmap0(k), logmap0(v))
        scores = jnp.einsum('bhqd,bhkd->bhqk', qt, kt) / math.sqrt(HD)
        attn = jax.nn.softmax(scores, axis=-1)
        out_h = expmap0(jnp.einsum('bhqk,bhkd->bhqd', attn, vt))
        attn_out = plin(_from_heads(out_h), w_o, b_o)
        attn_t = g_msa * logmap0(attn_out)
        x = mobius_add(residual, expmap0(attn_t))
        residual = x
        xn = layer_norm(logmap0(x))
        xm = expmap0(xn * (1 + sc_mlp) + sh_mlp)
        ff = plin(plin(xm, w_f1, b_f1), w_f2, b_f2)
        ff_t = g_mlp * logmap0(ff)
        return mobius_add(residual, expmap0(ff_t))

    def _L0_ffn_ref(x, wqkv, q_scale, k_scale, wo, ln_g, ln_b, w1, b1, w2, b2):
        import jax, jax.numpy as jnp
        import numpy as np
        DIM = 128
        DEPTH = 2
        HEADS = 8
        DIM_HEAD = 64
        WINDOW = 64
        INNER = HEADS * DIM_HEAD
        HID = int(DIM * 4 * 2 / 3)
        B, N = (2, 1024)
        QK_SCALE = 8.0

        def shift_token(t):
            t1, t2 = jnp.split(t, 2, axis=-1)
            t2 = jnp.pad(t2, ((0, 0), (1, 0), (0, 0)))[:, :-1]
            return jnp.concatenate([t1, t2], axis=-1)

        def l2norm(t):
            return t / jnp.clip(jnp.linalg.norm(t, axis=-1, keepdims=True), 1e-12)

        def rotate_half(x):
            x1, x2 = jnp.split(x, 2, axis=-1)
            return jnp.concatenate([-x2, x1], axis=-1)

        def rotary_xpos(q, k):
            n = q.shape[-2]
            half_idx = jnp.arange(0, DIM_HEAD, 2, dtype=jnp.float32)
            inv_freq = 1.0 / 10000.0 ** (half_idx / DIM_HEAD)
            t = jnp.arange(n, dtype=jnp.float32)
            freqs = t[:, None] * inv_freq[None, :]
            freqs = jnp.concatenate([freqs, freqs], axis=-1)
            base = (half_idx + 0.4 * DIM_HEAD) / (1.4 * DIM_HEAD)
            power = (t - n // 2) / float(WINDOW // 2)
            scale = base[None, :] ** power[:, None]
            scale = jnp.concatenate([scale, scale], axis=-1)
            cos, sin = (jnp.cos(freqs), jnp.sin(freqs))
            q = q * cos * scale + rotate_half(q) * sin * scale
            k = k * cos / scale + rotate_half(k) * sin / scale
            return (q, k)

        def local_attention(q, k, v):
            b, h, n, d = q.shape
            w = n // WINDOW
            bq = q.reshape(b, h, w, WINDOW, d) * QK_SCALE
            bk = k.reshape(b, h, w, WINDOW, d)
            bv = v.reshape(b, h, w, WINDOW, d)

            def look_around(t):
                p = jnp.pad(t, ((0, 0), (0, 0), (1, 0), (0, 0), (0, 0)))
                return jnp.concatenate([p[:, :, :w], p[:, :, 1:]], axis=3)
            bk, bv = (look_around(bk), look_around(bv))
            bt = jnp.arange(n).reshape(w, WINDOW)
            btp = jnp.pad(bt, ((1, 0), (0, 0)), constant_values=-1)
            btk = jnp.concatenate([btp[:w], btp[1:]], axis=1)
            sim = jnp.einsum('bhwid,bhwjd->bhwij', bq, bk)
            i = bt[:, :, None]
            j = btk[:, None, :]
            mask = (i < j) | (i > j + WINDOW) | (j == -1)
            sim = jnp.where(mask, -jnp.finfo(sim.dtype).max, sim)
            attn = jax.nn.softmax(sim, axis=-1)
            out = jnp.einsum('bhwij,bhwjd->bhwid', attn, bv)
            return out.reshape(b, h, n, d)

        def _layer(x, wqkv, qs, ksc, wo, lg, lb, w1, b1, w2, b2):
            b, n, _ = x.shape
            h = shift_token(x)
            qkv = h @ wqkv
            q, k, v = jnp.split(qkv, 3, axis=-1)
            to_heads = lambda t: t.reshape(b, n, HEADS, DIM_HEAD).transpose(0, 2, 1, 3)
            q, k, v = (to_heads(q), to_heads(k), to_heads(v))
            q = l2norm(q) * qs
            k = l2norm(k) * ksc
            q, k = rotary_xpos(q, k)
            o = local_attention(q, k, v)
            o = o.transpose(0, 2, 1, 3).reshape(b, n, INNER)
            x = x + o @ wo
            h = shift_token(x)
            mu = h.mean(-1, keepdims=True)
            var = h.var(-1, keepdims=True)
            h = (h - mu) / jnp.sqrt(var + 1e-05) * lg + lb
            h = h @ w1 + b1
            a, g = jnp.split(h, 2, axis=-1)
            h = a * jax.nn.gelu(g, approximate=False)
            x = x + h @ w2 + b2
            return x
        for l in range(DEPTH):
            x = _layer(x, wqkv[l], q_scale[l], k_scale[l], wo[l], ln_g[l], ln_b[l], w1[l], b1[l], w2[l], b2[l])
        return x
    x = x + _L0_ffn_ref(_L0_cond_ref(x, cond_1024[:, None, :], L0_cond_w_q, L0_cond_b_q, L0_cond_w_k, L0_cond_b_k, L0_cond_w_v, L0_cond_b_v, L0_cond_w_o, L0_cond_b_o, L0_cond_w_f1, L0_cond_b_f1, L0_cond_w_f2, L0_cond_b_f2, L0_cond_w_ada, L0_cond_b_ada), L0_ffn_wqkv, L0_ffn_q_scale, L0_ffn_k_scale, L0_ffn_wo, L0_ffn_ln_g, L0_ffn_ln_b, L0_ffn_w1, L0_ffn_b1, L0_ffn_w2, L0_ffn_b2)
    return x

_drawn_inputs = setup_inputs


def setup_inputs(seed=0):
    import zlib

    import numpy as np

    out = dict(_drawn_inputs(seed))
    spreads = {'L0_cond_b_q': (0.0, 0.8),
     'L0_cond_b_k': (0.0, 0.8),
     'L0_cond_b_v': (0.0, 0.1),
     'L0_cond_b_o': (0.0, 0.1),
     'L0_cond_b_f1': (0.0, 0.1),
     'L0_cond_b_f2': (0.0, 0.1),
     'L0_cond_b_ada': (0.0, 0.1),
     'L0_ffn_q_scale': (1.0, 0.6),
     'L0_ffn_k_scale': (1.0, 0.6),
     'L0_ffn_ln_g': (1.0, 0.2),
     'L0_ffn_ln_b': (0.0, 0.508),
     'L0_ffn_b1': (0.0, 0.1),
     'L0_ffn_b2': (0.0, 0.1)}
    factors = {'L0_cond_w_q': 8.0, 'L0_cond_w_k': 8.0, 'L0_cond_w_v': 4.781}
    for name, (base, spread) in spreads.items():
        noise = np.random.default_rng([zlib.crc32(name.encode()), seed]).standard_normal(out[name].shape)
        drawn = base * np.exp(spread * noise) if base else spread * noise
        out[name] = jnp.asarray(drawn.astype(out[name].dtype))
    for name, factor in factors.items():
        out[name] = (out[name] * factor).astype(out[name].dtype)
    return out
```

```python
import math
from contextlib import ExitStack

import concourse.bass as bass
from concourse import mybir

F32 = mybir.dt.float32
F16 = mybir.dt.float16
BF16 = mybir.dt.bfloat16
I32 = mybir.dt.int32
ALU = mybir.AluOpType
ACT = mybir.ActivationFunctionType
AXX = mybir.AxisListType.X

P = 128
EPS = 1e-7
MAX_TANH = 0.99998998641967773438
MAX_ARTANH = 0.5 * math.log((1 + MAX_TANH) / (1 - MAX_TANH))
EXP_SCALE_BITS = 12
RSQRT_MAGIC = 0x5F3759DF


def adaln_ffn_kernel(
    nc, x, cond_1024,
    w_q, b_q, w_k, b_k, w_v, b_v, w_o, b_o, w_f1, b_f1, w_f2, b_f2, w_ada, b_ada,
    wqkv, q_scale, k_scale, wo, ln_g, ln_b, w1, b1, w2, b2,
    rope, masks, eye, shift, denom_pick, out,
):
    B, S, D = x.shape
    TB = S // P
    T = B * TB
    H, HD = 16, D // 16
    G = H // 4
    FF = w_f1.shape[1]
    FC = FF // P
    beta = lambda a, b: math.exp(math.lgamma(a) + math.lgamma(b) - math.lgamma(a + b))
    RATIO = beta(HD / 2, 0.5) / beta(D / 2, 0.5)
    DEPTH, _, QKV = wqkv.shape
    INNER = QKV // 3
    LD = q_scale.shape[1]
    LH = INNER // LD
    PAIRS = LH // 2
    WIN = P // 2
    NW = T * 2
    HID = w2.shape[1]
    HC = [(c, min(P, HID - c)) for c in range(0, HID, P)]
    NH = len(HC)
    QK_SCALE = 8.0

    with ExitStack() as ctx:
        def sb(name, shape, dt=F32):
            return ctx.enter_context(nc.sbuf_tensor(name, shape, dt))

        def sem(name):
            return ctx.enter_context(nc.semaphore(name))

        bank = ctx.enter_context(nc.psum_tensor("bank", [P, 8, 512], F32))

        def bk(i, n=512):
            return bank[:, i, 0:n]

        eye_f = sb("eye_f", [P, P])
        eye_h = sb("eye_h", [P, P], F16)
        eye_b = sb("eye_b", [P, P], BF16)
        shift_f = sb("shift_f", [P, 2, P])
        pick_f = sb("pick_f", [P, P])
        ones_col = sb("ones_col", [P, 1])
        mask_f = sb("mask_f", [P, 2, P])
        mask_b = sb("mask_b", [P, 2, P], BF16)
        cond_T = sb("cond_T", [P, B])
        b_f1_sb = sb("b_f1_sb", [P, FC])
        x_in = sb("x_in", [P, T, D])
        xr = sb("xr", [P, T, D])

        bn6 = sb("bn6", [P, T, 12])
        mean_var = sb("mean_var", [P, T, 2])
        sml = sb("sml", [P, 32, 8])
        nt_i = sb("nt_i", [P, 256], I32)
        nt_f = sb("nt_f", [P, 256])
        h_mod = sb("h_mod", [P, T, D])
        hT = sb("hT", [P, T * P])
        room_q = sb("room_q", [P, PAIRS * NW * P])
        room_k = sb("room_k", [P, PAIRS * B * (S + WIN)])
        room_v = sb("room_v", [P, 2 * T * LH * (LD + 1)])
        room_r = sb("room_r", [P, 13 * 512])
        room_s = sb("room_s", [P, 9 * 512])

        def carve(room):
            at = [0]

            def take(pattern, n, **sizes):
                a = room[:, at[0]:at[0] + n].rearrange(f"p ({pattern}) -> p {pattern}", **sizes)
                at[0] += n
                return a
            return take

        room_w = sb("room_w", [P, 4224])
        room_a = sb("room_a", [P, B * 6 * D])
        room_m = sb("room_m", [P, 1026])
        take = carve(room_w)
        cond_rep = take("b n", B * P, b=B)
        w_ada_sb = take("n", 6 * D)
        b_ada_sb = take("n", 6 * D)
        w_qkv_sb = take("n", 3 * D)
        b_qkv_sb = take("n", 3 * D)
        w_o_sb = take("g n", G * D, g=G)
        w_f1_sb = take("n", FF)
        w_f2_sb = take("c n", FC * D, c=FC)
        b_f2_sb = take("n", D)
        ada = room_a[:, :].rearrange("p (b k d) -> p b k d", b=B, k=6)
        x_mid = room_m[:, 0:T * D].rearrange("p (t d) -> p t d", t=T)
        take = carve(room_r)
        u_qkv = take("t h d", TB * 3 * D, t=TB, d=HD)
        probs = take("r i n", 4 * 512, r=2, i=2)
        o_raw = take("n", 512)
        den_r = take("n", 512)
        o_T = take("g n", G * S, g=G)
        head_sq = sb("head_sq", [P, TB, 3 * H])
        all_sq = sb("all_sq", [P, TB, 3])
        head_f = sb("head_f", [P, TB, 3 * H])
        all_f = sb("all_f", [P, TB, 3])
        qk_f = sb("qk_f", [P, 2, 2 * H, HD])
        q_split = sb("q_split", [P, 2, H, 4, HD], F16)
        k_split = sb("k_split", [P, 2, H, 4, HD], F16)
        half_k = G * T * P // 2
        q_T = room_k[:, 0:half_k].bitcast(F16).rearrange("p (g n) -> p g n", g=G)
        k_T = room_k[:, half_k:2 * half_k].bitcast(F16).rearrange("p (g n) -> p g n", g=G)
        k_pad = room_q[:, :].bitcast(F16).rearrange("p (g j n) -> p g j n", g=G, j=4)
        take = carve(room_v)
        v_aug = take("t h d", T * H * 32, t=T, d=32)
        z_T = take("c n", FC * S, c=FC)
        z_sq = take("c n", FC * S, c=FC)
        take = carve(room_s)
        a_sb = take("b t d", T * D, b=B, d=D)
        w_sb = take("t d", TB * D, d=D)
        junk = take("i d", 16 * D, d=D)
        sq = take("n", 1024)

        q_blk = room_q[:, :].rearrange("p (r w c) -> p r w c", r=PAIRS, c=P)
        k_loc = room_k[:, :].rearrange("p (r b n) -> p r b n", r=PAIRS, b=B)
        v_loc = room_v[:, :].rearrange("p (k t h d) -> p k t h d", k=2, t=T, d=LD + 1)
        take = carve(room_r)
        qk_rot = take("r n", 4 * 2 * INNER, r=4)
        qk_cross = take("r n", 2 * 2 * INNER, r=2)
        take = carve(room_s)
        qk_raw = take("r n", 2 * 2 * INNER, r=2)
        qk_sq = take("r n", 2 * 2 * INNER, r=2)
        wqkv_sb = sb("wqkv_sb", [P, QKV])
        wo_sb = sb("wo_sb", [P, 2, 2, D])
        w1_sb = sb("w1_sb", [P, 2 * HID])
        w2_sb = sb("w2_sb", [P, NH, D])
        b1_sb = sb("b1_sb", [P, DEPTH, 2, NH])
        b2_sb = sb("b2_sb", [P, DEPTH, D])
        ln_gb = sb("ln_gb", [P, 2, DEPTH])
        rope_l = sb("rope_l", [P, DEPTH, 4, TB, LD])
        scale_sb = room_m[:, 0:DEPTH * 4 * LD].rearrange("p (l k d) -> p l k d", l=DEPTH, k=4)
        hs_T = room_m[:, 0:B * (S + 1)].rearrange("p (b n) -> p b n", b=B)
        norm_sq = sb("norm_sq", [P, T, 2 * LH])
        norm_r = sb("norm_r", [P, T, 2 * LH])
        row_max = sb("row_max", [P, 2, PAIRS])
        o_den = sb("o_den", [P, 2, PAIRS])
        take = carve(room_w)
        s_rel = take("k r c", 2 * PAIRS * P, k=2, r=PAIRS)
        p_loc = take("k r c", 2 * PAIRS * P, k=2, r=PAIRS)
        pT_loc = take("k r c", 2 * PAIRS * P, k=2, r=PAIRS)
        oT_loc = take("k r a c", 2 * 4 * P, k=2, r=2, a=2)
        take = carve(room_a)
        gate_T = take("k n", 2 * S, k=2)
        o_loc = take("k r d", 2 * PAIRS * LD, k=2, r=PAIRS)
        ff_T = room_r[:, 0:B * NH * S].rearrange("p (b c n) -> p b c n", b=B, c=NH)

        names = """consts w_a_in x_in_s ffw_in lw_in eyes cond_rep_s ada_mm ada_used ada_s dve_step act_step ln_num ln_den
        hmod_s hT_mm hT_s qkv_mm u_s usq_s split_s qkT_mm qkT_s kpad_0 kpad_1 zero_s
        scores_mm probs_s pv_mm oraw_s den_mm oT_s wo_mm a_s tanh_in tanh_s
        h2_s h2T_mm h2T_s z_mm z_s zsq_mm z2_mm z2_used x2_s out_s
        rope_in room_s_ rope_s lwt lwf lT_mm lT_s lqk_mm lqk_s lv_mm lv_s lsq_s lred_s lc_s lx_s lrot_s lqkT_mm lqkT_s
        ls_mm lmax_s lrel_s lp_s lpT_mm lpT_s lpv_mm lo_s loT_mm loT_s lwo_mm lx1_s lsh_mm lhn_s lhT_mm lhT_s
        la_mm lg_mm lgate_s lff_s lf2_mm lx2_s""".split()
        q = {n: sem(n) for n in names}
        kpad_s = [q["kpad_0"], q["kpad_1"]]

        block = ctx.enter_context(nc.Block())

        @block.sync
        def _(sp):
            row = lambda a, n: a.rearrange("(o n) -> o n", o=1).to_broadcast([P, n])
            sp.dma_start(x_in[:, :, :], x.rearrange("b (t p) d -> p (b t) d", p=P)).then_inc(q["x_in_s"], 16)
            sp.dma_start(eye_f[:, :], eye).then_inc(q["consts"], 16)
            sp.dma_start(shift_f[:, :, :], shift.rearrange("k p m -> p k m")).then_inc(q["consts"], 16)
            sp.dma_start(pick_f[:, :], denom_pick).then_inc(q["consts"], 16)
            sp.dma_start(mask_f[:, :, :], masks.rearrange("k p m -> p k m")).then_inc(q["consts"], 16)
            sp.dma_start(cond_T[:, :], cond_1024).then_inc(q["consts"], 16)
            sp.dma_start(w_ada_sb[:, :], w_ada).then_inc(q["w_a_in"], 16)
            sp.dma_start(b_ada_sb[:, :], row(b_ada, 6 * D)).then_inc(q["w_a_in"], 16)
            for i, (w, b) in enumerate(((w_q, b_q), (w_k, b_k), (w_v, b_v))):
                sp.dma_start(w_qkv_sb[:, i * D:(i + 1) * D], w).then_inc(q["w_a_in"], 16)
                sp.dma_start(b_qkv_sb[:, i * D:(i + 1) * D], row(b, D)).then_inc(q["w_a_in"], 16)
            sp.wait_ge(q["zero_s"], 3)
            for j in range(4):
                sp.dma_start(w_o_sb[32 * j:32 * j + HD, :, :],
                             w_o.rearrange("(g j d) n -> j d g n", g=G, j=4)[j]).then_inc(q["ffw_in"], 16)
            sp.dma_start(w_o_sb[HD:HD + 1, 0, :], b_o.rearrange("(o n) -> o n", o=1)).then_inc(q["ffw_in"], 16)
            sp.dma_start(w_f1_sb[:, :], w_f1).then_inc(q["ffw_in"], 16)
            sp.dma_start(b_f1_sb[:, :], b_f1).then_inc(q["ffw_in"], 16)
            sp.dma_start(w_f2_sb[:, :, :], w_f2.rearrange("(c p) n -> p c n", p=P)).then_inc(q["ffw_in"], 16)
            sp.dma_start(b_f2_sb[:, :], row(b_f2, D)).then_inc(q["ffw_in"], 16)
            sp.dma_start(rope_l[:, DEPTH - 1, :, :, :], rope.rearrange("k (t p) d -> p k t d", p=P)).then_inc(q["rope_in"], 16)
            for l in range(DEPTH):
                for k, sc in enumerate((q_scale, k_scale)):
                    sp.dma_start(scale_sb[:, l, k, :], row(sc[l], LD)).then_inc(q["rope_in"], 16)
                    for h0 in (0, LD // 2):
                        h1 = LD // 2 - h0
                        sp.dma_start(scale_sb[:, l, 2 + k, h0:h0 + LD // 2], row(sc[l, h1:h1 + LD // 2], LD // 2)).then_inc(q["rope_in"], 16)
                sp.dma_start(b2_sb[:, l, :], row(b2[l], D)).then_inc(q["lwt"], 16)
            sp.dma_start(b1_sb[:, :, :, :], b1.rearrange("p (l k c) -> p l k c", l=DEPTH, k=2)).then_inc(q["lwt"], 16)
            for k, g in enumerate((ln_g, ln_b)):
                sp.dma_start(ln_gb[:, k, :], g).then_inc(q["lwt"], 16)

            def layer_weights(l):
                if l:
                    sp.wait_ge(q["lv_mm"], l * T)
                sp.dma_start(wqkv_sb[:, :], wqkv[l]).then_inc(q["lwf"], 16)
                if l:
                    sp.wait_ge(q["lwo_mm"], l * T)
                for e in range(2):
                    for r in range(2):
                        sp.dma_start(wo_sb[LD * e:LD * e + LD, r, :, :],
                                     wo[l].rearrange("(r e a d) n -> r e d a n", r=2, e=2, a=2)[r, e]).then_inc(q["lwf"], 16)
                if l:
                    sp.wait_ge(q["lf2_mm"], l * B)
                sp.dma_start(w1_sb[:, :], w1[l]).then_inc(q["lwf"], 16)
                for c, (c0, cn) in enumerate(HC):
                    sp.dma_start(w2_sb[0:cn, c, :], w2[l, c0:c0 + cn, :]).then_inc(q["lwf"], 16)

            layer_weights(0)
            sp.wait_ge(q["zero_s"], 4)
            for b in range(B):
                sp.wait_ge(q["qkT_s"], 2 * TB * (b + 1))
                for j in range(4):
                    r = slice(32 * j, 32 * j + 32)
                    sp.dma_start(k_pad[r, :, j, b * S:(b + 1) * S], k_T[r, :, b * S:(b + 1) * S]).then_inc(kpad_s[b], 16)
            for l in range(1, DEPTH):
                layer_weights(l)
            sp.wait_ge(q["lx2_s"], 1 + B * DEPTH)
            sp.dma_start(out.rearrange("b (t p) d -> p (b t) d", p=P), xr[:, :, :]).then_inc(q["out_s"], 16)
            sp.wait_ge(q["out_s"], 16)

        @block.gpsimd
        def _(pool):
            nc.gpsimd.memset(v_aug[:, :, :, :], 0.0).then_inc(q["zero_s"], 1)
            nc.gpsimd.memset(w_o_sb[:, :, :], 0.0).then_inc(q["zero_s"], 1)
            pool.wait_ge(q["zero_s"], 2)
            nc.gpsimd.memset(v_aug[:, :, :, HD:HD + 1], 1.0).then_inc(q["zero_s"], 1)
            nc.gpsimd.memset(k_pad[:, :, :, :].rearrange("p g j t -> p (g j t)").bitcast(I32), 0).then_inc(q["zero_s"], 1)
            pool.wait_ge(q["rope_in"], 16 * (1 + 6 * DEPTH))
            for l in range(DEPTH):
                for k in range(4):
                    nc.gpsimd.tensor_tensor(rope_l[:, l, k, :, :], rope_l[:, DEPTH - 1, k, :, :],
                                            scale_sb[:, l, k, :].unsqueeze(1).to_broadcast([P, TB, LD]), ALU.mult).then_inc(q["rope_s"], 1)
            pool.wait_ge(q["x2_s"], B)
            nc.gpsimd.memset(q_blk, 0.0).then_inc(q["room_s_"], 1)
            nc.gpsimd.memset(k_loc[:, :, :, 0:WIN], 0.0).then_inc(q["room_s_"], 1)
            nc.gpsimd.memset(v_loc[:, 0, :, :, :], 0.0).then_inc(q["room_s_"], 1)
            pool.wait_ge(q["room_s_"], 3)
            nc.gpsimd.memset(hs_T[P // 2:P, :, 0:1], 0.0).then_inc(q["room_s_"], 1)
            pool.wait_ge(q["room_s_"], 4)
            nc.gpsimd.memset(v_loc[:, :, :, :, LD:LD + 1], 1.0).then_inc(q["room_s_"], 1)
            for l in range(DEPTH):
                for n in range(T):
                    i = l * T + n
                    pool.wait_ge(q["lqk_s"], i + 1)
                    if i >= 2:
                        pool.wait_ge(q["lx_s"], i - 1)
                    for k in range(2):
                        pool_src = qk_raw[:, i % 2, k * INNER:(k + 1) * INNER].rearrange("p (h a d) -> p h a d", h=LH, a=2)
                        last = nc.gpsimd.tensor_tensor(
                            qk_cross[:, i % 2, k * INNER:(k + 1) * INNER].rearrange("p (h a d) -> p h a d", h=LH, a=2),
                            pool_src[:, :, ::-1, :],
                            rope_l[:, l, 2 + k, n % TB, :].rearrange("p (a d) -> p a d", a=2).unsqueeze(1)
                            .to_broadcast([P, LH, 2, LD // 2]), ALU.mult)
                    last.then_inc(q["lc_s"], 1)

        @block.tensor
        def _(pe):
            pe.wait_ge(q["consts"], 80)
            pe.wait_ge(q["eyes"], 1)
            pe.wait_ge(q["w_a_in"], 16 * 8)
            for b in range(B):
                pe.wait_ge(q["cond_rep_s"], b + 1)
                for half in range(2):
                    last = nc.tensor.matmul(bk(2 * b + half, 3 * D), cond_rep[:, b, :],
                                            w_ada_sb[:, half * 3 * D:(half + 1) * 3 * D], start=True, stop=True)
                last.then_inc(q["ada_mm"], 1)

            def transpose_mod(b, dst, src_ready, done):
                pe.wait_ge(src_ready, b + 1)
                for t in range(TB):
                    last = nc.tensor.transpose(bank[:, dst, t * P:(t + 1) * P], h_mod[:, b * TB + t, :], eye_f[:, :])
                last.then_inc(done, 1)

            for b in range(B):
                transpose_mod(b, 4 + b, q["hmod_s"], q["hT_mm"])
                pe.wait_ge(q["hT_s"], b + 1)
                for t in range(TB):
                    n = b * TB + t
                    if n >= 2:
                        pe.wait_ge(q["u_s"], n - 1)
                    nc.tensor.matmul(bk(6 + n % 2, 3 * D), hT[:, n * P:(n + 1) * P], w_qkv_sb[:, :],
                                     start=True, stop=True).then_inc(q["qkv_mm"], 1)
                for t in range(TB):
                    n = b * TB + t
                    pe.wait_ge(q["split_s"], n + 1)
                    if n < 2:
                        pe.wait_ge(q["ada_s"], B)
                    else:
                        pe.wait_ge(q["qkT_s"], 2 * (n - 1))
                    dst = bank[:, 2 + n % 2, :].bitcast(F16)
                    for i, sp_t in enumerate((q_split, k_split)):
                        for g in range(G):
                            c = (i * G + g) * P
                            last = nc.tensor.transpose(dst[:, c:c + P],
                                                       sp_t[:, n % 2, 4 * g:4 * g + 4, :, :].rearrange("p a b c -> p (a b c)"),
                                                       eye_h[:, :])
                    last.then_inc(q["qkT_mm"], 1)

            steps = [(b, g, kt, hp) for b in range(B) for g in range(G) for kt in range(TB) for hp in range(2)]

            def scores(n):
                b, g, kt, hp = steps[n]
                if n < 2:
                    pe.wait_ge(q["qkT_s"], 2 * T)
                if (g, kt, hp) == (0, 0, 0):
                    pe.wait_ge(kpad_s[b], 64)
                if n >= 2:
                    pe.wait_ge(q["probs_s"], n - 1)
                for i in range(2):
                    j = 2 * hp + i
                    k0 = (b * TB + kt) * P
                    last = nc.tensor.matmul(bk(2 * (n % 2) + i), k_pad[:, g, j, k0:k0 + P],
                                            q_T[:, g, b * S:(b + 1) * S], start=True, stop=True)
                last.then_inc(q["scores_mm"], 1)

            def weigh(n):
                b, g, kt, hp = steps[n]
                bg = b * G + g
                pe.wait_ge(q["probs_s"], n + 1)
                if kt == 0 and hp == 0 and bg >= 2:
                    pe.wait_ge(q["oraw_s"], bg - 1)
                if n == 0:
                    pe.wait_ge(q["hT_s"], 2)
                for i in range(2):
                    j = 2 * hp + i
                    last = nc.tensor.matmul(bank[32 * j:32 * j + 32, 4 + bg % 2, :],
                                            v_aug[:, b * TB + kt, 4 * g + j, :], probs[:, n % 2, i, :],
                                            start=(kt == 0), stop=(kt == TB - 1), skip_group_check=True)
                last.then_inc(q["pv_mm"], 1)

            def denominators(bg):
                pe.wait_ge(q["oraw_s"], bg + 1)
                if bg == 0:
                    pe.wait_ge(q["u_s"], T)
                if bg >= 1:
                    pe.wait_ge(q["oT_s"], bg)
                nc.tensor.matmul(bk(6), pick_f[:, :], o_raw[:, :], start=True, stop=True).then_inc(q["den_mm"], 1)

            def project(b):
                pe.wait_ge(q["oT_s"], G * (b + 1))
                pe.wait_ge(q["ffw_in"], 16 * 9)
                if b >= 1:
                    pe.wait_ge(q["a_s"], b)
                for t in range(TB):
                    for g in range(G):
                        last = nc.tensor.matmul(bank[:, 7, t * P:(t + 1) * P], o_T[:, g, t * P:(t + 1) * P],
                                                w_o_sb[:, g, :], start=(g == 0), stop=(g == G - 1))
                last.then_inc(q["wo_mm"], 1)

            N = len(steps)
            per = TB * 2
            for n in range(N + 6):
                if n < N:
                    scores(n)
                if 1 <= n <= N:
                    weigh(n - 1)
                if n >= per + 3 and (n - 3) % per == 0:
                    denominators((n - 3) // per - 1)
                if n >= per * G + 5 and (n - 5) % (per * G) == 0:
                    project((n - 5) // (per * G) - 1)

            for b in range(B):
                transpose_mod(b, 0, q["h2_s"], q["h2T_mm"])
                pe.wait_ge(q["h2T_s"], b + 1)
                for c in range(FC):
                    n = b * FC + c
                    if n >= 2:
                        pe.wait_ge(q["z_s"], 2 * (n - 1))
                    nc.tensor.matmul(bk(1 + n % 2), w_f1_sb[:, c * P:(c + 1) * P], hT[:, b * S:(b + 1) * S],
                                     start=True, stop=True).then_inc(q["z_mm"], 1)
                pe.wait_ge(q["z_s"], 2 * FC * (b + 1))
                if b >= 1:
                    pe.wait_ge(q["z2_used"], b)
                for t in range(TB):
                    for c in range(FC):
                        last = nc.tensor.matmul(bank[:, 3, t:t + 1], z_sq[:, c, t * P:(t + 1) * P], ones_col[:, :],
                                                start=(c == 0), stop=(c == FC - 1))
                last.then_inc(q["zsq_mm"], 1)
                for t in range(TB):
                    for c in range(FC):
                        last = nc.tensor.matmul(bank[:, 4, t * P:(t + 1) * P], z_T[:, c, t * P:(t + 1) * P],
                                                w_f2_sb[:, c, :], start=(c == 0), stop=(c == FC - 1))
                last.then_inc(q["z2_mm"], 1)

            pe.wait_ge(q["lwt"], 16 * (DEPTH + 3))
            for l in range(DEPTH):
                pe.wait_ge(q["lwf"], 16 * 9 * (l + 1))
                x_ready = lambda b: pe.wait_ge(q["x2_s"], b + 1) if l == 0 else pe.wait_ge(q["lx2_s"], B * (l - 1) + b + 1)
                for b in range(B):
                    x_ready(b)
                    if l or b:
                        pe.wait_ge(q["lT_s"], l * B + b)
                    for t in range(TB):
                        last = nc.tensor.transpose(bank[:, 0, t * P:(t + 1) * P], xr[:, b * TB + t, :], eye_f[:, :])
                    last.then_inc(q["lT_mm"], 1)
                if l == 0:
                    pe.wait_ge(q["x2_s"], B)
                for n in range(T + 3):
                    i = l * T + n
                    if n < T:
                        b, t = divmod(n, TB)
                        pe.wait_ge(q["lT_s"], l * B + b + 1)
                        if i >= 2:
                            pe.wait_ge(q["lqk_s"], i - 1)
                            pe.wait_ge(q["lsq_s"], i - 1)
                        for k in range(2):
                            last = nc.tensor.matmul(bk(1 + 2 * (i % 2) + k), hs_T[:, b, t * P:(t + 1) * P],
                                                    wqkv_sb[:, k * INNER:(k + 1) * INNER], start=True, stop=True)
                        last.then_inc(q["lqk_mm"], 1)
                        if i >= 1:
                            pe.wait_ge(q["lv_s"], i)
                        nc.tensor.matmul(bk(5), hs_T[:, b, t * P:(t + 1) * P], wqkv_sb[:, 2 * INNER:],
                                         start=True, stop=True).then_inc(q["lv_mm"], 1)
                    if n >= 3:
                        i = l * T + n - 3
                        pe.wait_ge(q["lrot_s"], i + 1)
                        if i >= 1:
                            pe.wait_ge(q["lqkT_s"], i)
                        for c in range(2 * PAIRS):
                            last = nc.tensor.transpose(bank[:, 6 + c // PAIRS, (c % PAIRS) * P:(c % PAIRS + 1) * P],
                                                       qk_rot[:, i % 4, c * P:(c + 1) * P], eye_f[:, :])
                        last.then_inc(q["lqkT_mm"], 1)
                pe.wait_ge(q["lqkT_s"], (l + 1) * T)
                for w in range(NW + 5):
                    j = l * NW + w
                    if w < NW:
                        b, wb = divmod(w, NW // B)
                        if w >= 2:
                            pe.wait_ge(q["lrel_s"], j - 1)
                        nc.tensor.matmul(bk(j % 2), eye_b[:, :], mask_b[:, int(wb == 0), :].unsqueeze(1).to_broadcast([P, PAIRS, P]),
                                         start=True, stop=False)
                        for r in range(PAIRS):
                            last = nc.tensor.matmul(bank[:, j % 2, r * P:(r + 1) * P], q_blk[:, r, w, :],
                                                    k_loc[:, r, b, wb * WIN:wb * WIN + P], start=False, stop=(r == PAIRS - 1))
                        last.then_inc(q["ls_mm"], 1)
                    if 1 <= w <= NW:
                        j = l * NW + w - 1
                        pe.wait_ge(q["lp_s"], j + 1)
                        if j >= 2:
                            pe.wait_ge(q["lpT_s"], j - 1)
                        for r in range(PAIRS):
                            last = nc.tensor.transpose(bank[:, 2 + j % 2, r * P:(r + 1) * P], p_loc[:, j % 2, r, :], eye_f[:, :])
                        last.then_inc(q["lpT_mm"], 1)
                    if 2 <= w <= NW + 1:
                        j = l * NW + w - 2
                        pe.wait_ge(q["lpT_s"], j + 1)
                        if j >= 2:
                            pe.wait_ge(q["lo_s"], j - 1)
                        for r in range(PAIRS):
                            for a in range(2):
                                last = nc.tensor.matmul(bank[WIN * a:WIN * a + WIN, 4 + j % 2, r * (LD + 1):(r + 1) * (LD + 1)],
                                                        pT_loc[:, j % 2, r, WIN * a:WIN * a + WIN],
                                                        v_loc[:, (w - 2) % 2, (w - 2) // 2, 2 * r + a, :],
                                                        start=True, stop=True, skip_group_check=True)
                        last.then_inc(q["lpv_mm"], 1)
                    if 3 <= w <= NW + 2:
                        j = l * NW + w - 3
                        pe.wait_ge(q["lo_s"], j + 1)
                        if j >= 1:
                            pe.wait_ge(q["loT_s"], j)
                        for r in range(2):
                            last = nc.tensor.transpose(bank[:, 6, r * P:(r + 1) * P],
                                                       o_loc[:, j % 2, 2 * r:2 * r + 2, :].rearrange("p r d -> p (r d)"), eye_f[:, :])
                        last.then_inc(q["loT_mm"], 1)
                    if w >= 5 and w % 2 == 1:
                        n = (w - 5) // 2
                        i = l * T + n
                        pe.wait_ge(q["loT_s"], 2 * i + 2)
                        if i:
                            pe.wait_ge(q["lx1_s"], i)
                        for c in range(4):
                            last = nc.tensor.matmul(bank[:, 7, (n % 4) * P:(n % 4 + 1) * P], oT_loc[:, n % 2, c // 2, c % 2, :],
                                                    wo_sb[:, c // 2, c % 2, :], start=(c == 0), stop=(c == 3), skip_group_check=True)
                        last.then_inc(q["lwo_mm"], 1)
                for b in range(B):
                    for t in range(TB):
                        n = b * TB + t
                        pe.wait_ge(q["lx1_s"], l * T + n + 1)
                        last = nc.tensor.matmul(bank[:, b, n % TB * 64:n % TB * 64 + 64], shift_f[:, 0, :], xr[:, n, 64:128],
                                         start=True, stop=(t == 0), skip_group_check=True)
                        if t:
                            last = nc.tensor.matmul(bank[:, b, n % TB * 64:n % TB * 64 + 64], shift_f[:, 1, :], xr[:, n - 1, 64:128],
                                             start=False, stop=True, skip_group_check=True)
                    last.then_inc(q["lsh_mm"], 1)
                for b in range(B):
                    m = l * B + b
                    pe.wait_ge(q["lhn_s"], m + 1)
                    for t in range(TB):
                        last = nc.tensor.transpose(bank[:, b, t * P:(t + 1) * P], h_mod[:, b * TB + t, :], eye_f[:, :])
                    last.then_inc(q["lhT_mm"], 1)
                for b in range(B):
                    m = l * B + b
                    pe.wait_ge(q["lhT_s"], m + 1)
                    for c, (c0, cn) in enumerate(HC):
                        i = m * NH + c
                        if i >= 2:
                            pe.wait_ge(q["lgate_s"], i - 1)
                        nc.tensor.matmul(bank[0:cn, 4 + i % 2, :], w1_sb[:, HID + c0:HID + c0 + cn], hT[:, b * S:(b + 1) * S],
                                         start=True, stop=True).then_inc(q["lg_mm"], 1)
                        if i >= 2:
                            pe.wait_ge(q["lff_s"], i - 1)
                        nc.tensor.matmul(bank[0:cn, 2 + i % 2, :], w1_sb[:, c0:c0 + cn], hT[:, b * S:(b + 1) * S],
                                         start=True, stop=True).then_inc(q["la_mm"], 1)
                    pe.wait_ge(q["lff_s"], (m + 1) * NH)
                    for t in range(TB):
                        for c, (c0, cn) in enumerate(HC):
                            last = nc.tensor.matmul(bank[:, 6 + b, t * P:(t + 1) * P], ff_T[0:cn, b, c, t * P:(t + 1) * P],
                                                    w2_sb[0:cn, c, :], start=(c == 0), stop=(c == NH - 1), skip_group_check=True)
                    last.then_inc(q["lf2_mm"], 1)

        @block.scalar
        def _(act):
            chain = [0]

            def link(ins):
                chain[0] += 1
                ins.then_inc(q["act_step"], 1)
                act.wait_ge(q["act_step"], chain[0])

            def logs(k):
                act.wait_ge(q["ln_num"], k + 1)
                nc.scalar.activation(sml[:, 2, :], sml[:, 0, :], ACT.Ln, bias=ones_col[:, 0:1], scale=1.0)
                nc.scalar.activation(sml[:, 3, :], sml[:, 0, :], ACT.Ln, bias=ones_col[:, 0:1], scale=-1.0).then_inc(q["ln_den"], 1)

            logs(0)
            for b in range(B):
                act.wait_ge(q["hT_mm"], b + 1)
                nc.scalar.activation(hT[:, b * S:(b + 1) * S], bk(4 + b), ACT.Copy).then_inc(q["hT_s"], 1)
                for t in range(TB):
                    n = b * TB + t
                    act.wait_ge(q["u_s"], n + 1)
                    if n >= 2:
                        act.wait_ge(q["usq_s"], 2 * (n - 1))
                    nc.scalar.activation(sq[:, 512 * (n % 2):512 * (n % 2) + 3 * D],
                                         u_qkv[:, t, :, :].rearrange("p h d -> p (h d)"), ACT.Square).then_inc(q["usq_s"], 1)
                for t in range(TB):
                    n = b * TB + t
                    act.wait_ge(q["qkT_mm"], n + 1)
                    src = bank[:, 2 + n % 2, :].bitcast(F16).rearrange("p (i g t) -> p i g t", i=2, g=G)
                    nc.scalar.activation(q_T[:, :, n * P:(n + 1) * P], src[:, 0, :, :], ACT.Copy).then_inc(q["qkT_s"], 1)
                    nc.scalar.activation(k_T[:, :, n * P:(n + 1) * P], src[:, 1, :, :], ACT.Copy).then_inc(q["qkT_s"], 1)

            def evacuate(b):
                act.wait_ge(q["wo_mm"], b + 1)
                nc.scalar.activation(a_sb[:, b, :, :].rearrange("p t d -> p (t d)"), bk(7), ACT.Copy).then_inc(q["a_s"], 1)

            N = B * G * TB * 2
            for n in range(N):
                act.wait_ge(q["scores_mm"], n + 1)
                if n >= 2:
                    act.wait_ge(q["pv_mm"], n - 1)
                nc.scalar.activation(probs[:, n % 2, :, :], bank[:, 2 * (n % 2):2 * (n % 2) + 2, :], ACT.Exp,
                                     scale=2.0 ** (-2 * EXP_SCALE_BITS) / math.sqrt(HD)).then_inc(q["probs_s"], 1)
                if n == G * TB * 2 + 8:
                    evacuate(0)
            evacuate(1)

            for b in range(B):
                act.wait_ge(q["tanh_in"], b + 1)
                nc.scalar.activation(sml[:, 9, 0:TB], sml[:, 8, 0:TB], ACT.Tanh).then_inc(q["tanh_s"], 1)
                logs(b + 1)
            for b in range(B):
                act.wait_ge(q["h2T_mm"], b + 1)
                nc.scalar.activation(hT[:, b * S:(b + 1) * S], bk(0), ACT.Copy).then_inc(q["h2T_s"], 1)
                if b >= 1:
                    act.wait_ge(q["z2_mm"], b)
                for c in range(FC):
                    n = b * FC + c
                    act.wait_ge(q["z_mm"], n + 1)
                    nc.scalar.activation(z_T[:, c, :], bk(1 + n % 2), ACT.Identity, bias=b_f1_sb[:, c:c + 1]).then_inc(q["z_s"], 1)
                    nc.scalar.activation(z_sq[:, c, :], bk(1 + n % 2), ACT.Square, bias=b_f1_sb[:, c:c + 1]).then_inc(q["z_s"], 1)
            for b in range(B):
                act.wait_ge(q["tanh_in"], B + b + 1)
                nc.scalar.activation(sml[:, 9, 0:TB], sml[:, 8, 0:TB], ACT.Tanh).then_inc(q["tanh_s"], 1)

            act.wait_ge(q["room_s_"], 5)
            Hf = P // 2
            for l in range(DEPTH):
                for b in range(B):
                    act.wait_ge(q["lT_mm"], l * B + b + 1)
                    nc.scalar.activation(hs_T[0:Hf, b, 0:S], bank[0:Hf, 0, :], ACT.Copy)
                    nc.scalar.activation(hs_T[Hf:P, b, 1:S + 1], bank[Hf:P, 0, :], ACT.Copy).then_inc(q["lT_s"], 1)
                for n in range(T + 3):
                    i = l * T + n
                    if n < T:
                        b, t = divmod(n, TB)
                        act.wait_ge(q["lqk_mm"], i + 1)
                        if i >= 2:
                            act.wait_ge(q["lx_s"], i - 1)
                            act.wait_ge(q["lred_s"], i - 1)
                        src = bank[:, 1 + 2 * (i % 2):3 + 2 * (i % 2), :].rearrange("p k n -> p (k n)")
                        nc.scalar.activation(qk_raw[:, i % 2, :], src, ACT.Copy).then_inc(q["lqk_s"], 1)
                        nc.scalar.activation(qk_sq[:, i % 2, :], src, ACT.Square).then_inc(q["lsq_s"], 1)
                        act.wait_ge(q["lv_mm"], i + 1)
                        vs = bk(5).rearrange("p (h d) -> p h d", d=LD)
                        nc.scalar.activation(v_loc[:, 1, n, :, 0:LD], vs, ACT.Copy)
                        if t < TB - 1:
                            nc.scalar.activation(v_loc[WIN:P, 0, n + 1, :, 0:LD], vs[WIN:P], ACT.Copy)
                        nc.scalar.activation(v_loc[0:WIN, 0, n, :, 0:LD], vs[0:WIN], ACT.Copy).then_inc(q["lv_s"], 1)
                    if n >= 3:
                        n2 = n - 3
                        i = l * T + n2
                        b, t = divmod(n2, TB)
                        act.wait_ge(q["lqkT_mm"], i + 1)
                        qs = bk(6).rearrange("p (r w c) -> p r w c", r=PAIRS, w=2)
                        nc.scalar.activation(q_blk[0:Hf, :, 2 * n2:2 * n2 + 2, 0:WIN], qs[0:Hf], ACT.Copy)
                        nc.scalar.activation(q_blk[Hf:P, :, 2 * n2:2 * n2 + 2, WIN:P], qs[Hf:P], ACT.Copy)
                        nc.scalar.activation(k_loc[:, :, b, WIN + t * P:WIN + (t + 1) * P],
                                             bk(7).rearrange("p (r c) -> p r c", r=PAIRS), ACT.Copy).then_inc(q["lqkT_s"], 1)
                for w in range(NW + 3):
                    if w < NW:
                        j = l * NW + w
                        act.wait_ge(q["lrel_s"], j + 1)
                        if j >= 2:
                            act.wait_ge(q["lpT_mm"], j - 1)
                        to = p_loc[:, j % 2, :, :].rearrange("p r (k c) -> p r k c", k=2)
                        if w % 2 == 0:
                            to = to[:, :, ::-1, :]
                        nc.scalar.activation(to, s_rel[:, j % 2, :, :].rearrange("p r (k c) -> p r k c", k=2), ACT.Exp,
                                             scale=QK_SCALE).then_inc(q["lp_s"], 1)
                    if 1 <= w <= NW:
                        j = l * NW + w - 1
                        act.wait_ge(q["lpT_mm"], j + 1)
                        if j >= 2:
                            act.wait_ge(q["lpv_mm"], j - 1)
                        nc.scalar.activation(pT_loc[:, j % 2, :, :].rearrange("p r c -> p (r c)"), bk(2 + j % 2), ACT.Copy).then_inc(q["lpT_s"], 1)
                    if w >= 3:
                        w2_ = w - 3
                        j = l * NW + w2_
                        n = w2_ // 2
                        act.wait_ge(q["loT_mm"], j + 1)
                        if l * T + n >= 2:
                            act.wait_ge(q["lwo_mm"], l * T + n - 1)
                        nc.scalar.activation(oT_loc[:, n % 2, :, :, (w2_ % 2) * WIN:(w2_ % 2 + 1) * WIN],
                                             bk(6, 2 * P).rearrange("p (r a c) -> p r a c", r=2, a=2), ACT.Copy).then_inc(q["loT_s"], 1)
                for b in range(B):
                    act.wait_ge(q["lhT_mm"], l * B + b + 1)
                    nc.scalar.activation(hT[:, b * S:(b + 1) * S], bk(b), ACT.Identity, scale=ln_gb[:, 0, l:l + 1],
                                         bias=ln_gb[:, 1, l:l + 1]).then_inc(q["lhT_s"], 1)
                for b in range(B):
                    for c, (c0, cn) in enumerate(HC):
                        i = (l * B + b) * NH + c
                        act.wait_ge(q["lg_mm"], i + 1)
                        if i >= 2:
                            act.wait_ge(q["lff_s"], i - 1)
                        nc.scalar.activation(gate_T[0:cn, i % 2, :], bank[0:cn, 4 + i % 2, :], ACT.Gelu,
                                             bias=b1_sb[0:cn, l, 1, c:c + 1]).then_inc(q["lgate_s"], 1)

        @block.vector
        def _(dve):
            chain = [0]
            v = nc.vector

            def link(ins):
                chain[0] += 1
                ins.then_inc(q["dve_step"], 1)
                dve.wait_ge(q["dve_step"], chain[0])

            def publish(ins, sem, value):
                ins.then_inc(sem, 1)
                dve.wait_ge(sem, value)

            def tt(o, a, b, op):
                link(v.tensor_tensor(o, a, b, op))

            def ts(o, a, s1, op0, s2=None, op1=ALU.bypass):
                link(v.tensor_scalar(o, a, s1, s2, op0, op1))

            def stt(o, a, sc, b, op0, op1):
                link(v.scalar_tensor_tensor(o, a, sc, b, op0, op1))

            def rsqrt(o, a, n):
                i, f = nt_i[:, 0:n], nt_f[:, 0:n]
                ts(i, a.bitcast(I32), 1, ALU.logical_shift_right)
                ts(o.bitcast(I32), i, -1.0, ALU.mult, float(RSQRT_MAGIC), ALU.add)
                for _ in range(3):
                    tt(f, o, o, ALU.mult)
                    stt(f, f, -0.5, a, ALU.mult, ALU.mult)
                    stt(o, f, 1.5, o, ALU.add, ALU.mult)

            dve.wait_ge(q["consts"], 80)
            v.tensor_copy(eye_h[:, :], eye_f[:, :])
            v.tensor_copy(eye_b[:, :], eye_f[:, :])
            v.tensor_copy(mask_b[:, :, :], mask_f[:, :, :])
            v.memset(ones_col[:, :], 1.0).then_inc(q["eyes"], 1)
            dve.wait_ge(q["eyes"], 1)
            for b in range(B):
                v.tensor_copy(cond_rep[:, b, :], cond_T[:, b:b + 1].to_broadcast([P, P])).then_inc(q["cond_rep_s"], 1)

            def moments(src, t0, n):
                for t in range(t0, t0 + n):
                    last = v.bn_stats(bn6[:, t, 0:6], src[:, t, :])
                link(last)
                for t in range(t0, t0 + n):
                    last = v.bn_aggr(mean_var[:, t, :], bn6[:, t, 0:6])
                link(last)

            logs_asked = [0]

            def inverse_std(t0, n):
                mean, var = mean_var[:, t0:t0 + n, 0], mean_var[:, t0:t0 + n, 1]
                r = lambda k: sml[:, k, 0:n]
                tt(r(1), mean, mean, ALU.mult)
                tt(r(1), r(1), var, ALU.add)
                ts(r(1), r(1), float(D), ALU.mult, EPS * EPS, ALU.max)
                rsqrt(r(4), r(1), n)
                tt(r(5), r(1), r(4), ALU.mult)
                logs_asked[0] += 1
                v.tensor_scalar(sml[:, 0, 0:n], r(5), MAX_TANH, None, ALU.min).then_inc(q["ln_num"], 1)
                dve.wait_ge(q["ln_num"], logs_asked[0])
                ts(r(5), r(1), 0.0625, ALU.min)
                ts(r(6), r(5), 1.0 / 9, ALU.mult, 1.0 / 7, ALU.add)
                for c in (1.0 / 5, 1.0 / 3, 1.0):
                    tt(r(6), r(6), r(5), ALU.mult)
                    ts(r(6), r(6), c, ALU.add)
                ts(r(7), r(1), 0.0625, ALU.is_lt)
                dve.wait_ge(q["ln_den"], logs_asked[0])
                tt(r(5), sml[:, 2, 0:n], sml[:, 3, 0:n], ALU.subtract)
                stt(r(5), r(5), 0.5, r(4), ALU.mult, ALU.mult)
                tt(r(6), r(6), r(5), ALU.subtract)
                tt(r(6), r(6), r(7), ALU.mult)
                tt(r(5), r(5), r(6), ALU.add)
                tt(r(5), r(5), r(5), ALU.mult)
                link(v.reciprocal(r(6), r(5)))
                stt(r(6), r(6), 1e-6, var, ALU.mult, ALU.add)
                rsqrt(r(5), r(6), n)

            def modulate(src, b, k_scale_row, k_shift_row, r0, done=None):
                for t in range(TB):
                    last = v.tensor_scalar(h_mod[:, b * TB + t, :], src[:, b * TB + t, :], mean_var[:, b * TB + t, 0:1],
                                           sml[:, 5, r0 + t:r0 + t + 1], ALU.subtract, ALU.mult)
                link(last)
                hb = h_mod[:, b * TB:(b + 1) * TB, :]
                wide = lambda k: ada[:, b, k, :].unsqueeze(1).to_broadcast([P, TB, D])
                tt(hb, hb, wide(k_scale_row), ALU.mult)
                link(v.tensor_tensor(hb, hb, wide(k_shift_row), ALU.add))
                for t in range(TB):
                    last = v.tensor_tensor_reduce(out=junk[:, t, :], in0=h_mod[:, b * TB + t, :], in1=h_mod[:, b * TB + t, :],
                                                  scale=1.0, scalar=0.0, op0=ALU.mult, op1=ALU.add,
                                                  accum_out=sml[:, 6, t:t + 1])
                link(last)
                ts(sml[:, 6, 0:TB], sml[:, 6, 0:TB], EPS * EPS, ALU.max)
                rsqrt(sml[:, 7, 0:TB], sml[:, 6, 0:TB], TB)
                last = v.tensor_scalar(sml[:, 7, 0:TB], sml[:, 7, 0:TB], MAX_ARTANH, 1.0, ALU.mult, ALU.min)
                if done is None:
                    link(last)
                else:
                    publish(last, done, b + 1)

            dve.wait_ge(q["x_in_s"], 16)
            moments(x_in, 0, T)
            inverse_std(0, T)
            dve.wait_ge(q["w_a_in"], 16 * 8)
            for b in range(B):
                dve.wait_ge(q["ada_mm"], b + 1)
                for half in range(2):
                    last = v.tensor_tensor(ada[:, b, 3 * half:3 * half + 3, :].rearrange("p k d -> p (k d)"),
                                           bk(2 * b + half, 3 * D), b_ada_sb[:, half * 3 * D:(half + 1) * 3 * D], ALU.add)
                link(last)
                for k in (1, 4):
                    last = v.tensor_scalar(ada[:, b, k, :], ada[:, b, k, :], 1.0, None, ALU.add)
                last.then_inc(q["ada_s"], 1)
            dve.wait_ge(q["ada_s"], B)
            for b in range(B):
                modulate(x_in, b, 1, 0, b * TB, q["hmod_s"])
                for t in range(TB):
                    n = b * TB + t
                    dve.wait_ge(q["qkv_mm"], n + 1)
                    v.scalar_tensor_tensor(u_qkv[:, t, :, :].rearrange("p h d -> p (h d)"), bk(6 + n % 2, 3 * D),
                                           sml[:, 7, t:t + 1], b_qkv_sb[:, :], ALU.mult, ALU.add).then_inc(q["u_s"], 1)
                    dve.wait_ge(q["usq_s"], 2 * n + 1)
                    v.tensor_reduce(head_sq[:, t, :],
                                    sq[:, 512 * (n % 2):512 * (n % 2) + 3 * D].rearrange("p (h d) -> p h d", d=HD),
                                    AXX, ALU.add).then_inc(q["usq_s"], 1)
                dve.wait_ge(q["usq_s"], 2 * TB * (b + 1))
                flat = lambda a: a[:, :, :].rearrange("p t h -> p (t h)")
                link(v.tensor_reduce(all_sq[:, :, :].rearrange("p t i -> p (t i)"),
                                     head_sq[:, :, :].rearrange("p t (i h) -> p (t i) h", h=H), AXX, ALU.add))
                ts(flat(head_sq), flat(head_sq), EPS * EPS, ALU.max)
                ts(flat(all_sq), flat(all_sq), EPS * EPS, ALU.max)
                rsqrt(flat(head_f), flat(head_sq), TB * 3 * H)
                rsqrt(flat(all_f), flat(all_sq), TB * 3)
                ts(flat(all_f), flat(all_f), RATIO * MAX_ARTANH, ALU.mult, RATIO, ALU.min)
                ts(flat(head_f), flat(head_f), MAX_ARTANH, ALU.mult)
                hf = head_f[:, :, :].rearrange("p t (i h) -> p (t i) h", h=H)
                tt(hf, hf, all_f[:, :, :].rearrange("p t i -> p (t i)").unsqueeze(2).to_broadcast([P, TB * 3, H]), ALU.min)
                ts(head_f[:, :, 0:2 * H], head_f[:, :, 0:2 * H], 2.0 ** EXP_SCALE_BITS, ALU.mult)
                ts(head_f[:, :, 2 * H:3 * H], head_f[:, :, 2 * H:3 * H], 1.0 / RATIO, ALU.mult)
                if b == 0:
                    dve.wait_ge(q["zero_s"], 3)
                for t in range(TB):
                    n = b * TB + t
                    v.tensor_tensor(v_aug[:, n, :, 0:HD], u_qkv[:, t, 2 * H:3 * H, :],
                                    head_f[:, t, 2 * H:3 * H].unsqueeze(2).to_broadcast([P, H, HD]), ALU.mult)
                    if n >= 2:
                        dve.wait_ge(q["qkT_mm"], n - 1)
                    qf, kf = qk_f[:, n % 2, 0:H, :], qk_f[:, n % 2, H:2 * H, :]
                    qs, ks = q_split[:, n % 2, :, :, :], k_split[:, n % 2, :, :, :]
                    tt(qk_f[:, n % 2, :, :], u_qkv[:, t, 0:2 * H, :],
                       head_f[:, t, 0:2 * H].unsqueeze(2).to_broadcast([P, 2 * H, HD]), ALU.mult)
                    twice = lambda a: a.unsqueeze(2).to_broadcast([P, H, 2, HD])
                    v.tensor_copy(qs[:, :, 0:2, :], twice(qf))
                    link(v.tensor_copy(ks[:, :, 0:3:2, :], twice(kf)))
                    v.tensor_tensor(qs[:, :, 2:4, :], twice(qf), qs[:, :, 0:2, :], ALU.subtract)
                    v.tensor_tensor(ks[:, :, 1:4:2, :], twice(kf), ks[:, :, 0:3:2, :], ALU.subtract).then_inc(q["split_s"], 1)

            for bg in range(B * G):
                b, g = divmod(bg, G)
                dve.wait_ge(q["pv_mm"], (bg + 1) * TB * 2)
                v.tensor_copy(o_raw[:, :], bk(4 + bg % 2)).then_inc(q["oraw_s"], 1)
                dve.wait_ge(q["den_mm"], bg + 1)
                link(v.reciprocal(den_r[:, :], bk(6)))
                if b >= 1 and g == 0:
                    dve.wait_ge(q["wo_mm"], b)
                publish(v.tensor_tensor(o_T[:, g, :], o_raw[:, :], den_r[:, :], ALU.mult), q["oT_s"], bg + 1)

            tanh_asked = [0]

            def mobius_step(b, k_gate, x_old, x_new, done=None):
                r = lambda k: sml[:, k, 0:TB]
                gate = ada[:, b, k_gate, :].unsqueeze(1).to_broadcast([P, TB, D])
                tt(w_sb[:, :, :], a_sb[:, b, :, :], gate, ALU.mult)
                for t in range(TB):
                    xt = x_old[:, b * TB + t, :]
                    for i, (k, l, m) in enumerate(((10, a_sb[:, b, t, :], a_sb[:, b, t, :]), (11, w_sb[:, t, :], w_sb[:, t, :]),
                                    (12, xt, w_sb[:, t, :]), (13, xt, xt))):
                        last = v.tensor_tensor_reduce(out=junk[:, 4 * t + i, :], in0=l, in1=m, scale=1.0, scalar=0.0,
                                                      op0=ALU.mult, op1=ALU.add, accum_out=sml[:, k, t:t + 1])
                link(last)
                ts(r(14), r(10), EPS * EPS, ALU.max)
                rsqrt(r(15), r(14), TB)
                ts(r(15), r(15), MAX_ARTANH, ALU.mult, 1.0, ALU.min)
                ts(r(14), r(11), EPS * EPS, ALU.max)
                rsqrt(r(16), r(14), TB)
                tt(r(16), r(16), r(14), ALU.mult)
                tt(r(16), r(16), r(15), ALU.mult)
                tanh_asked[0] += 1
                v.tensor_scalar(r(8), r(16), EPS, None, ALU.max).then_inc(q["tanh_in"], 1)
                dve.wait_ge(q["tanh_in"], tanh_asked[0])
                link(v.reciprocal(r(16), r(8)))
                tt(r(15), r(15), r(16), ALU.mult)
                dve.wait_ge(q["tanh_s"], tanh_asked[0])
                tt(r(15), r(15), r(9), ALU.mult)
                tt(r(12), r(12), r(15), ALU.mult)
                tt(r(11), r(11), r(15), ALU.mult)
                tt(r(11), r(11), r(15), ALU.mult)
                ts(r(12), r(12), 2.0, ALU.mult, 1.0, ALU.add)
                tt(r(17), r(13), r(11), ALU.mult)
                tt(r(17), r(17), r(12), ALU.add)
                ts(r(17), r(17), EPS, ALU.max)
                link(v.reciprocal(r(18), r(17)))
                tt(r(12), r(12), r(11), ALU.add)
                tt(r(12), r(12), r(18), ALU.mult)
                ts(r(13), r(13), -1.0, ALU.mult, 1.0, ALU.add)
                tt(r(13), r(13), r(15), ALU.mult)
                tt(r(13), r(13), r(18), ALU.mult)
                for t in range(TB):
                    last = v.tensor_scalar(w_sb[:, t, :], w_sb[:, t, :], sml[:, 13, t:t + 1], None, ALU.mult)
                link(last)
                for t in range(TB):
                    last = v.scalar_tensor_tensor(x_new[:, b * TB + t, :], x_old[:, b * TB + t, :], sml[:, 12, t:t + 1],
                                                  w_sb[:, t, :], ALU.mult, ALU.add)
                if done is None:
                    link(last)
                else:
                    publish(last, done, b + 1)

            dve.wait_ge(q["rope_s"], 4 * DEPTH)
            for b in range(B):
                dve.wait_ge(q["a_s"], b + 1)
                mobius_step(b, 2, x_in, x_mid)
                moments(x_mid, b * TB, TB)
                inverse_std(b * TB, TB)
                modulate(x_mid, b, 4, 3, 0)
                for t in range(TB):
                    last = v.tensor_scalar(h_mod[:, b * TB + t, :], h_mod[:, b * TB + t, :], sml[:, 7, t:t + 1], None, ALU.mult)
                last.then_inc(q["h2_s"], 1)

            dve.wait_ge(q["ffw_in"], 16 * 9)
            for b in range(B):
                dve.wait_ge(q["zsq_mm"], b + 1)
                ts(sml[:, 6, 0:TB], bank[:, 3, 0:TB], EPS * EPS, ALU.max)
                rsqrt(sml[:, 7, 0:TB], sml[:, 6, 0:TB], TB)
                ts(sml[:, 7, 0:TB], sml[:, 7, 0:TB], MAX_ARTANH, ALU.mult, 1.0, ALU.min)
                dve.wait_ge(q["z2_mm"], b + 1)
                for t in range(TB):
                    last = v.scalar_tensor_tensor(a_sb[:, b, t, :], bank[:, 4, t * P:(t + 1) * P], sml[:, 7, t:t + 1],
                                                  b_f2_sb[:, :], ALU.mult, ALU.add)
                last.then_inc(q["z2_used"], 1)
                dve.wait_ge(q["z2_used"], b + 1)
                mobius_step(b, 5, x_mid, xr, q["x2_s"])

            dve.wait_ge(q["rope_s"], 4 * DEPTH)
            dve.wait_ge(q["x2_s"], B)
            for l in range(DEPTH):
                for u in range(T // 2):
                    for n in (2 * u, 2 * u + 1):
                        i = l * T + n
                        dve.wait_ge(q["lsq_s"], i + 1)
                        v.tensor_reduce(norm_sq[:, n, :], qk_sq[:, i % 2, :].rearrange("p (h d) -> p h d", d=LD),
                                        AXX, ALU.add).then_inc(q["lred_s"], 1)
                        if i >= 4:
                            dve.wait_ge(q["lqkT_mm"], i - 3)
                        for k in range(2):
                            last = v.tensor_tensor(qk_rot[:, i % 4, k * INNER:(k + 1) * INNER].rearrange("p (h d) -> p h d", d=LD),
                                                   qk_raw[:, i % 2, k * INNER:(k + 1) * INNER].rearrange("p (h d) -> p h d", d=LD),
                                                   rope_l[:, l, k, n % TB, :].unsqueeze(1).to_broadcast([P, LH, LD]), ALU.mult)
                        link(last)
                        dve.wait_ge(q["lc_s"], i + 1)
                        publish(v.tensor_tensor(qk_rot[:, i % 4, :], qk_rot[:, i % 4, :], qk_cross[:, i % 2, :], ALU.add), q["lx_s"], i + 1)
                    dve.wait_ge(q["lred_s"], l * T + 2 * u + 2)
                    pair = lambda a: a[:, 2 * u:2 * u + 2, :].rearrange("p t h -> p (t h)")
                    ts(pair(norm_sq), pair(norm_sq), 1e-24, ALU.max)
                    rsqrt(pair(norm_r), pair(norm_sq), 4 * LH)
                    for n in (2 * u, 2 * u + 1):
                        i = l * T + n
                        to = qk_rot[:, i % 4, :].rearrange("p (h d) -> p h d", d=LD)
                        publish(v.tensor_tensor(to, to, norm_r[:, n, :].unsqueeze(2).to_broadcast([P, 2 * LH, LD]), ALU.mult),
                                q["lrot_s"], i + 1)
                for w in range(NW + 5):
                    if w < NW:
                        j = l * NW + w
                        dve.wait_ge(q["ls_mm"], j + 1)
                        S4 = bk(j % 2).rearrange("p (r c) -> p r c", r=PAIRS)
                        link(v.tensor_reduce(row_max[:, j % 2, :], S4, AXX, ALU.max))
                        if j >= 2:
                            dve.wait_ge(q["lp_s"], j - 1)
                        v.tensor_tensor(s_rel[:, j % 2, :, :], S4, row_max[:, j % 2, :].unsqueeze(2).to_broadcast([P, PAIRS, P]),
                                        ALU.subtract).then_inc(q["lrel_s"], 1)
                    if 3 <= w <= NW + 2:
                        j = l * NW + w - 3
                        dve.wait_ge(q["lpv_mm"], j + 1)
                        O4 = bk(4 + j % 2, PAIRS * (LD + 1)).rearrange("p (r d) -> p r d", r=PAIRS)
                        if j >= 2:
                            dve.wait_ge(q["loT_mm"], j - 1)
                        link(v.reciprocal(o_den[:, j % 2, :], O4[:, :, LD]))
                        v.tensor_tensor(o_loc[:, j % 2, :, :], O4[:, :, 0:LD], o_den[:, j % 2, :].unsqueeze(2).to_broadcast([P, PAIRS, LD]),
                                        ALU.mult).then_inc(q["lo_s"], 1)
                    if w >= 5 and w % 2 == 1:
                        n = (w - 5) // 2
                        dve.wait_ge(q["lwo_mm"], l * T + n + 1)
                        v.tensor_tensor(xr[:, n, :], xr[:, n, :], bank[:, 7, (n % 4) * P:(n % 4 + 1) * P], ALU.add).then_inc(q["lx1_s"], 1)
                dve.wait_ge(q["lx1_s"], (l + 1) * T)
                for b in range(B):
                    m = l * B + b
                    ns = range(b * TB, (b + 1) * TB)
                    dve.wait_ge(q["lsh_mm"], m + 1)
                    up = lambda n: bank[:, b, n % TB * 64:n % TB * 64 + 64]
                    for n in ns:
                        v.bn_stats(bn6[:, n, 0:6], xr[:, n, 0:64])
                        last = v.bn_stats(bn6[:, n, 6:12], up(n))
                    link(last)
                    for n in ns:
                        last = v.bn_aggr(mean_var[:, n, :], bn6[:, n, :])
                    link(last)
                    ts(sml[:, 1, 0:TB], mean_var[:, b * TB:(b + 1) * TB, 1], 1e-5, ALU.add)
                    rsqrt(sml[:, 5, 0:TB], sml[:, 1, 0:TB], TB)
                    for n in ns:
                        r = sml[:, 5, n % TB:n % TB + 1]
                        v.tensor_scalar(h_mod[:, n, 0:64], xr[:, n, 0:64], mean_var[:, n, 0:1], r, ALU.subtract, ALU.mult)
                        last = v.tensor_scalar(h_mod[:, n, 64:128], up(n), mean_var[:, n, 0:1], r, ALU.subtract, ALU.mult)
                    publish(last, q["lhn_s"], m + 1)
                dve.wait_ge(q["lqkT_mm"], (l + 1) * T)
                for b in range(B):
                    m = l * B + b
                    for c, (c0, cn) in enumerate(HC):
                        i = m * NH + c
                        dve.wait_ge(q["lgate_s"], i + 1)
                        dve.wait_ge(q["la_mm"], i + 1)
                        v.scalar_tensor_tensor(ff_T[0:cn, b, c, :], bank[0:cn, 2 + i % 2, :], b1_sb[0:cn, l, 0, c:c + 1],
                                               gate_T[0:cn, i % 2, :], ALU.add, ALU.mult).then_inc(q["lff_s"], 1)
                    xb = xr[:, b * TB:(b + 1) * TB, :]
                    tt(xb, xb, b2_sb[:, l, :].unsqueeze(1).to_broadcast([P, TB, D]), ALU.add)
                    dve.wait_ge(q["lf2_mm"], m + 1)
                    publish(v.tensor_tensor(xb, xb, bk(6 + b).rearrange("p (t d) -> p t d", d=D), ALU.add), q["lx2_s"], m + 1)
            v.tensor_tensor(xr[:, :, :], xr[:, :, :], x_in[:, :, :], ALU.add).then_inc(q["lx2_s"], 1)


_INS = ['x', 'cond_1024', 'L0_cond_w_q', 'L0_cond_b_q', 'L0_cond_w_k', 'L0_cond_b_k', 'L0_cond_w_v', 'L0_cond_b_v',
        'L0_cond_w_o', 'L0_cond_b_o', 'L0_cond_w_f1', 'L0_cond_b_f1', 'L0_cond_w_f2', 'L0_cond_b_f2', 'L0_cond_w_ada',
        'L0_cond_b_ada', 'L0_ffn_wqkv', 'L0_ffn_q_scale', 'L0_ffn_k_scale', 'L0_ffn_wo', 'L0_ffn_ln_g', 'L0_ffn_ln_b',
        'L0_ffn_w1', 'L0_ffn_b1', 'L0_ffn_w2', 'L0_ffn_b2']


def _constants(S, depth_head, window):
    import numpy as np
    f = np.float32
    half = np.arange(0, depth_head, 2, dtype=f)
    inv = (f(1.0) / f(10000.0) ** (half / f(depth_head))).astype(f)
    t = np.arange(S, dtype=f)
    fr = (t[:, None] * inv[None, :]).astype(f)
    fr = np.concatenate([fr, fr], -1)
    base = (half + f(0.4 * depth_head)) / f(1.4 * depth_head)
    power = (t - S // 2) / f(window // 2)
    sc = (base[None, :] ** power[:, None]).astype(f)
    sc = np.concatenate([sc, sc], -1)
    cos, sin = np.cos(fr).astype(f), np.sin(fr).astype(f)
    sign = np.concatenate([-np.ones(depth_head // 2, f), np.ones(depth_head // 2, f)])
    rope = np.stack([cos * sc, cos / sc, sign * sin * sc, sign * sin / sc]).astype(f)
    i = np.arange(128)[:, None] % window
    j = np.arange(2 * window)[None, :]
    band = np.where((j >= i) & (j <= i + window), f(0), f(-1e30)).astype(f)
    first = np.where(j >= window, band, f(-1e30)).astype(f)
    masks = np.stack([band, first])
    eye = np.eye(128, dtype=f)
    shift = np.zeros((2, 128, 128), f)
    shift[0, np.arange(127), np.arange(1, 128)] = 1
    shift[1, 127, 0] = 1
    pick = np.zeros((128, 128), f)
    for r in range(128):
        pick[32 * (r // 32) + 8, r] = 1
    return {'rope': rope, 'masks': masks, 'eye': eye, 'shift': shift, 'denom_pick': pick}


def kernel(**inputs):
    import numpy as _np
    import concourse.bacc as _bacc
    from concourse import mybir as _mybir
    from concourse.bass_utils import run_bass_kernel_spmd as _run

    nc = _bacc.Bacc("TRN2", target_bir_lowering=False, num_devices=1)
    arrays, args = {}, []
    values = {n: inputs[n] for n in _INS}
    shape = values['x'].shape
    values['cond_1024'] = _np.asarray(values['cond_1024']).T
    values['L0_cond_b_f1'] = _np.asarray(values['L0_cond_b_f1']).reshape(-1, 128).T
    values['L0_ffn_ln_g'] = _np.asarray(values['L0_ffn_ln_g']).T
    values['L0_ffn_ln_b'] = _np.asarray(values['L0_ffn_ln_b']).T
    b1 = _np.asarray(values['L0_ffn_b1'])
    depth, hid = b1.shape[0], b1.shape[1] // 2
    b1 = _np.pad(b1.reshape(depth, 2, hid), ((0, 0), (0, 0), (0, -hid % 128)))
    values['L0_ffn_b1'] = b1.reshape(depth * 2 * (b1.shape[2] // 128), 128).T
    values.update(_constants(shape[1], values['L0_ffn_q_scale'].shape[1], 64))
    for name, a in values.items():
        a = _np.ascontiguousarray(a)
        arrays[f"in_{name}"] = a
        args.append(nc.dram_tensor(f"in_{name}", a.shape, _mybir.dt.from_np(a.dtype), kind="ExternalInput").ap())
    args.append(nc.dram_tensor("out_0", shape, _mybir.dt.float32, kind="ExternalOutput").ap())
    adaln_ffn_kernel(nc, *args)
    r = _run(nc, [arrays], core_ids=[0])
    return r.results[0]["out_0"]
```

```python
import math
from contextlib import ExitStack

import concourse.bass as bass
from concourse import mybir

F32 = mybir.dt.float32
F16 = mybir.dt.float16
BF16 = mybir.dt.bfloat16
I32 = mybir.dt.int32
ALU = mybir.AluOpType
ACT = mybir.ActivationFunctionType
AXX = mybir.AxisListType.X

P = 128
EPS = 1e-7
MAX_TANH = 0.99998998641967773438
MAX_ARTANH = 0.5 * math.log((1 + MAX_TANH) / (1 - MAX_TANH))
EXP_SCALE_BITS = 12
RSQRT_MAGIC = 0x5F3759DF


def adaln_ffn_kernel(
    nc, x, cond_1024,
    w_q, b_q, w_k, b_k, w_v, b_v, w_o, b_o, w_f1, b_f1, w_f2, b_f2, w_ada, b_ada,
    wqkv, q_scale, k_scale, wo, ln_g, ln_b, w1, b1, w2, b2,
    rope, masks, eye, shift, denom_pick, out,
):
    B, S, D = x.shape
    TB = S // P
    T = B * TB
    H, HD = 16, D // 16
    G = H // 4
    FF = w_f1.shape[1]
    FC = FF // P
    beta = lambda a, b: math.exp(math.lgamma(a) + math.lgamma(b) - math.lgamma(a + b))
    RATIO = beta(HD / 2, 0.5) / beta(D / 2, 0.5)
    DEPTH, _, QKV = wqkv.shape
    INNER = QKV // 3
    LD = q_scale.shape[1]
    LH = INNER // LD
    PAIRS = LH // 2
    WIN = P // 2
    NW = T * 2
    HID = w2.shape[1]
    HC = [(c, min(P, HID - c)) for c in range(0, HID, P)]
    NH = len(HC)
    QK_SCALE = 8.0

    with ExitStack() as ctx:
        def sb(name, shape, dt=F32):
            return ctx.enter_context(nc.sbuf_tensor(name, shape, dt))

        def sem(name):
            return ctx.enter_context(nc.semaphore(name))

        bank = ctx.enter_context(nc.psum_tensor("bank", [P, 8, 512], F32))

        def bk(i, n=512):
            return bank[:, i, 0:n]

        eye_f = sb("eye_f", [P, P])
        eye_h = sb("eye_h", [P, P], F16)
        eye_b = sb("eye_b", [P, P], BF16)
        shift_f = sb("shift_f", [P, 2, P])
        pick_f = sb("pick_f", [P, P])
        ones_col = sb("ones_col", [P, 1])
        mask_f = sb("mask_f", [P, 2, P])
        mask_b = sb("mask_b", [P, 2, P], BF16)
        cond_T = sb("cond_T", [P, B])
        b_f1_sb = sb("b_f1_sb", [P, FC])
        x_in = sb("x_in", [P, T, D])
        xr = sb("xr", [P, T, D])

        bn6 = sb("bn6", [P, T, 12])
        mean_var = sb("mean_var", [P, T, 2])
        sml = sb("sml", [P, 32, 8])
        nt_i = sb("nt_i", [P, 256], I32)
        nt_f = sb("nt_f", [P, 256])
        h_mod = sb("h_mod", [P, T, D])
        hT = sb("hT", [P, T * P])
        room_q = sb("room_q", [P, PAIRS * NW * P])
        room_k = sb("room_k", [P, PAIRS * B * (S + WIN)])
        room_v = sb("room_v", [P, 2 * T * LH * (LD + 1)])
        room_r = sb("room_r", [P, 12 * 512])
        room_s = sb("room_s", [P, 9 * 512])

        def carve(room):
            at = [0]

            def take(pattern, n, **sizes):
                a = room[:, at[0]:at[0] + n].rearrange(f"p ({pattern}) -> p {pattern}", **sizes)
                at[0] += n
                return a
            return take

        room_w = sb("room_w", [P, 4224])
        room_a = sb("room_a", [P, B * 6 * D])
        room_m = sb("room_m", [P, 1026])
        take = carve(room_w)
        cond_rep = take("b n", B * P, b=B)
        w_ada_sb = take("n", 6 * D)
        b_ada_sb = take("n", 6 * D)
        w_qkv_sb = take("n", 3 * D)
        b_qkv_sb = take("n", 3 * D)
        w_o_sb = take("g n", G * D, g=G)
        w_f1_sb = take("n", FF)
        w_f2_sb = take("c n", FC * D, c=FC)
        b_f2_sb = take("n", D)
        ada = room_a[:, :].rearrange("p (b k d) -> p b k d", b=B, k=6)
        x_mid = room_m[:, 0:T * D].rearrange("p (t d) -> p t d", t=T)
        take = carve(room_r)
        probs = take("r i n", 6 * 512, r=3, i=2)
        o_raw = take("n", 512)
        den_r = take("n", 512)
        o_T = take("g n", G * S, g=G)
        head_sq = sb("head_sq", [P, TB, 3 * H])
        all_sq = sb("all_sq", [P, TB, 3])
        head_f = sb("head_f", [P, TB, 3 * H])
        all_f = sb("all_f", [P, TB, 3])
        qk_f = sb("qk_f", [P, 2, 2 * H, HD])
        q_split = sb("q_split", [P, 2, H, 4, HD], F16)
        k_split = sb("k_split", [P, 2, H, 4, HD], F16)
        half_k = G * T * P // 2
        q_T = room_k[:, 0:half_k].bitcast(F16).rearrange("p (g n) -> p g n", g=G)
        k_T = room_k[:, half_k:2 * half_k].bitcast(F16).rearrange("p (g n) -> p g n", g=G)
        k_pad = room_q[:, :].bitcast(F16).rearrange("p (g j n) -> p g j n", g=G, j=4)
        take = carve(room_v)
        v_aug = take("t h d", T * H * 32, t=T, d=32)
        z_T = take("c n", FC * S, c=FC)
        z_sq = take("c n", FC * S, c=FC)
        u_qkv = z_T[:, :, :].rearrange("p c n -> p (c n)")[:, 0:TB * 3 * D].rearrange("p (t h d) -> p t h d", t=TB, d=HD)
        take = carve(room_s)
        a_sb = take("b t d", T * D, b=B, d=D)
        w_sb = take("t d", TB * D, d=D)
        junk = take("i d", 16 * D, d=D)
        sq = take("n", 1024)

        q_blk = room_q[:, :].rearrange("p (r w c) -> p r w c", r=PAIRS, c=P)
        k_loc = room_k[:, :].rearrange("p (r b n) -> p r b n", r=PAIRS, b=B)
        v_loc = room_v[:, :].rearrange("p (k t h d) -> p k t h d", k=2, t=T, d=LD + 1)
        take = carve(room_r)
        qk_rot = take("r n", 4 * 2 * INNER, r=4)
        qk_cross = take("r n", 2 * 2 * INNER, r=2)
        take = carve(room_s)
        qk_raw = take("r n", 2 * 2 * INNER, r=2)
        qk_sq = take("r n", 2 * 2 * INNER, r=2)
        wqkv_sb = sb("wqkv_sb", [P, QKV])
        wo_sb = sb("wo_sb", [P, 2, 2, D])
        w1_sb = sb("w1_sb", [P, 2 * HID])
        w2_sb = sb("w2_sb", [P, NH, D])
        b1_sb = sb("b1_sb", [P, DEPTH, 2, NH])
        b2_sb = sb("b2_sb", [P, DEPTH, D])
        ln_gb = sb("ln_gb", [P, 2, DEPTH])
        rope_l = sb("rope_l", [P, DEPTH, 4, TB, LD])
        scale_sb = room_m[:, 0:DEPTH * 4 * LD].rearrange("p (l k d) -> p l k d", l=DEPTH, k=4)
        hs_T = room_m[:, 0:B * (S + 1)].rearrange("p (b n) -> p b n", b=B)
        norm_sq = sb("norm_sq", [P, T, 2 * LH])
        norm_r = sb("norm_r", [P, T, 2 * LH])
        row_max = sb("row_max", [P, 2, PAIRS])
        o_den = sb("o_den", [P, 2, PAIRS])
        take = carve(room_w)
        s_rel = take("k r c", 2 * PAIRS * P, k=2, r=PAIRS)
        p_loc = take("k r c", 2 * PAIRS * P, k=2, r=PAIRS)
        pT_loc = take("k r c", 2 * PAIRS * P, k=2, r=PAIRS)
        oT_loc = take("k r a c", 2 * 4 * P, k=2, r=2, a=2)
        take = carve(room_a)
        gate_T = take("k n", 2 * S, k=2)
        o_loc = take("k r d", 2 * PAIRS * LD, k=2, r=PAIRS)
        ff_T = room_r[:, 0:B * NH * S].rearrange("p (b c n) -> p b c n", b=B, c=NH)

        names = """consts w_a_in x_in_s ffw_in lw_in eyes cond_rep_s ada_mm ada_used ada_s dve_step act_step ln_num ln_den
        hmod_s hT_mm hT_s qkv_mm u_s usq_s split_s qkT_mm qkT_s kpad_0 kpad_1 zero_s
        scores_mm probs_s pv_mm oraw_s den_mm oT_s wo_mm a_s tanh_in tanh_s
        h2_s h2T_mm h2T_s z_mm z_s zsq_mm z2_mm z2_used x2_s out_s
        rope_in room_s_ rope_s lwt lw_qkv lw_wo lw_ff lT_mm lT_s lqk_mm lqk_s lv_mm lv_s lsq_s lred_s lc_s lx_s lrot_s lqkT_mm lqkT_s
        ls_mm lmax_s lrel_s lp_s lpT_mm lpT_s lpv_mm lo_s loT_mm loT_s lwo_mm lx1_s lsh_mm lhn_s lhT_mm lhT_s
        la_mm lg_mm lgate_s lff_s lf2_mm lx2_s""".split()
        q = {n: sem(n) for n in names}
        kpad_s = [q["kpad_0"], q["kpad_1"]]

        NB = NW // B
        NS = G * TB * 2
        LENGTH = dict(pre=14 + 2 * TB, att=NS + 5, post=28 + FC, rope=TB + 4, win=NB + 5, feed=NH + 6)

        def spread(part, kind, a=0.0, b=1.0):
            here = end = step = 0.0
            for y in part:
                if y is None:
                    here = min(here + step, end)
                elif isinstance(y, tuple):
                    here, end, step = y[0], y[1], (y[1] - y[0]) / y[2]
                else:
                    here, end, step = y, y, 0.0
                yield a + (b - a) * here / LENGTH[kind]

        def one_after_another(*parts):
            for part in parts:
                yield from part

        def together(*parts):
            live = [[next(part), k, part] for k, part in enumerate(parts)]
            while live:
                first = min(live, key=lambda p: p[:2])
                at = next(first[2], None)
                if at is None:
                    live.remove(first)
                else:
                    first[0] = at

        def schedule(pre, att, post, rope_part, windows, feed):
            together(spread(pre(0), "pre"))
            together(spread(att(0), "att"), spread(pre(1), "pre"))
            together(spread(att(1), "att"), spread(post(0), "post"))
            together(spread(post(1), "post"))
            together(spread(rope_part(0, 0), "rope"))
            together(spread(windows(0, 0), "win"), spread(rope_part(0, 1), "rope"))
            for l in range(DEPTH - 1):
                for b in range(B):
                    together(spread(windows(l + b, 1 - b), "win"),
                             one_after_another(spread(feed(l, b), "feed", 0.0, 0.5), spread(rope_part(l + 1, b), "rope", 0.5, 1.0)))
            together(spread(windows(DEPTH - 1, 1), "win"), spread(feed(DEPTH - 1, 0), "feed"))
            together(spread(feed(DEPTH - 1, 1), "feed"))

        block = ctx.enter_context(nc.Block())

        @block.sync
        def _(sp):
            row = lambda a, n: a.rearrange("(o n) -> o n", o=1).to_broadcast([P, n])
            sp.dma_start(x_in[:, :, :], x.rearrange("b (t p) d -> p (b t) d", p=P)).then_inc(q["x_in_s"], 16)
            sp.dma_start(eye_f[:, :], eye).then_inc(q["consts"], 16)
            sp.dma_start(shift_f[:, :, :], shift.rearrange("k p m -> p k m")).then_inc(q["consts"], 16)
            sp.dma_start(pick_f[:, :], denom_pick).then_inc(q["consts"], 16)
            sp.dma_start(mask_f[:, :, :], masks.rearrange("k p m -> p k m")).then_inc(q["consts"], 16)
            sp.dma_start(cond_T[:, :], cond_1024).then_inc(q["consts"], 16)
            sp.dma_start(w_ada_sb[:, :], w_ada).then_inc(q["w_a_in"], 16)
            sp.dma_start(b_ada_sb[:, :], row(b_ada, 6 * D)).then_inc(q["w_a_in"], 16)
            for i, (w, b) in enumerate(((w_q, b_q), (w_k, b_k), (w_v, b_v))):
                sp.dma_start(w_qkv_sb[:, i * D:(i + 1) * D], w).then_inc(q["w_a_in"], 16)
                sp.dma_start(b_qkv_sb[:, i * D:(i + 1) * D], row(b, D)).then_inc(q["w_a_in"], 16)
            sp.wait_ge(q["zero_s"], 3)
            for j in range(4):
                sp.dma_start(w_o_sb[32 * j:32 * j + HD, :, :],
                             w_o.rearrange("(g j d) n -> j d g n", g=G, j=4)[j]).then_inc(q["ffw_in"], 16)
            sp.dma_start(w_o_sb[HD:HD + 1, 0, :], b_o.rearrange("(o n) -> o n", o=1)).then_inc(q["ffw_in"], 16)
            sp.dma_start(w_f1_sb[:, :], w_f1).then_inc(q["ffw_in"], 16)
            sp.dma_start(b_f1_sb[:, :], b_f1).then_inc(q["ffw_in"], 16)
            sp.dma_start(w_f2_sb[:, :, :], w_f2.rearrange("(c p) n -> p c n", p=P)).then_inc(q["ffw_in"], 16)
            sp.dma_start(b_f2_sb[:, :], row(b_f2, D)).then_inc(q["ffw_in"], 16)
            sp.dma_start(rope_l[:, DEPTH - 1, :, :, :], rope.rearrange("k (t p) d -> p k t d", p=P)).then_inc(q["rope_in"], 16)
            for l in range(DEPTH):
                for k, sc in enumerate((q_scale, k_scale)):
                    sp.dma_start(scale_sb[:, l, k, :], row(sc[l], LD)).then_inc(q["rope_in"], 16)
                    for h0 in (0, LD // 2):
                        h1 = LD // 2 - h0
                        sp.dma_start(scale_sb[:, l, 2 + k, h0:h0 + LD // 2], row(sc[l, h1:h1 + LD // 2], LD // 2)).then_inc(q["rope_in"], 16)
                sp.dma_start(b2_sb[:, l, :], row(b2[l], D)).then_inc(q["lwt"], 16)
            sp.dma_start(b1_sb[:, :, :, :], b1.rearrange("p (l k c) -> p l k c", l=DEPTH, k=2)).then_inc(q["lwt"], 16)
            for k, g in enumerate((ln_g, ln_b)):
                sp.dma_start(ln_gb[:, k, :], g).then_inc(q["lwt"], 16)

            def layer_weights(l):
                if l:
                    sp.wait_ge(q["lv_mm"], l * T)
                sp.dma_start(wqkv_sb[:, :], wqkv[l]).then_inc(q["lw_qkv"], 16)
                if l:
                    sp.wait_ge(q["lwo_mm"], l * T)
                for e in range(2):
                    for r in range(2):
                        sp.dma_start(wo_sb[LD * e:LD * e + LD, r, :, :],
                                     wo[l].rearrange("(r e a d) n -> r e d a n", r=2, e=2, a=2)[r, e]).then_inc(q["lw_wo"], 16)
                if l:
                    sp.wait_ge(q["lf2_mm"], l * B)
                sp.dma_start(w1_sb[:, :], w1[l]).then_inc(q["lw_ff"], 16)
                for c, (c0, cn) in enumerate(HC):
                    sp.dma_start(w2_sb[0:cn, c, :], w2[l, c0:c0 + cn, :]).then_inc(q["lw_ff"], 16)

            layer_weights(0)
            sp.wait_ge(q["zero_s"], 4)
            for b in range(B):
                sp.wait_ge(q["qkT_s"], 2 * TB * (b + 1))
                for j in range(4):
                    r = slice(32 * j, 32 * j + 32)
                    sp.dma_start(k_pad[r, :, j, b * S:(b + 1) * S], k_T[r, :, b * S:(b + 1) * S]).then_inc(kpad_s[b], 16)
            for l in range(1, DEPTH):
                layer_weights(l)
            sp.wait_ge(q["lx2_s"], 1 + B * DEPTH)
            sp.dma_start(out.rearrange("b (t p) d -> p (b t) d", p=P), xr[:, :, :]).then_inc(q["out_s"], 16)
            sp.wait_ge(q["out_s"], 16)

        @block.gpsimd
        def _(pool):
            nc.gpsimd.memset(v_aug[:, :, :, :], 0.0).then_inc(q["zero_s"], 1)
            nc.gpsimd.memset(w_o_sb[:, :, :], 0.0).then_inc(q["zero_s"], 1)
            pool.wait_ge(q["zero_s"], 2)
            nc.gpsimd.memset(v_aug[:, :, :, HD:HD + 1], 1.0).then_inc(q["zero_s"], 1)
            nc.gpsimd.memset(k_pad[:, :, :, :].rearrange("p g j t -> p (g j t)").bitcast(I32), 0).then_inc(q["zero_s"], 1)
            pool.wait_ge(q["rope_in"], 16 * (1 + 6 * DEPTH))
            for l in range(DEPTH):
                for k in range(4):
                    nc.gpsimd.tensor_tensor(rope_l[:, l, k, :, :], rope_l[:, DEPTH - 1, k, :, :],
                                            scale_sb[:, l, k, :].unsqueeze(1).to_broadcast([P, TB, LD]), ALU.mult).then_inc(q["rope_s"], 1)
            pool.wait_ge(q["x2_s"], B)
            nc.gpsimd.memset(q_blk, 0.0).then_inc(q["room_s_"], 1)
            nc.gpsimd.memset(k_loc[:, :, :, 0:WIN], 0.0).then_inc(q["room_s_"], 1)
            nc.gpsimd.memset(v_loc[:, 0, :, :, :], 0.0).then_inc(q["room_s_"], 1)
            pool.wait_ge(q["room_s_"], 3)
            nc.gpsimd.memset(hs_T[P // 2:P, :, 0:1], 0.0).then_inc(q["room_s_"], 1)
            pool.wait_ge(q["room_s_"], 4)
            nc.gpsimd.memset(v_loc[:, :, :, :, LD:LD + 1], 1.0).then_inc(q["room_s_"], 1)
            for l in range(DEPTH):
                for n in range(T):
                    i = l * T + n
                    pool.wait_ge(q["lqk_s"], 2 * (i + 1))
                    if i >= 2:
                        pool.wait_ge(q["lx_s"], i - 1)
                    for k in range(2):
                        pool_src = qk_raw[:, i % 2, k * INNER:(k + 1) * INNER].rearrange("p (h a d) -> p h a d", h=LH, a=2)
                        last = nc.gpsimd.tensor_tensor(
                            qk_cross[:, i % 2, k * INNER:(k + 1) * INNER].rearrange("p (h a d) -> p h a d", h=LH, a=2),
                            pool_src[:, :, ::-1, :],
                            rope_l[:, l, 2 + k, n % TB, :].rearrange("p (a d) -> p a d", a=2).unsqueeze(1)
                            .to_broadcast([P, LH, 2, LD // 2]), ALU.mult)
                    last.then_inc(q["lc_s"], 1)

        @block.tensor
        def _(pe):
            pe.wait_ge(q["consts"], 80)
            pe.wait_ge(q["eyes"], 1)
            pe.wait_ge(q["w_a_in"], 16 * 8)

            def transpose_mod(b, dst, src_ready, done):
                pe.wait_ge(src_ready, b + 1)
                for t in range(TB):
                    last = nc.tensor.transpose(bank[:, dst, t * P:(t + 1) * P], h_mod[:, b * TB + t, :], eye_f[:, :])
                last.then_inc(done, 1)

            def pre(b):
                yield 0
                if b == 0:
                    for c in range(B):
                        pe.wait_ge(q["cond_rep_s"], c + 1)
                        for half in range(2):
                            last = nc.tensor.matmul(bk(2 * c + half, 3 * D), cond_rep[:, c, :],
                                                    w_ada_sb[:, half * 3 * D:(half + 1) * 3 * D], start=True, stop=True)
                        last.then_inc(q["ada_mm"], 1)
                else:
                    pe.wait_ge(q["qkT_s"], 2 * TB * b)
                yield 4
                transpose_mod(b, 6, q["hmod_s"], q["hT_mm"])
                for t in range(TB):
                    yield 5 + t
                    n = b * TB + t
                    if t == 0:
                        pe.wait_ge(q["hT_s"], b + 1)
                    if t >= 2:
                        pe.wait_ge(q["u_s"], n - 1)
                    nc.tensor.matmul(bk(7 - t % 2, 3 * D), hT[:, n * P:(n + 1) * P], w_qkv_sb[:, :],
                                     start=True, stop=True).then_inc(q["qkv_mm"], 1)
                for t in range(TB):
                    yield 14 + 2 * t
                    n = b * TB + t
                    pe.wait_ge(q["split_s"], n + 1)
                    if t >= 2:
                        pe.wait_ge(q["qkT_s"], 2 * (n - 1))
                    dst = bank[:, 6 + t % 2, :].bitcast(F16)
                    for i, sp_t in enumerate((q_split, k_split)):
                        for g in range(G):
                            c = (i * G + g) * P
                            last = nc.tensor.transpose(dst[:, c:c + P],
                                                       sp_t[:, n % 2, 4 * g:4 * g + 4, :, :].rearrange("p a b c -> p (a b c)"),
                                                       eye_h[:, :])
                    last.then_inc(q["qkT_mm"], 1)

            steps = [(g, kt, hp) for g in range(G) for kt in range(TB) for hp in range(2)]

            def scores(b, i):
                g, kt, hp = steps[i]
                n = b * NS + i
                if i == 0:
                    pe.wait_ge(q["ada_s"], B)
                    pe.wait_ge(q["qkT_s"], 2 * TB * (b + 1))
                    pe.wait_ge(kpad_s[b], 64)
                if n >= 2:
                    pe.wait_ge(q["probs_s"], n - 1)
                for i in range(2):
                    j = 2 * hp + i
                    k0 = (b * TB + kt) * P
                    last = nc.tensor.matmul(bk(2 * (n % 2) + i), k_pad[:, g, j, k0:k0 + P],
                                            q_T[:, g, b * S:(b + 1) * S], start=True, stop=True)
                last.then_inc(q["scores_mm"], 1)

            def weigh(b, i):
                g, kt, hp = steps[i]
                n = b * NS + i
                bg = b * G + g
                pe.wait_ge(q["probs_s"], n + 1)
                if kt == 0 and hp == 0 and bg >= 2:
                    pe.wait_ge(q["oT_s"], bg - 1)
                for i in range(2):
                    j = 2 * hp + i
                    last = nc.tensor.matmul(bank[32 * j:32 * j + 32, 4 + bg % 2, :],
                                            v_aug[:, b * TB + kt, 4 * g + j, :], probs[:, n % 3, i, :],
                                            start=(kt == 0), stop=(kt == TB - 1), skip_group_check=True)
                last.then_inc(q["pv_mm"], 1)

            def att(b):
                per = TB * 2
                for i in range(NS + 5):
                    yield i
                    if i < NS:
                        scores(b, i)
                    if 2 <= i < NS + 2:
                        weigh(b, i - 2)
                    if i >= per + 4 and (i - 4) % per == 0:
                        bg = b * G + (i - 4) // per - 1
                        pe.wait_ge(q["oraw_s"], bg + 1)
                        nc.tensor.matmul(bk(4 + bg % 2), pick_f[:, :], o_raw[:, :], start=True, stop=True).then_inc(q["den_mm"], 1)

            def post(b):
                for t in range(TB):
                    yield t / TB
                    if t == 0:
                        pe.wait_ge(q["qkT_s"], 2 * T)
                        pe.wait_ge(q["oT_s"], G * (b + 1))
                        pe.wait_ge(q["ffw_in"], 16 * 9)
                        if b:
                            pe.wait_ge(q["z2_used"], b)
                    for g in range(G):
                        last = nc.tensor.matmul(bank[:, 6, t * P:(t + 1) * P], o_T[:, g, t * P:(t + 1) * P],
                                                w_o_sb[:, g, :], start=(g == 0), stop=(g == G - 1))
                last.then_inc(q["wo_mm"], 1)
                yield 17
                transpose_mod(b, 7, q["h2_s"], q["h2T_mm"])
                for c in range(FC):
                    yield 18 + c
                    n = b * FC + c
                    if c == 0:
                        pe.wait_ge(q["h2T_s"], b + 1)
                    if c >= 2:
                        pe.wait_ge(q["z_s"], 2 * (n - 1))
                    nc.tensor.matmul(bk(6 + c % 2), w_f1_sb[:, c * P:(c + 1) * P], hT[:, b * S:(b + 1) * S],
                                     start=True, stop=True).then_inc(q["z_mm"], 1)
                yield 18 + FC
                pe.wait_ge(q["z_s"], 2 * FC * (b + 1))
                for t in range(TB):
                    for c in range(FC):
                        last = nc.tensor.matmul(bank[:, 6, t:t + 1], z_sq[:, c, t * P:(t + 1) * P], ones_col[:, :],
                                                start=(c == 0), stop=(c == FC - 1))
                last.then_inc(q["zsq_mm"], 1)
                for t in range(TB):
                    yield 18 + FC + (t + 1) / TB
                    for c in range(FC):
                        last = nc.tensor.matmul(bank[:, 7, t * P:(t + 1) * P], z_T[:, c, t * P:(t + 1) * P],
                                                w_f2_sb[:, c, :], start=(c == 0), stop=(c == FC - 1))
                last.then_inc(q["z2_mm"], 1)

            def rope_part(l, b):
                m = l * B + b
                yield 0
                if m == 0:
                    pe.wait_ge(q["lwt"], 16 * (DEPTH + 3))
                else:
                    pe.wait_ge(q["lqkT_s"], m * TB)
                    pe.wait_ge(q["lv_s"], m * TB)
                if b == 0:
                    pe.wait_ge(q["lw_qkv"], 16 * (l + 1))
                pe.wait_ge(q["x2_s"], B) if l == 0 else pe.wait_ge(q["lx2_s"], m - B + 1)
                for t in range(TB):
                    last = nc.tensor.transpose(bank[:, 7, t * P:(t + 1) * P], xr[:, b * TB + t, :], eye_f[:, :])
                last.then_inc(q["lT_mm"], 1)
                for t in range(TB + 3):
                    i = m * TB + t
                    if t < TB:
                        for k in range(2):
                            yield 1 + t + k / 3
                            if t == 0 and k == 0:
                                pe.wait_ge(q["lT_s"], m + 1)
                            if i >= 1:
                                pe.wait_ge(q["lsq_s"], 2 * i + k - 1)
                            if t >= 4:
                                pe.wait_ge(q["lqkT_s"], i - 3)
                            nc.tensor.matmul(bk(5 + k), hs_T[:, b, t * P:(t + 1) * P],
                                             wqkv_sb[:, k * INNER:(k + 1) * INNER], start=True, stop=True).then_inc(q["lqk_mm"], 1)
                        yield 1 + t + 2 / 3
                        if i >= 1:
                            pe.wait_ge(q["lv_s"], i)
                        nc.tensor.matmul(bk(7), hs_T[:, b, t * P:(t + 1) * P], wqkv_sb[:, 2 * INNER:],
                                         start=True, stop=True).then_inc(q["lv_mm"], 1)
                    if t >= 3:
                        yield 1 + t + 0.9
                        i = m * TB + t - 3
                        pe.wait_ge(q["lrot_s"], i + 1)
                        pe.wait_ge(q["lsq_s"], 2 * (m * TB + min(t, TB - 1) + 1))
                        if i >= 1:
                            pe.wait_ge(q["lqkT_s"], i)
                        for c in range(2 * PAIRS):
                            last = nc.tensor.transpose(bank[:, 5 + c // PAIRS, (c % PAIRS) * P:(c % PAIRS + 1) * P],
                                                       qk_rot[:, i % 4, c * P:(c + 1) * P], eye_f[:, :])
                        last.then_inc(q["lqkT_mm"], 1)

            def windows(l, b):
                m = l * B + b
                for w in range(NB + 5):
                    yield w
                    if w == 0:
                        pe.wait_ge(q["lqkT_s"], (m + 1) * TB)
                        pe.wait_ge(q["lv_s"], (m + 1) * TB)
                    if w < NB:
                        j = m * NB + w
                        if j >= 2:
                            pe.wait_ge(q["lrel_s"], j - 1)
                        nc.tensor.matmul(bk(j % 2), eye_b[:, :], mask_b[:, int(w == 0), :].unsqueeze(1).to_broadcast([P, PAIRS, P]),
                                         start=True, stop=False)
                        for r in range(PAIRS):
                            last = nc.tensor.matmul(bank[:, j % 2, r * P:(r + 1) * P], q_blk[:, r, b * NB + w, :],
                                                    k_loc[:, r, b, w * WIN:w * WIN + P], start=False, stop=(r == PAIRS - 1))
                        last.then_inc(q["ls_mm"], 1)
                    if w >= 6 and w % 2 == 0:
                        i = m * TB + (w - 6) // 2
                        if b == 0 and w == 6:
                            pe.wait_ge(q["lw_wo"], 64 * (l + 1))
                        pe.wait_ge(q["loT_s"], min(2 * i + 3, NB * (m + 1)))
                        for c in range(4):
                            last = nc.tensor.matmul(bank[:, 4, 2 * P:3 * P], oT_loc[:, i % 2, c // 2, c % 2, :],
                                                    wo_sb[:, c // 2, c % 2, :], start=(c == 0), stop=(c == 3), skip_group_check=True)
                        last.then_inc(q["lwo_mm"], 1)
                    yield w + 0.3
                    if 1 <= w <= NB:
                        j = m * NB + w - 1
                        pe.wait_ge(q["lp_s"], j + 1)
                        if j >= 1:
                            pe.wait_ge(q["lpT_s"], j)
                        for r in range(PAIRS):
                            last = nc.tensor.transpose(bank[:, 2, r * P:(r + 1) * P], p_loc[:, j % 2, r, :], eye_f[:, :])
                        last.then_inc(q["lpT_mm"], 1)
                    if 2 <= w <= NB + 1:
                        yield w + 0.6
                        j = m * NB + w - 2
                        pe.wait_ge(q["lpT_s"], j + 1)
                        if j >= 1:
                            pe.wait_ge(q["lo_s"], j)
                        for r in range(PAIRS):
                            for a in range(2):
                                last = nc.tensor.matmul(bank[WIN * a:WIN * a + WIN, 3, r * (LD + 1):(r + 1) * (LD + 1)],
                                                        pT_loc[:, j % 2, r, WIN * a:WIN * a + WIN],
                                                        v_loc[:, (w - 2) % 2, b * TB + (w - 2) // 2, 2 * r + a, :],
                                                        start=True, stop=True, skip_group_check=True)
                        last.then_inc(q["lpv_mm"], 1)
                    if 3 <= w <= NB + 2:
                        yield w + 0.8
                        j = m * NB + w - 3
                        pe.wait_ge(q["lo_s"], j + 1)
                        if j >= 1:
                            pe.wait_ge(q["loT_s"], j)
                        if w >= 6 or m:
                            pe.wait_ge(q["lx1_s"], m * TB + max(0, (w - 4) // 2))
                        for r in range(2):
                            last = nc.tensor.transpose(bank[:, 4, r * P:(r + 1) * P],
                                                       o_loc[:, j % 2, 2 * r:2 * r + 2, :].rearrange("p r d -> p (r d)"), eye_f[:, :])
                        last.then_inc(q["loT_mm"], 1)

            def feed(l, b):
                m = l * B + b
                yield 0
                before = min((m + 2) * TB, DEPTH * T)
                pe.wait_ge(q["lqkT_s"], before)
                pe.wait_ge(q["lv_s"], before)
                if m:
                    pe.wait_ge(q["lx2_s"], m)
                for t in range(TB):
                    n = b * TB + t
                    pe.wait_ge(q["lx1_s"], l * T + n + 1)
                    last = nc.tensor.matmul(bank[:, 5, t * 64:t * 64 + 64], shift_f[:, 0, :], xr[:, n, 64:128],
                                            start=True, stop=(t == 0), skip_group_check=True)
                    if t:
                        last = nc.tensor.matmul(bank[:, 5, t * 64:t * 64 + 64], shift_f[:, 1, :], xr[:, n - 1, 64:128],
                                                start=False, stop=True, skip_group_check=True)
                last.then_inc(q["lsh_mm"], 1)
                yield 3
                pe.wait_ge(q["lhn_s"], m + 1)
                for t in range(TB):
                    last = nc.tensor.transpose(bank[:, 6, t * P:(t + 1) * P], h_mod[:, b * TB + t, :], eye_f[:, :])
                last.then_inc(q["lhT_mm"], 1)
                for c, (c0, cn) in enumerate(HC):
                    i = m * NH + c
                    yield 4 + c
                    if c == 0:
                        pe.wait_ge(q["lhT_s"], m + 1)
                        if b == 0:
                            pe.wait_ge(q["lw_ff"], 16 * (1 + NH) * (l + 1))
                    if c >= 2:
                        pe.wait_ge(q["lff_s"], i - 1)
                    nc.tensor.matmul(bank[0:cn, 5 + 2 * c % 3, :], w1_sb[:, HID + c0:HID + c0 + cn], hT[:, b * S:(b + 1) * S],
                                     start=True, stop=True).then_inc(q["lg_mm"], 1)
                    yield 4 + c + 0.5
                    if c >= 1:
                        pe.wait_ge(q["lgate_s"], i)
                    nc.tensor.matmul(bank[0:cn, 5 + (2 * c + 1) % 3, :], w1_sb[:, c0:c0 + cn], hT[:, b * S:(b + 1) * S],
                                     start=True, stop=True).then_inc(q["la_mm"], 1)
                for t in range(TB):
                    yield 4 + NH + t / TB
                    if t == 0:
                        pe.wait_ge(q["lff_s"], (m + 1) * NH)
                    for c, (c0, cn) in enumerate(HC):
                        last = nc.tensor.matmul(bank[:, 5, t * P:(t + 1) * P], ff_T[0:cn, b, c, t * P:(t + 1) * P],
                                                w2_sb[0:cn, c, :], start=(c == 0), stop=(c == NH - 1), skip_group_check=True)
                last.then_inc(q["lf2_mm"], 1)

            schedule(pre, att, post, rope_part, windows, feed)

        @block.scalar
        def _(act):
            Hf = P // 2

            def logs(k):
                act.wait_ge(q["ln_num"], k + 1)
                nc.scalar.activation(sml[:, 2, :], sml[:, 0, :], ACT.Ln, bias=ones_col[:, 0:1], scale=1.0)
                nc.scalar.activation(sml[:, 3, :], sml[:, 0, :], ACT.Ln, bias=ones_col[:, 0:1], scale=-1.0).then_inc(q["ln_den"], 1)

            def tanh(k):
                act.wait_ge(q["tanh_in"], k + 1)
                nc.scalar.activation(sml[:, 9, 0:TB], sml[:, 8, 0:TB], ACT.Tanh).then_inc(q["tanh_s"], 1)

            def pre(b):
                if b == 0:
                    yield 0
                    logs(0)
                yield 4
                act.wait_ge(q["hT_mm"], b + 1)
                nc.scalar.activation(hT[:, b * S:(b + 1) * S], bk(6), ACT.Copy).then_inc(q["hT_s"], 1)
                for t in range(TB):
                    yield 5 + t
                    n = b * TB + t
                    act.wait_ge(q["u_s"], n + 1)
                    if n >= 2:
                        act.wait_ge(q["usq_s"], 2 * (n - 1))
                    nc.scalar.activation(sq[:, 512 * (n % 2):512 * (n % 2) + 3 * D],
                                         u_qkv[:, t, :, :].rearrange("p h d -> p (h d)"), ACT.Square).then_inc(q["usq_s"], 1)
                for t in range(TB):
                    yield 14 + 2 * t
                    n = b * TB + t
                    act.wait_ge(q["qkT_mm"], n + 1)
                    src = bank[:, 6 + t % 2, :].bitcast(F16).rearrange("p (i g t) -> p i g t", i=2, g=G)
                    nc.scalar.activation(q_T[:, :, n * P:(n + 1) * P], src[:, 0, :, :], ACT.Copy).then_inc(q["qkT_s"], 1)
                    nc.scalar.activation(k_T[:, :, n * P:(n + 1) * P], src[:, 1, :, :], ACT.Copy).then_inc(q["qkT_s"], 1)

            def att(b):
                for i in range(NS):
                    yield i
                    n = b * NS + i
                    act.wait_ge(q["scores_mm"], n + 1)
                    if n >= 3:
                        act.wait_ge(q["pv_mm"], n - 2)
                    nc.scalar.activation(probs[:, n % 3, :, :], bank[:, 2 * (n % 2):2 * (n % 2) + 2, :], ACT.Exp,
                                         scale=2.0 ** (-2 * EXP_SCALE_BITS) / math.sqrt(HD)).then_inc(q["probs_s"], 1)

            def post(b):
                yield 1
                act.wait_ge(q["wo_mm"], b + 1)
                nc.scalar.activation(a_sb[:, b, :, :].rearrange("p t d -> p (t d)"), bk(6), ACT.Copy).then_inc(q["a_s"], 1)
                yield 5
                tanh(2 * b)
                yield 12
                logs(b + 1)
                yield 17
                act.wait_ge(q["h2T_mm"], b + 1)
                nc.scalar.activation(hT[:, b * S:(b + 1) * S], bk(7), ACT.Copy).then_inc(q["h2T_s"], 1)
                for c in range(FC):
                    yield 18 + c
                    n = b * FC + c
                    act.wait_ge(q["z_mm"], n + 1)
                    nc.scalar.activation(z_T[:, c, :], bk(6 + c % 2), ACT.Identity, bias=b_f1_sb[:, c:c + 1]).then_inc(q["z_s"], 1)
                    nc.scalar.activation(z_sq[:, c, :], bk(6 + c % 2), ACT.Square, bias=b_f1_sb[:, c:c + 1]).then_inc(q["z_s"], 1)
                yield 24 + FC
                tanh(2 * b + 1)

            def rope_part(l, b):
                m = l * B + b
                yield 0
                if m == 0:
                    act.wait_ge(q["room_s_"], 5)
                act.wait_ge(q["lT_mm"], m + 1)
                nc.scalar.activation(hs_T[0:Hf, b, 0:S], bank[0:Hf, 7, :], ACT.Copy)
                nc.scalar.activation(hs_T[Hf:P, b, 1:S + 1], bank[Hf:P, 7, :], ACT.Copy).then_inc(q["lT_s"], 1)
                for t in range(TB + 3):
                    i = m * TB + t
                    n = b * TB + t
                    if t < TB:
                        for k in range(2):
                            yield 1 + t + k / 3
                            if i >= 2 and k == 0:
                                act.wait_ge(q["lx_s"], i - 1)
                                act.wait_ge(q["lred_s"], i - 1)
                            act.wait_ge(q["lqk_mm"], 2 * i + k + 1)
                            part = slice(k * INNER, (k + 1) * INNER)
                            nc.scalar.activation(qk_raw[:, i % 2, part], bk(5 + k), ACT.Copy).then_inc(q["lqk_s"], 1)
                            nc.scalar.activation(qk_sq[:, i % 2, part], bk(5 + k), ACT.Square).then_inc(q["lsq_s"], 1)
                        yield 1 + t + 2 / 3
                        act.wait_ge(q["lv_mm"], i + 1)
                        vs = bk(7).rearrange("p (h d) -> p h d", d=LD)
                        nc.scalar.activation(v_loc[:, 1, n, :, 0:LD], vs, ACT.Copy)
                        if t < TB - 1:
                            nc.scalar.activation(v_loc[WIN:P, 0, n + 1, :, 0:LD], vs[WIN:P], ACT.Copy)
                        nc.scalar.activation(v_loc[0:WIN, 0, n, :, 0:LD], vs[0:WIN], ACT.Copy).then_inc(q["lv_s"], 1)
                    if t >= 3:
                        yield 1 + t + 0.9
                        n, i, t3 = n - 3, i - 3, t - 3
                        act.wait_ge(q["lqkT_mm"], i + 1)
                        qs = bk(5).rearrange("p (r w c) -> p r w c", r=PAIRS, w=2)
                        nc.scalar.activation(q_blk[0:Hf, :, 2 * n:2 * n + 2, 0:WIN], qs[0:Hf], ACT.Copy)
                        nc.scalar.activation(q_blk[Hf:P, :, 2 * n:2 * n + 2, WIN:P], qs[Hf:P], ACT.Copy)
                        nc.scalar.activation(k_loc[:, :, b, WIN + t3 * P:WIN + (t3 + 1) * P],
                                             bk(6).rearrange("p (r c) -> p r c", r=PAIRS), ACT.Copy).then_inc(q["lqkT_s"], 1)

            def windows(l, b):
                m = l * B + b
                for w in range(NB + 3):
                    if w < NB:
                        yield w
                        j = m * NB + w
                        act.wait_ge(q["lrel_s"], j + 1)
                        if j >= 2:
                            act.wait_ge(q["lpT_mm"], j - 1)
                        to = p_loc[:, j % 2, :, :].rearrange("p r (k c) -> p r k c", k=2)
                        if w % 2 == 0:
                            to = to[:, :, ::-1, :]
                        nc.scalar.activation(to, s_rel[:, j % 2, :, :].rearrange("p r (k c) -> p r k c", k=2), ACT.Exp,
                                             scale=QK_SCALE).then_inc(q["lp_s"], 1)
                    if 1 <= w <= NB:
                        yield w + 0.3
                        j = m * NB + w - 1
                        act.wait_ge(q["lpT_mm"], j + 1)
                        if j >= 2:
                            act.wait_ge(q["lpv_mm"], j - 1)
                        nc.scalar.activation(pT_loc[:, j % 2, :, :].rearrange("p r c -> p (r c)"), bk(2), ACT.Copy).then_inc(q["lpT_s"], 1)
                    if 3 <= w:
                        yield w + 0.8
                        j = m * NB + w - 3
                        i = j // 2
                        act.wait_ge(q["loT_mm"], j + 1)
                        if i >= 2:
                            act.wait_ge(q["lwo_mm"], i - 1)
                        nc.scalar.activation(oT_loc[:, i % 2, :, :, (j % 2) * WIN:(j % 2 + 1) * WIN],
                                             bk(4, 2 * P).rearrange("p (r a c) -> p r a c", r=2, a=2), ACT.Copy).then_inc(q["loT_s"], 1)

            def feed(l, b):
                m = l * B + b
                yield 3
                act.wait_ge(q["lhT_mm"], m + 1)
                nc.scalar.activation(hT[:, b * S:(b + 1) * S], bk(6), ACT.Identity, scale=ln_gb[:, 0, l:l + 1],
                                     bias=ln_gb[:, 1, l:l + 1]).then_inc(q["lhT_s"], 1)
                for c, (c0, cn) in enumerate(HC):
                    yield 4 + c
                    i = m * NH + c
                    act.wait_ge(q["lg_mm"], i + 1)
                    if i >= 2:
                        act.wait_ge(q["lff_s"], i - 1)
                    nc.scalar.activation(gate_T[0:cn, i % 2, :], bank[0:cn, 5 + 2 * c % 3, :], ACT.Gelu,
                                         bias=b1_sb[0:cn, l, 1, c:c + 1]).then_inc(q["lgate_s"], 1)

            schedule(pre, att, post, rope_part, windows, feed)

        @block.vector
        def _(dve):
            chain = [0]
            v = nc.vector

            def link(ins):
                chain[0] += 1
                here = chain[0]
                ins.then_inc(q["dve_step"], 1)
                yield
                dve.wait_ge(q["dve_step"], here)

            def publish(ins, sem, value):
                ins.then_inc(sem, 1)
                yield
                dve.wait_ge(sem, value)

            def tt(o, a, b, op):
                yield from link(v.tensor_tensor(o, a, b, op))

            def ts(o, a, s1, op0, s2=None, op1=ALU.bypass):
                yield from link(v.tensor_scalar(o, a, s1, s2, op0, op1))

            def stt(o, a, sc, b, op0, op1):
                yield from link(v.scalar_tensor_tensor(o, a, sc, b, op0, op1))

            def rsqrt(o, a, n):
                i, f = nt_i[:, 0:n], nt_f[:, 0:n]
                yield from ts(i, a.bitcast(I32), 1, ALU.logical_shift_right)
                yield from ts(o.bitcast(I32), i, -1.0, ALU.mult, float(RSQRT_MAGIC), ALU.add)
                for _ in range(3):
                    yield from tt(f, o, o, ALU.mult)
                    yield from stt(f, f, -0.5, a, ALU.mult, ALU.mult)
                    yield from stt(o, f, 1.5, o, ALU.add, ALU.mult)

            dve.wait_ge(q["consts"], 80)
            v.tensor_copy(eye_h[:, :], eye_f[:, :])
            v.tensor_copy(eye_b[:, :], eye_f[:, :])
            v.tensor_copy(mask_b[:, :, :], mask_f[:, :, :])
            v.memset(ones_col[:, :], 1.0).then_inc(q["eyes"], 1)
            dve.wait_ge(q["eyes"], 1)
            for b in range(B):
                v.tensor_copy(cond_rep[:, b, :], cond_T[:, b:b + 1].to_broadcast([P, P])).then_inc(q["cond_rep_s"], 1)

            def moments(src, t0, n):
                for t in range(t0, t0 + n):
                    last = v.bn_stats(bn6[:, t, 0:6], src[:, t, :])
                yield from link(last)
                for t in range(t0, t0 + n):
                    last = v.bn_aggr(mean_var[:, t, :], bn6[:, t, 0:6])
                yield from link(last)

            logs_asked = [0]

            def inverse_std(t0, n, half=0, end=0):
                mean, var = mean_var[:, t0:t0 + n, 0], mean_var[:, t0:t0 + n, 1]
                r = lambda k: sml[:, k, 0:n]
                yield from tt(r(1), mean, mean, ALU.mult)
                yield from tt(r(1), r(1), var, ALU.add)
                yield from ts(r(1), r(1), float(D), ALU.mult, EPS * EPS, ALU.max)
                yield from rsqrt(r(4), r(1), n)
                yield from tt(r(5), r(1), r(4), ALU.mult)
                logs_asked[0] += 1
                yield half, end, 56
                v.tensor_scalar(sml[:, 0, 0:n], r(5), MAX_TANH, None, ALU.min).then_inc(q["ln_num"], 1)
                dve.wait_ge(q["ln_num"], logs_asked[0])
                yield from ts(r(5), r(1), 0.0625, ALU.min)
                yield from ts(r(6), r(5), 1.0 / 9, ALU.mult, 1.0 / 7, ALU.add)
                for c in (1.0 / 5, 1.0 / 3, 1.0):
                    yield from tt(r(6), r(6), r(5), ALU.mult)
                    yield from ts(r(6), r(6), c, ALU.add)
                yield from ts(r(7), r(1), 0.0625, ALU.is_lt)
                dve.wait_ge(q["ln_den"], logs_asked[0])
                yield from tt(r(5), sml[:, 2, 0:n], sml[:, 3, 0:n], ALU.subtract)
                yield from stt(r(5), r(5), 0.5, r(4), ALU.mult, ALU.mult)
                yield from tt(r(6), r(6), r(5), ALU.subtract)
                yield from tt(r(6), r(6), r(7), ALU.mult)
                yield from tt(r(5), r(5), r(6), ALU.add)
                yield from tt(r(5), r(5), r(5), ALU.mult)
                yield from link(v.reciprocal(r(6), r(5)))
                yield from stt(r(6), r(6), 1e-6, var, ALU.mult, ALU.add)
                yield from rsqrt(r(5), r(6), n)

            def modulate(src, b, k_scale_row, k_shift_row, r0, done=None):
                for t in range(TB):
                    last = v.tensor_scalar(h_mod[:, b * TB + t, :], src[:, b * TB + t, :], mean_var[:, b * TB + t, 0:1],
                                           sml[:, 5, r0 + t:r0 + t + 1], ALU.subtract, ALU.mult)
                yield from link(last)
                hb = h_mod[:, b * TB:(b + 1) * TB, :]
                wide = lambda k: ada[:, b, k, :].unsqueeze(1).to_broadcast([P, TB, D])
                yield from tt(hb, hb, wide(k_scale_row), ALU.mult)
                yield from link(v.tensor_tensor(hb, hb, wide(k_shift_row), ALU.add))
                for t in range(TB):
                    last = v.tensor_tensor_reduce(out=junk[:, t, :], in0=h_mod[:, b * TB + t, :], in1=h_mod[:, b * TB + t, :],
                                                  scale=1.0, scalar=0.0, op0=ALU.mult, op1=ALU.add,
                                                  accum_out=sml[:, 6, t:t + 1])
                yield from link(last)
                yield from ts(sml[:, 6, 0:TB], sml[:, 6, 0:TB], EPS * EPS, ALU.max)
                yield from rsqrt(sml[:, 7, 0:TB], sml[:, 6, 0:TB], TB)
                last = v.tensor_scalar(sml[:, 7, 0:TB], sml[:, 7, 0:TB], MAX_ARTANH, 1.0, ALU.mult, ALU.min)
                if done is None:
                    yield from link(last)
                else:
                    yield from publish(last, done, b + 1)

            def pre(b):
                if b == 0:
                    yield 0
                    dve.wait_ge(q["x_in_s"], 16)
                    yield from moments(x_in, 0, T)
                    yield from inverse_std(0, T)
                    dve.wait_ge(q["w_a_in"], 16 * 8)
                    for c in range(B):
                        dve.wait_ge(q["ada_mm"], c + 1)
                        for half in range(2):
                            last = v.tensor_tensor(ada[:, c, 3 * half:3 * half + 3, :].rearrange("p k d -> p (k d)"),
                                                   bk(2 * c + half, 3 * D), b_ada_sb[:, half * 3 * D:(half + 1) * 3 * D], ALU.add)
                        yield from link(last)
                        for k in (1, 4):
                            last = v.tensor_scalar(ada[:, c, k, :], ada[:, c, k, :], 1.0, None, ALU.add)
                        last.then_inc(q["ada_s"], 1)
                    dve.wait_ge(q["ada_s"], B)
                yield 0, 4, 20
                yield from modulate(x_in, b, 1, 0, b * TB, q["hmod_s"])
                for t in range(TB):
                    yield 5 + t
                    n = b * TB + t
                    dve.wait_ge(q["qkv_mm"], n + 1)
                    v.scalar_tensor_tensor(u_qkv[:, t, :, :].rearrange("p h d -> p (h d)"), bk(7 - t % 2, 3 * D),
                                           sml[:, 7, t:t + 1], b_qkv_sb[:, :], ALU.mult, ALU.add).then_inc(q["u_s"], 1)
                    yield
                    dve.wait_ge(q["usq_s"], 2 * n + 1)
                    v.tensor_reduce(head_sq[:, t, :],
                                    sq[:, 512 * (n % 2):512 * (n % 2) + 3 * D].rearrange("p (h d) -> p h d", d=HD),
                                    AXX, ALU.add).then_inc(q["usq_s"], 1)
                yield 5 + TB, 14, 32
                dve.wait_ge(q["usq_s"], 2 * TB * (b + 1))
                flat = lambda a: a[:, :, :].rearrange("p t h -> p (t h)")
                yield from link(v.tensor_reduce(all_sq[:, :, :].rearrange("p t i -> p (t i)"),
                                     head_sq[:, :, :].rearrange("p t (i h) -> p (t i) h", h=H), AXX, ALU.add))
                yield from ts(flat(head_sq), flat(head_sq), EPS * EPS, ALU.max)
                yield from ts(flat(all_sq), flat(all_sq), EPS * EPS, ALU.max)
                yield from rsqrt(flat(head_f), flat(head_sq), TB * 3 * H)
                yield from rsqrt(flat(all_f), flat(all_sq), TB * 3)
                yield from ts(flat(all_f), flat(all_f), RATIO * MAX_ARTANH, ALU.mult, RATIO, ALU.min)
                yield from ts(flat(head_f), flat(head_f), MAX_ARTANH, ALU.mult)
                hf = head_f[:, :, :].rearrange("p t (i h) -> p (t i) h", h=H)
                yield from tt(hf, hf, all_f[:, :, :].rearrange("p t i -> p (t i)").unsqueeze(2).to_broadcast([P, TB * 3, H]), ALU.min)
                yield from ts(head_f[:, :, 0:2 * H], head_f[:, :, 0:2 * H], 2.0 ** EXP_SCALE_BITS, ALU.mult)
                yield from ts(head_f[:, :, 2 * H:3 * H], head_f[:, :, 2 * H:3 * H], 1.0 / RATIO, ALU.mult)
                if b == 0:
                    dve.wait_ge(q["zero_s"], 3)
                for t in range(TB):
                    yield 13 + 2 * t, 14 + 2 * t, 3
                    n = b * TB + t
                    v.tensor_tensor(v_aug[:, n, :, 0:HD], u_qkv[:, t, 2 * H:3 * H, :],
                                    head_f[:, t, 2 * H:3 * H].unsqueeze(2).to_broadcast([P, H, HD]), ALU.mult)
                    if n >= 2:
                        dve.wait_ge(q["qkT_mm"], n - 1)
                    qf, kf = qk_f[:, n % 2, 0:H, :], qk_f[:, n % 2, H:2 * H, :]
                    qs, ks = q_split[:, n % 2, :, :, :], k_split[:, n % 2, :, :, :]
                    yield from tt(qk_f[:, n % 2, :, :], u_qkv[:, t, 0:2 * H, :],
                       head_f[:, t, 0:2 * H].unsqueeze(2).to_broadcast([P, 2 * H, HD]), ALU.mult)
                    twice = lambda a: a.unsqueeze(2).to_broadcast([P, H, 2, HD])
                    v.tensor_copy(qs[:, :, 0:2, :], twice(qf))
                    yield from link(v.tensor_copy(ks[:, :, 0:3:2, :], twice(kf)))
                    v.tensor_tensor(qs[:, :, 2:4, :], twice(qf), qs[:, :, 0:2, :], ALU.subtract)
                    v.tensor_tensor(ks[:, :, 1:4:2, :], twice(kf), ks[:, :, 0:3:2, :], ALU.subtract).then_inc(q["split_s"], 1)

            def att(b):
                per = TB * 2
                for g in range(G):
                    bg = b * G + g
                    yield per * (g + 1) + 1
                    dve.wait_ge(q["pv_mm"], (bg + 1) * per)
                    v.tensor_copy(o_raw[:, :], bk(4 + bg % 2)).then_inc(q["oraw_s"], 1)
                    yield per * (g + 1) + 4
                    dve.wait_ge(q["den_mm"], bg + 1)
                    yield from link(v.reciprocal(den_r[:, :], bk(4 + bg % 2)))
                    if b >= 1 and g == 0:
                        dve.wait_ge(q["wo_mm"], b)
                    yield from publish(v.tensor_tensor(o_T[:, g, :], o_raw[:, :], den_r[:, :], ALU.mult), q["oT_s"], bg + 1)

            tanh_asked = [0]

            def mobius_step(b, k_gate, x_old, x_new, half, end, done=None):
                r = lambda k: sml[:, k, 0:TB]
                gate = ada[:, b, k_gate, :].unsqueeze(1).to_broadcast([P, TB, D])
                yield from tt(w_sb[:, :, :], a_sb[:, b, :, :], gate, ALU.mult)
                for t in range(TB):
                    xt = x_old[:, b * TB + t, :]
                    for i, (k, l, m) in enumerate(((10, a_sb[:, b, t, :], a_sb[:, b, t, :]), (11, w_sb[:, t, :], w_sb[:, t, :]),
                                    (12, xt, w_sb[:, t, :]), (13, xt, xt))):
                        last = v.tensor_tensor_reduce(out=junk[:, 4 * t + i, :], in0=l, in1=m, scale=1.0, scalar=0.0,
                                                      op0=ALU.mult, op1=ALU.add, accum_out=sml[:, k, t:t + 1])
                yield from link(last)
                yield from ts(r(14), r(10), EPS * EPS, ALU.max)
                yield from rsqrt(r(15), r(14), TB)
                yield from ts(r(15), r(15), MAX_ARTANH, ALU.mult, 1.0, ALU.min)
                yield from ts(r(14), r(11), EPS * EPS, ALU.max)
                yield from rsqrt(r(16), r(14), TB)
                yield from tt(r(16), r(16), r(14), ALU.mult)
                yield from tt(r(16), r(16), r(15), ALU.mult)
                tanh_asked[0] += 1
                yield half
                v.tensor_scalar(r(8), r(16), EPS, None, ALU.max).then_inc(q["tanh_in"], 1)
                yield half, end, 18
                dve.wait_ge(q["tanh_in"], tanh_asked[0])
                yield from link(v.reciprocal(r(16), r(8)))
                yield from tt(r(15), r(15), r(16), ALU.mult)
                dve.wait_ge(q["tanh_s"], tanh_asked[0])
                yield from tt(r(15), r(15), r(9), ALU.mult)
                yield from tt(r(12), r(12), r(15), ALU.mult)
                yield from tt(r(11), r(11), r(15), ALU.mult)
                yield from tt(r(11), r(11), r(15), ALU.mult)
                yield from ts(r(12), r(12), 2.0, ALU.mult, 1.0, ALU.add)
                yield from tt(r(17), r(13), r(11), ALU.mult)
                yield from tt(r(17), r(17), r(12), ALU.add)
                yield from ts(r(17), r(17), EPS, ALU.max)
                yield from link(v.reciprocal(r(18), r(17)))
                yield from tt(r(12), r(12), r(11), ALU.add)
                yield from tt(r(12), r(12), r(18), ALU.mult)
                yield from ts(r(13), r(13), -1.0, ALU.mult, 1.0, ALU.add)
                yield from tt(r(13), r(13), r(15), ALU.mult)
                yield from tt(r(13), r(13), r(18), ALU.mult)
                for t in range(TB):
                    last = v.tensor_scalar(w_sb[:, t, :], w_sb[:, t, :], sml[:, 13, t:t + 1], None, ALU.mult)
                yield from link(last)
                for t in range(TB):
                    last = v.scalar_tensor_tensor(x_new[:, b * TB + t, :], x_old[:, b * TB + t, :], sml[:, 12, t:t + 1],
                                                  w_sb[:, t, :], ALU.mult, ALU.add)
                if done is None:
                    yield from link(last)
                else:
                    yield from publish(last, done, b + 1)

            def post(b):
                yield 1, 5, 32
                dve.wait_ge(q["rope_s"], 4 * DEPTH)
                dve.wait_ge(q["a_s"], b + 1)
                yield from mobius_step(b, 2, x_in, x_mid, 5, 9)
                yield 9, 12, 18
                yield from moments(x_mid, b * TB, TB)
                yield from inverse_std(b * TB, TB, 12, 17)
                yield from modulate(x_mid, b, 4, 3, 0)
                for t in range(TB):
                    last = v.tensor_scalar(h_mod[:, b * TB + t, :], h_mod[:, b * TB + t, :], sml[:, 7, t:t + 1], None, ALU.mult)
                last.then_inc(q["h2_s"], 1)

                yield 18 + FC, 20 + FC, 13
                dve.wait_ge(q["ffw_in"], 16 * 9)
                dve.wait_ge(q["zsq_mm"], b + 1)
                yield from ts(sml[:, 6, 0:TB], bank[:, 6, 0:TB], EPS * EPS, ALU.max)
                yield from rsqrt(sml[:, 7, 0:TB], sml[:, 6, 0:TB], TB)
                yield from ts(sml[:, 7, 0:TB], sml[:, 7, 0:TB], MAX_ARTANH, ALU.mult, 1.0, ALU.min)
                yield 20 + FC, 24 + FC, 32
                dve.wait_ge(q["z2_mm"], b + 1)
                for t in range(TB):
                    last = v.scalar_tensor_tensor(a_sb[:, b, t, :], bank[:, 7, t * P:(t + 1) * P], sml[:, 7, t:t + 1],
                                                  b_f2_sb[:, :], ALU.mult, ALU.add)
                yield from publish(last, q["z2_used"], b + 1)
                yield from mobius_step(b, 5, x_mid, xr, 24 + FC, 28 + FC, q["x2_s"])

            def rope_part(l, b):
                m = l * B + b
                for u in range(TB // 2):
                    for t in (2 * u, 2 * u + 1):
                        yield 1 + t + 1 / 3, 2 + t, 4
                        n = b * TB + t
                        i = m * TB + t
                        if m == 0 and t == 0:
                            dve.wait_ge(q["x2_s"], B)
                        dve.wait_ge(q["lsq_s"], 2 * (i + 1))
                        v.tensor_reduce(norm_sq[:, n, :], qk_sq[:, i % 2, :].rearrange("p (h d) -> p h d", d=LD),
                                        AXX, ALU.add).then_inc(q["lred_s"], 1)
                        yield
                        if i >= 4:
                            dve.wait_ge(q["lqkT_mm"], i - 3)
                        for k in range(2):
                            last = v.tensor_tensor(qk_rot[:, i % 4, k * INNER:(k + 1) * INNER].rearrange("p (h d) -> p h d", d=LD),
                                                   qk_raw[:, i % 2, k * INNER:(k + 1) * INNER].rearrange("p (h d) -> p h d", d=LD),
                                                   rope_l[:, l, k, t, :].unsqueeze(1).to_broadcast([P, LH, LD]), ALU.mult)
                        yield from link(last)
                        dve.wait_ge(q["lc_s"], i + 1)
                        yield from publish(v.tensor_tensor(qk_rot[:, i % 4, :], qk_rot[:, i % 4, :], qk_cross[:, i % 2, :], ALU.add), q["lx_s"], i + 1)
                    yield 3 + 2 * u, 3 + 2 * u + 0.9, 13
                    dve.wait_ge(q["lred_s"], m * TB + 2 * u + 2)
                    pair = lambda a: a[:, b * TB + 2 * u:b * TB + 2 * u + 2, :].rearrange("p t h -> p (t h)")
                    yield from ts(pair(norm_sq), pair(norm_sq), 1e-24, ALU.max)
                    yield from rsqrt(pair(norm_r), pair(norm_sq), 4 * LH)
                    for t in (2 * u, 2 * u + 1):
                        i = m * TB + t
                        to = qk_rot[:, i % 4, :].rearrange("p (h d) -> p h d", d=LD)
                        yield from publish(v.tensor_tensor(to, to, norm_r[:, b * TB + t, :].unsqueeze(2).to_broadcast([P, 2 * LH, LD]), ALU.mult),
                                           q["lrot_s"], i + 1)

            def windows(l, b):
                m = l * B + b
                for w in range(NB + 5):
                    if w < NB:
                        yield w
                        j = m * NB + w
                        dve.wait_ge(q["ls_mm"], j + 1)
                        S4 = bk(j % 2).rearrange("p (r c) -> p r c", r=PAIRS)
                        yield from link(v.tensor_reduce(row_max[:, j % 2, :], S4, AXX, ALU.max))
                        if j >= 2:
                            dve.wait_ge(q["lp_s"], j - 1)
                        v.tensor_tensor(s_rel[:, j % 2, :, :], S4, row_max[:, j % 2, :].unsqueeze(2).to_broadcast([P, PAIRS, P]),
                                        ALU.subtract).then_inc(q["lrel_s"], 1)
                    if w >= 6 and w % 2 == 0:
                        yield w
                        i = m * TB + (w - 6) // 2
                        n = b * TB + (w - 6) // 2
                        dve.wait_ge(q["lwo_mm"], i + 1)
                        v.tensor_tensor(xr[:, n, :], xr[:, n, :], bank[:, 4, 2 * P:3 * P], ALU.add).then_inc(q["lx1_s"], 1)
                    if 3 <= w <= NB + 2:
                        yield w + 0.3
                        j = m * NB + w - 3
                        dve.wait_ge(q["lpv_mm"], j + 1)
                        O4 = bk(3, PAIRS * (LD + 1)).rearrange("p (r d) -> p r d", r=PAIRS)
                        if j >= 2:
                            dve.wait_ge(q["loT_mm"], j - 1)
                        yield from link(v.reciprocal(o_den[:, j % 2, :], O4[:, :, LD]))
                        v.tensor_tensor(o_loc[:, j % 2, :, :], O4[:, :, 0:LD], o_den[:, j % 2, :].unsqueeze(2).to_broadcast([P, PAIRS, LD]),
                                        ALU.mult).then_inc(q["lo_s"], 1)

            def feed(l, b):
                m = l * B + b
                ns = range(b * TB, (b + 1) * TB)
                yield 0, 3, 16
                dve.wait_ge(q["lx1_s"], (m + 1) * TB)
                dve.wait_ge(q["lsh_mm"], m + 1)
                up = lambda n: bank[:, 5, n % TB * 64:n % TB * 64 + 64]
                for n in ns:
                    v.bn_stats(bn6[:, n, 0:6], xr[:, n, 0:64])
                    last = v.bn_stats(bn6[:, n, 6:12], up(n))
                yield from link(last)
                for n in ns:
                    last = v.bn_aggr(mean_var[:, n, :], bn6[:, n, :])
                yield from link(last)
                yield from ts(sml[:, 1, 0:TB], mean_var[:, b * TB:(b + 1) * TB, 1], 1e-5, ALU.add)
                yield from rsqrt(sml[:, 5, 0:TB], sml[:, 1, 0:TB], TB)
                for n in ns:
                    r = sml[:, 5, n % TB:n % TB + 1]
                    v.tensor_scalar(h_mod[:, n, 0:64], xr[:, n, 0:64], mean_var[:, n, 0:1], r, ALU.subtract, ALU.mult)
                    last = v.tensor_scalar(h_mod[:, n, 64:128], up(n), mean_var[:, n, 0:1], r, ALU.subtract, ALU.mult)
                yield from publish(last, q["lhn_s"], m + 1)
                for c, (c0, cn) in enumerate(HC):
                    yield 4.5 + c
                    i = m * NH + c
                    if c == 0:
                        dve.wait_ge(q["lqkT_mm"], min((m + 2) * TB, DEPTH * T))
                    dve.wait_ge(q["lgate_s"], i + 1)
                    dve.wait_ge(q["la_mm"], i + 1)
                    v.scalar_tensor_tensor(ff_T[0:cn, b, c, :], bank[0:cn, 5 + (2 * c + 1) % 3, :], b1_sb[0:cn, l, 0, c:c + 1],
                                           gate_T[0:cn, i % 2, :], ALU.add, ALU.mult).then_inc(q["lff_s"], 1)
                yield 4 + NH
                xb = xr[:, b * TB:(b + 1) * TB, :]
                yield from tt(xb, xb, b2_sb[:, l, :].unsqueeze(1).to_broadcast([P, TB, D]), ALU.add)
                yield 5 + NH
                dve.wait_ge(q["lf2_mm"], m + 1)
                yield from publish(v.tensor_tensor(xb, xb, bk(5).rearrange("p (t d) -> p t d", d=D), ALU.add), q["lx2_s"], m + 1)
                if m == DEPTH * B - 1:
                    v.tensor_tensor(xr[:, :, :], xr[:, :, :], x_in[:, :, :], ALU.add).then_inc(q["lx2_s"], 1)

            schedule(pre, att, post, rope_part, windows, feed)


_INS = ['x', 'cond_1024', 'L0_cond_w_q', 'L0_cond_b_q', 'L0_cond_w_k', 'L0_cond_b_k', 'L0_cond_w_v', 'L0_cond_b_v',
        'L0_cond_w_o', 'L0_cond_b_o', 'L0_cond_w_f1', 'L0_cond_b_f1', 'L0_cond_w_f2', 'L0_cond_b_f2', 'L0_cond_w_ada',
        'L0_cond_b_ada', 'L0_ffn_wqkv', 'L0_ffn_q_scale', 'L0_ffn_k_scale', 'L0_ffn_wo', 'L0_ffn_ln_g', 'L0_ffn_ln_b',
        'L0_ffn_w1', 'L0_ffn_b1', 'L0_ffn_w2', 'L0_ffn_b2']


def _constants(S, depth_head, window):
    import numpy as np
    f = np.float32
    half = np.arange(0, depth_head, 2, dtype=f)
    inv = (f(1.0) / f(10000.0) ** (half / f(depth_head))).astype(f)
    t = np.arange(S, dtype=f)
    fr = (t[:, None] * inv[None, :]).astype(f)
    fr = np.concatenate([fr, fr], -1)
    base = (half + f(0.4 * depth_head)) / f(1.4 * depth_head)
    power = (t - S // 2) / f(window // 2)
    sc = (base[None, :] ** power[:, None]).astype(f)
    sc = np.concatenate([sc, sc], -1)
    cos, sin = np.cos(fr).astype(f), np.sin(fr).astype(f)
    sign = np.concatenate([-np.ones(depth_head // 2, f), np.ones(depth_head // 2, f)])
    rope = np.stack([cos * sc, cos / sc, sign * sin * sc, sign * sin / sc]).astype(f)
    i = np.arange(128)[:, None] % window
    j = np.arange(2 * window)[None, :]
    band = np.where((j >= i) & (j <= i + window), f(0), f(-1e30)).astype(f)
    first = np.where(j >= window, band, f(-1e30)).astype(f)
    masks = np.stack([band, first])
    eye = np.eye(128, dtype=f)
    shift = np.zeros((2, 128, 128), f)
    shift[0, np.arange(127), np.arange(1, 128)] = 1
    shift[1, 127, 0] = 1
    pick = np.zeros((128, 128), f)
    for r in range(128):
        pick[32 * (r // 32) + 8, r] = 1
    return {'rope': rope, 'masks': masks, 'eye': eye, 'shift': shift, 'denom_pick': pick}


def kernel(**inputs):
    import numpy as _np
    import concourse.bacc as _bacc
    from concourse import mybir as _mybir
    from concourse.bass_utils import run_bass_kernel_spmd as _run

    nc = _bacc.Bacc("TRN2", target_bir_lowering=False, num_devices=1)
    arrays, args = {}, []
    values = {n: inputs[n] for n in _INS}
    shape = values['x'].shape
    values['cond_1024'] = _np.asarray(values['cond_1024']).T
    values['L0_cond_b_f1'] = _np.asarray(values['L0_cond_b_f1']).reshape(-1, 128).T
    values['L0_ffn_ln_g'] = _np.asarray(values['L0_ffn_ln_g']).T
    values['L0_ffn_ln_b'] = _np.asarray(values['L0_ffn_ln_b']).T
    b1 = _np.asarray(values['L0_ffn_b1'])
    depth, hid = b1.shape[0], b1.shape[1] // 2
    b1 = _np.pad(b1.reshape(depth, 2, hid), ((0, 0), (0, 0), (0, -hid % 128)))
    values['L0_ffn_b1'] = b1.reshape(depth * 2 * (b1.shape[2] // 128), 128).T
    values.update(_constants(shape[1], values['L0_ffn_q_scale'].shape[1], 64))
    for name, a in values.items():
        a = _np.ascontiguousarray(a)
        arrays[f"in_{name}"] = a
        args.append(nc.dram_tensor(f"in_{name}", a.shape, _mybir.dt.from_np(a.dtype), kind="ExternalInput").ap())
    args.append(nc.dram_tensor("out_0", shape, _mybir.dt.float32, kind="ExternalOutput").ap())
    adaln_ffn_kernel(nc, *args)
    r = _run(nc, [arrays], core_ids=[0])
    return r.results[0]["out_0"]
```

```python
import math
from contextlib import ExitStack

import concourse.bass as bass
from concourse import mybir

F32 = mybir.dt.float32
F16 = mybir.dt.float16
BF16 = mybir.dt.bfloat16
I32 = mybir.dt.int32
ALU = mybir.AluOpType
ACT = mybir.ActivationFunctionType
AXX = mybir.AxisListType.X

P = 128
EPS = 1e-7
MAX_TANH = 0.99998998641967773438
MAX_ARTANH = 0.5 * math.log((1 + MAX_TANH) / (1 - MAX_TANH))
EXP_SCALE_BITS = 12
RSQRT_MAGIC = 0x5F1FFFF9
RSQRT_C = (3 / 8) ** 0.2
RSQRT_MUL = -0.703952253 * RSQRT_C
RSQRT_ADD = 1.68191391 * RSQRT_C
SMALL_NORM = 1 / 32
SMALL_RATIO = math.atanh(SMALL_NORM) / SMALL_NORM


def adaln_ffn_kernel(
    nc, x, cond_1024,
    w_q, b_q, w_k, b_k, w_v, b_v, w_o, b_o, w_f1, b_f1, w_f2, b_f2, w_ada, b_ada,
    wqkv, q_scale, k_scale, wo, ln_g, ln_b, w1, b1, w2, b2,
    rope, masks, eye, shift, denom_pick, out,
):
    B, S, D = x.shape
    TB = S // P
    T = B * TB
    H, HD = 16, D // 16
    G = H // 4
    FF = w_f1.shape[1]
    FC = FF // P
    beta = lambda a, b: math.exp(math.lgamma(a) + math.lgamma(b) - math.lgamma(a + b))
    RATIO = beta(HD / 2, 0.5) / beta(D / 2, 0.5)
    DEPTH, _, QKV = wqkv.shape
    INNER = QKV // 3
    LD = q_scale.shape[1]
    LH = INNER // LD
    PAIRS = LH // 2
    WIN = P // 2
    NW = T * 2
    HID = w2.shape[1]
    HC = [(c, min(P, HID - c)) for c in range(0, HID, P)]
    NH = len(HC)
    QK_SCALE = 8.0

    with ExitStack() as ctx:
        def sb(name, shape, dt=F32):
            return ctx.enter_context(nc.sbuf_tensor(name, shape, dt))

        def sem(name):
            return ctx.enter_context(nc.semaphore(name))

        bank = ctx.enter_context(nc.psum_tensor("bank", [P, 8, 512], F32))

        def bk(i, n=512):
            return bank[:, i, 0:n]

        eye_f = sb("eye_f", [P, P])
        eye_h = sb("eye_h", [P, P], F16)
        eye_b = sb("eye_b", [P, P], BF16)
        shift_f = sb("shift_f", [P, 2, P])
        pick_f = sb("pick_f", [P, P])
        ones_col = sb("ones_col", [P, 1])
        mask_f = sb("mask_f", [P, 2, P])
        mask_b = sb("mask_b", [P, 2, P], BF16)
        cond_T = sb("cond_T", [P, B])
        b_f1_sb = sb("b_f1_sb", [P, FC])
        x_in = sb("x_in", [P, T, D])
        xr = sb("xr", [P, T, D])

        bn6 = sb("bn6", [P, T, 12])
        mean_var = sb("mean_var", [P, T, 2])
        sml = sb("sml", [P, 32, 8])
        root_l = sb("root_l", [P, 4 * LH])
        root_f = sb("root_f", [P, B, TB * 3 * (H + 1)])
        h_mod = sb("h_mod", [P, T, D])
        hT = sb("hT", [P, T * P])
        room_q = sb("room_q", [P, PAIRS * NW * P])
        room_k = sb("room_k", [P, PAIRS * B * (S + WIN)])
        room_v = sb("room_v", [P, 2 * T * LH * (LD + 1)])
        room_r = sb("room_r", [P, 12 * 512])
        room_s = sb("room_s", [P, 8 * 512])

        def carve(room):
            at = [0]

            def take(pattern, n, **sizes):
                a = room[:, at[0]:at[0] + n].rearrange(f"p ({pattern}) -> p {pattern}", **sizes)
                at[0] += n
                return a
            return take

        room_w = sb("room_w", [P, 4224])
        room_a = sb("room_a", [P, B * 6 * D + 512])
        room_m = sb("room_m", [P, 1026])
        take = carve(room_w)
        cond_rep = take("b n", B * P, b=B)
        w_ada_sb = take("n", 6 * D)
        b_ada_sb = take("n", 6 * D)
        w_qkv_sb = take("n", 3 * D)
        b_qkv_sb = take("n", 3 * D)
        w_o_sb = take("g n", G * D, g=G)
        w_f1_sb = take("n", FF)
        w_f2_sb = take("c n", FC * D, c=FC)
        b_f2_sb = take("n", D)
        ada = room_a[:, 0:B * 6 * D].rearrange("p (b k d) -> p b k d", b=B, k=6)
        x_mid = room_m[:, 2:2 + T * D].rearrange("p (t d) -> p t d", t=T)
        take = carve(room_r)
        probs = take("r i n", 6 * 512, r=3, i=2)
        o_raw = take("n", 512)
        den_r = take("n", 512)
        o_T = take("g n", G * S, g=G)
        head_f = sb("head_f", [P, B, TB, 3 * H])
        all_f = sb("all_f", [P, B, TB, 3])
        room_qk = sb("room_qk", [P, 2, 6 * D])
        half_k = G * T * P // 2
        q_T = room_k[:, 0:half_k].bitcast(F16).rearrange("p (g n) -> p g n", g=G)
        k_T = room_k[:, half_k:2 * half_k].bitcast(F16).rearrange("p (g n) -> p g n", g=G)
        k_pad = room_q[:, :].bitcast(F16).rearrange("p (b g j n) -> p b g j n", b=B, g=G, j=4)
        take = carve(room_v)
        v_aug = take("t h d", T * H * 32, t=T, d=32)
        take("n", room_v.shape[1] // 2 - T * H * 32)
        a_sb = take("b t d", T * D, b=B, d=D)
        w_sb = [take("t d", TB * D, d=D), room_a[:, B * 6 * D:B * 6 * D + TB * D].rearrange("p (t d) -> p t d", d=D)]
        junk = take("b n", B * 16 * D // 2, b=B).bitcast(BF16).rearrange("p b (i d) -> p b i d", d=D)
        head_sq = take("b t h", B * TB * 3 * H, b=B, t=TB)
        all_sq = take("b t h", B * TB * 3, b=B, t=TB)
        qk_f, q_split, k_split = {}, {}, {}
        for b, k, f_room, split_room in (
                (0, 0, room_qk[:, 0, 0:2 * D], room_qk[:, 0, 2 * D:]), (1, 0, room_qk[:, 1, 0:2 * D], room_qk[:, 1, 2 * D:]),
                (0, 1, room_r[:, 0:2 * D], room_r[:, 2 * D:6 * D]), (1, 1, room_m[:, 4 * D:6 * D], room_a[:, B * 6 * D:])):
            qk_f[b, k] = f_room.rearrange("p (h d) -> p h d", d=HD)
            for n, to in ((0, q_split), (2, k_split)):
                to[b, k] = split_room[:, n * D:(n + 2) * D].bitcast(F16).rearrange("p (h i d) -> p h i d", h=H, i=4)
        sq_at = room_v.shape[1] // 2
        sq = room_v[:, sq_at:sq_at + B * 2 * 3 * D].rearrange("p (b k n) -> p b k n", b=B, k=2)
        chunks = lambda a: a.rearrange("p (c n) -> p c n", c=FC)
        z_rooms = (room_s[:, :], room_q[:, room_q.shape[1] // 2:])
        z_T = [chunks(r[:, 0:FC * S]) for r in z_rooms]
        z_sq = [chunks(r[:, FC * S:2 * FC * S]) for r in z_rooms]
        u_qkv = room_s[:, 0:T * 3 * D].rearrange("p (b t h d) -> p b t h d", b=B, t=TB, d=HD)

        q_blk = room_q[:, :].rearrange("p (b r w c) -> p b r w c", b=B, r=PAIRS, c=P)
        k_loc = room_k[:, :].rearrange("p (b r n) -> p b r n", b=B, r=PAIRS)
        v_loc = room_v[:, :].rearrange("p (b k t h d) -> p b k t h d", b=B, k=2, t=TB, d=LD + 1)
        take = carve(room_r)
        qk_rot = take("r n", 4 * 2 * INNER, r=4)
        qk_cross = take("r n", 2 * 2 * INNER, r=2)
        take = carve(room_s)
        qk_raw = take("r n", 2 * 2 * INNER, r=2)
        qk_sq = take("r n", 2 * 2 * INNER, r=2)
        wqkv_sb = sb("wqkv_sb", [P, QKV])
        wo_sb = sb("wo_sb", [P, 2, 2, D])
        w1_sb = sb("w1_sb", [P, 2 * HID])
        w2_sb = sb("w2_sb", [P, NH, D])
        b1_sb = sb("b1_sb", [P, DEPTH, 2, NH])
        b2_sb = sb("b2_sb", [P, DEPTH, D])
        ln_gb = sb("ln_gb", [P, 2, DEPTH])
        rope_l = sb("rope_l", [P, DEPTH, 4, TB, LD])
        scale_sb = room_m[:, 0:DEPTH * 4 * LD].rearrange("p (l k d) -> p l k d", l=DEPTH, k=4)
        hs_T = room_m[:, 0:B * (S + 1)].rearrange("p (b n) -> p b n", b=B)
        norm_sq = sb("norm_sq", [P, T, 2 * LH])
        norm_r = sb("norm_r", [P, T, 2 * LH])
        row_max = sb("row_max", [P, 2, PAIRS])
        o_den = sb("o_den", [P, 2, PAIRS])
        take = carve(room_w)
        s_rel = take("k r c", 2 * PAIRS * P, k=2, r=PAIRS)
        p_loc = take("k r c", 2 * PAIRS * P, k=2, r=PAIRS)
        pT_loc = take("k r c", 2 * PAIRS * P, k=2, r=PAIRS)
        oT_loc = take("k r a c", 2 * 4 * P, k=2, r=2, a=2)
        take = carve(room_a)
        gate_T = take("k n", NH * S, k=NH)
        o_loc = take("k r d", 2 * PAIRS * LD, k=2, r=PAIRS)
        ff_T = room_r[:, 0:B * NH * S].rearrange("p (b c n) -> p b c n", b=B, c=NH)

        names = """consts w_a_in x_in_s ffw_in eyes cond_rep_s ada_mm ada_s dve_step kpad_0 kpad_1 zero_s scores_mm
        probs_s pv_mm oraw_s den_mm oT_s wo_mm a_s h2_s h2T_mm h2T_s z_mm z_s zsq_mm z2_mm z2_used x2_s
        out_s zsum tanh_in_0 tanh_in_1 tanh_s_0 tanh_s_1 ln_num_0 ln_num_1 ln_num_all ln_den_0 ln_den_1
        ln_den_all rope_in room_0 room_1 rope_s lwt lw_qkv lw_wo lw_ff lT_mm lT_s lqk_mm lqk_s lv_mm lv_s
        lsq_s lred_s lc_s lx_s lrot_s lqkT_mm lqkT_s ls_mm lrel_s lp_s lpT_mm lpT_s lpv_mm lo_s loT_mm loT_s
        lwo_mm lx1_s lsh_mm lhn_s lhT_mm lhT_s la_mm lg_mm lgate_s lff_s lf2_mm lx2_s""".split()
        for b in range(B):
            names += [f"{n}_{b}" for n in "v head qk_f high hmod hT_mm hT qkv_mm u usq usum split qkT_mm qkT".split()]
        q = {n: sem(n) for n in names}
        kpad_s = [q["kpad_0"], q["kpad_1"]]

        NB = NW // B
        pre_bank = lambda b: 4 + 2 * b
        post_bank = lambda b: 6 if b == 0 else 0
        PRE_0, PRE_1, PRE_1_END = -1.95, -1.75, -0.68
        ATT_0, ATT_1_END = -0.95, 0.475
        POST_0, POST_1, POST_1_END = 0.03, 0.48, 1.6
        ROPE_0, WIN_0, ROPE_1, PERIOD = 1.06, 1.6, 1.69, 1
        WINDOWS_AFTER, FEED_AFTER = 0, 1
        FEED_LENGTH, LAST_FEED = 0.5, 0.55
        Z = 29 + 1.25 * FC
        NS = G * TB * 2
        LENGTH = dict(pre=14 + 2 * TB, att=NS + 5, post=Z + 16, rope=TB + 4, win=NB + 5, feed=NH + 6)

        def spread(part, kind, a=0.0, b=1.0):
            here = end = step = 0.0
            for y in part:
                if y is None:
                    here = min(here + step, end)
                elif isinstance(y, tuple):
                    here, end, step = y[0], y[1], (y[1] - y[0]) / y[2]
                else:
                    here, end, step = y, y, 0.0
                yield a + (b - a) * here / LENGTH[kind]

        def together(*parts):
            live = [[next(part), k, part] for k, part in enumerate(parts)]
            while live:
                first = min(live, key=lambda p: p[:2])
                at = next(first[2], None)
                if at is None:
                    live.remove(first)
                else:
                    first[0] = at

        def schedule(pre, att, post, rope_part, windows, feed):
            parts = [spread(pre(0), "pre", PRE_0, ATT_0), spread(pre(1), "pre", PRE_1, PRE_1_END),
                     spread(att(0), "att", ATT_0, 0.0), spread(att(1), "att", 0.0, ATT_1_END),
                     spread(post(0), "post", POST_0, POST_0 + 1), spread(post(1), "post", POST_1, POST_1_END),
                     spread(rope_part(0, 0), "rope", ROPE_0, WIN_0), spread(rope_part(0, 1), "rope", ROPE_1, WIN_0 + PERIOD)]
            for m in range(DEPTH * B):
                l, b = divmod(m, B)
                at = WIN_0 + m * PERIOD
                parts.append(spread(windows(l, b), "win", at + WINDOWS_AFTER, at + WINDOWS_AFTER + 1))
                at += FEED_AFTER
                if l + 1 < DEPTH:
                    parts.append(spread(feed(l, b), "feed", at, at + FEED_LENGTH))
                    parts.append(spread(rope_part(l + 1, b), "rope", at + FEED_LENGTH, WIN_0 + (m + B) * PERIOD))
                else:
                    parts.append(spread(feed(l, b), "feed", at, at + LAST_FEED))
            together(*parts)

        block = ctx.enter_context(nc.Block())

        @block.sync
        def _(sp):
            row = lambda a, n: a.rearrange("(o n) -> o n", o=1).to_broadcast([P, n])
            sp.dma_start(x_in[:, :, :], x.rearrange("b (t p) d -> p (b t) d", p=P)).then_inc(q["x_in_s"], 16)
            sp.dma_start(eye_f[:, :], eye).then_inc(q["consts"], 16)
            sp.dma_start(shift_f[:, :, :], shift.rearrange("k p m -> p k m")).then_inc(q["consts"], 16)
            sp.dma_start(pick_f[:, :], denom_pick).then_inc(q["consts"], 16)
            sp.dma_start(mask_f[:, :, :], masks.rearrange("k p m -> p k m")).then_inc(q["consts"], 16)
            sp.dma_start(cond_T[:, :], cond_1024).then_inc(q["consts"], 16)
            sp.dma_start(w_ada_sb[:, :], w_ada).then_inc(q["w_a_in"], 16)
            sp.dma_start(b_ada_sb[:, :], row(b_ada, 6 * D)).then_inc(q["w_a_in"], 16)
            for i, (w, b) in enumerate(((w_q, b_q), (w_k, b_k), (w_v, b_v))):
                sp.dma_start(w_qkv_sb[:, i * D:(i + 1) * D], w).then_inc(q["w_a_in"], 16)
                sp.dma_start(b_qkv_sb[:, i * D:(i + 1) * D], row(b, D)).then_inc(q["w_a_in"], 16)
            sp.wait_ge(q["zero_s"], 3)
            for j in range(4):
                sp.dma_start(w_o_sb[32 * j:32 * j + HD, :, :],
                             w_o.rearrange("(g j d) n -> j d g n", g=G, j=4)[j]).then_inc(q["ffw_in"], 16)
            sp.dma_start(w_o_sb[HD:HD + 1, 0, :], b_o.rearrange("(o n) -> o n", o=1)).then_inc(q["ffw_in"], 16)
            sp.dma_start(w_f1_sb[:, :], w_f1).then_inc(q["ffw_in"], 16)
            sp.dma_start(b_f1_sb[:, :], b_f1).then_inc(q["ffw_in"], 16)
            sp.dma_start(w_f2_sb[:, :, :], w_f2.rearrange("(c p) n -> p c n", p=P)).then_inc(q["ffw_in"], 16)
            sp.dma_start(b_f2_sb[:, :], row(b_f2, D)).then_inc(q["ffw_in"], 16)
            sp.dma_start(rope_l[:, DEPTH - 1, :, :, :], rope.rearrange("k (t p) d -> p k t d", p=P)).then_inc(q["rope_in"], 16)
            for l in range(DEPTH):
                for k, sc in enumerate((q_scale, k_scale)):
                    sp.dma_start(scale_sb[:, l, k, :], row(sc[l], LD)).then_inc(q["rope_in"], 16)
                    for h0 in (0, LD // 2):
                        h1 = LD // 2 - h0
                        sp.dma_start(scale_sb[:, l, 2 + k, h0:h0 + LD // 2], row(sc[l, h1:h1 + LD // 2], LD // 2)).then_inc(q["rope_in"], 16)
                sp.dma_start(b2_sb[:, l, :], row(b2[l], D)).then_inc(q["lwt"], 16)
            sp.dma_start(b1_sb[:, :, :, :], b1.rearrange("p (l k c) -> p l k c", l=DEPTH, k=2)).then_inc(q["lwt"], 16)
            for k, g in enumerate((ln_g, ln_b)):
                sp.dma_start(ln_gb[:, k, :], g).then_inc(q["lwt"], 16)

            def layer_weights(l):
                if l:
                    sp.wait_ge(q["lv_mm"], l * T)
                sp.dma_start(wqkv_sb[:, :], wqkv[l]).then_inc(q["lw_qkv"], 16)
                if l:
                    sp.wait_ge(q["lwo_mm"], l * T)
                for e in range(2):
                    for r in range(2):
                        sp.dma_start(wo_sb[LD * e:LD * e + LD, r, :, :],
                                     wo[l].rearrange("(r e a d) n -> r e d a n", r=2, e=2, a=2)[r, e]).then_inc(q["lw_wo"], 16)
                if l:
                    sp.wait_ge(q["lf2_mm"], l * B)
                sp.dma_start(w1_sb[:, :], w1[l]).then_inc(q["lw_ff"], 16)
                for c, (c0, cn) in enumerate(HC):
                    sp.dma_start(w2_sb[0:cn, c, :], w2[l, c0:c0 + cn, :]).then_inc(q["lw_ff"], 16)

            layer_weights(0)
            sp.wait_ge(q["zero_s"], 4)
            for b in range(B):
                sp.wait_ge(q[f"qkT_{b}"], 2 * TB)
                for j in range(4):
                    r = slice(32 * j, 32 * j + 32)
                    sp.dma_start(k_pad[r, b, :, j, :], k_T[r, :, b * S:(b + 1) * S]).then_inc(kpad_s[b], 16)
            for l in range(1, DEPTH):
                layer_weights(l)
            sp.wait_ge(q["lx2_s"], 1 + B * DEPTH)
            sp.dma_start(out.rearrange("b (t p) d -> p (b t) d", p=P), xr[:, :, :]).then_inc(q["out_s"], 16)
            sp.wait_ge(q["out_s"], 16)

        @block.gpsimd
        def _(pool):
            nc.gpsimd.memset(v_aug[:, :, :, :], 0.0).then_inc(q["zero_s"], 1)
            nc.gpsimd.memset(w_o_sb[:, :, :], 0.0).then_inc(q["zero_s"], 1)
            pool.wait_ge(q["zero_s"], 2)
            nc.gpsimd.memset(v_aug[:, :, :, HD:HD + 1], 1.0).then_inc(q["zero_s"], 1)
            nc.gpsimd.memset(k_pad[:, :, :, :, :].rearrange("p b g j t -> p (b g j t)").bitcast(I32), 0).then_inc(q["zero_s"], 1)
            def zeros(b):
                done = q[f"room_{b}"]
                nc.gpsimd.memset(k_loc[:, b, :, 0:WIN], 0.0).then_inc(done, 1)
                nc.gpsimd.memset(v_loc[:, b, 0, 0, :, 0:LD], 0.0).then_inc(done, 1)
                nc.gpsimd.memset(v_loc[:, b, :, :, :, LD:LD + 1], 1.0).then_inc(done, 1)
                pool.wait_ge(done, 4)
                nc.gpsimd.memset(hs_T[P // 2:P, b, 0:1], 0.0).then_inc(done, 1)
                pool.wait_ge(done, 5)

            def pre(b):
                yield 13
                pool.wait_ge(q[f"head_{b}"], 1)
                for t in range(TB):
                    nc.gpsimd.tensor_tensor(v_aug[:, b * TB + t, :, 0:HD], u_qkv[:, b, t, 2 * H:3 * H, :],
                                            head_f[:, b, t, 2 * H:3 * H].unsqueeze(2).to_broadcast([P, H, HD]),
                                            ALU.mult).then_inc(q[f"v_{b}"], 1)

            def att(b):
                if b == 0:
                    yield 0
                    pool.wait_ge(q["rope_in"], 16 * (1 + 6 * DEPTH))
                    for l in range(DEPTH):
                        for k in range(4):
                            nc.gpsimd.tensor_tensor(rope_l[:, l, k, :, :], rope_l[:, DEPTH - 1, k, :, :],
                                                    scale_sb[:, l, k, :].unsqueeze(1).to_broadcast([P, TB, LD]),
                                                    ALU.mult).then_inc(q["rope_s"], 1)
                else:
                    yield 0
                    pool.wait_ge(q["scores_mm"], NS)
                    nc.gpsimd.memset(q_blk[:, 0], 0.0).then_inc(q["room_0"], 1)
                    yield NS + 4.5
                    pool.wait_ge(q["oT_s"], B * G)
                    zeros(0)

            def post(b):
                for c in range(1, FC):
                    yield 29.1 + 1.25 * c
                    pool.wait_ge(q["z_s"], 2 * (b * FC + c + 1))
                    if c > 1:
                        pool.wait_ge(q["zsum"], b * (FC - 1) + c - 1)
                    nc.gpsimd.tensor_tensor(z_sq[b][:, 0, :], z_sq[b][:, 0, :], z_sq[b][:, c, :], ALU.add).then_inc(q["zsum"], 1)

            def rope_part(l, b):
                m = l * B + b
                yield 0
                if m == 0:
                    pool.wait_ge(q["wo_mm"], B)
                if m == 1:
                    pool.wait_ge(q["x2_s"], B)
                    nc.gpsimd.memset(q_blk[:, 1], 0.0).then_inc(q["room_1"], 1)
                    zeros(1)
                for t in range(TB):
                    i = m * TB + t
                    yield 1 + t + 0.333
                    pool.wait_ge(q["lqk_s"], 2 * (i + 1))
                    if i >= 2:
                        pool.wait_ge(q["lx_s"], i - 1)
                    for k in range(2):
                        pool_src = qk_raw[:, i % 2, k * INNER:(k + 1) * INNER].rearrange("p (h a d) -> p h a d", h=LH, a=2)
                        last = nc.gpsimd.tensor_tensor(
                            qk_cross[:, i % 2, k * INNER:(k + 1) * INNER].rearrange("p (h a d) -> p h a d", h=LH, a=2),
                            pool_src[:, :, ::-1, :],
                            rope_l[:, l, 2 + k, t, :].rearrange("p (a d) -> p a d", a=2).unsqueeze(1)
                            .to_broadcast([P, LH, 2, LD // 2]), ALU.mult)
                    last.then_inc(q["lc_s"], 1)

            def nothing(l, b):
                yield 0

            schedule(pre, att, post, rope_part, nothing, nothing)

        @block.tensor
        def _(pe):
            pe.wait_ge(q["consts"], 80)
            pe.wait_ge(q["eyes"], 1)
            pe.wait_ge(q["w_a_in"], 16 * 8)

            def transpose_mod(b, dst):
                for t in range(TB):
                    last = nc.tensor.transpose(bank[:, dst, t * P:(t + 1) * P], h_mod[:, b * TB + t, :], eye_f[:, :])
                return last

            def pre(b):
                lo = pre_bank(b)
                if b == 0:
                    yield 0
                    for c in range(B):
                        pe.wait_ge(q["cond_rep_s"], c + 1)
                        for half in range(2):
                            last = nc.tensor.matmul(bk(2 * c + half, 3 * D), cond_rep[:, c, :],
                                                    w_ada_sb[:, half * 3 * D:(half + 1) * 3 * D], start=True, stop=True)
                        last.then_inc(q["ada_mm"], 1)
                yield 4
                pe.wait_ge(q[f"hmod_{b}"], 1)
                transpose_mod(b, lo).then_inc(q[f"hT_mm_{b}"], 1)
                for t in range(TB):
                    yield 5 + t
                    n = b * TB + t
                    if t == 0:
                        pe.wait_ge(q[f"hT_{b}"], 1)
                    if t >= 2:
                        pe.wait_ge(q[f"u_{b}"], t - 1)
                    nc.tensor.matmul(bk(lo + 1 - t % 2, 3 * D), hT[:, n * P:(n + 1) * P], w_qkv_sb[:, :],
                                     start=True, stop=True).then_inc(q[f"qkv_mm_{b}"], 1)
                for t in range(TB):
                    yield 15.8 + 2 * t
                    pe.wait_ge(q[f"split_{b}"], t + 1)
                    if t >= 2:
                        pe.wait_ge(q[f"qkT_{b}"], 2 * (t - 1))
                    dst = bank[:, lo + t % 2, :].bitcast(F16)
                    for i, sp_t in enumerate((q_split, k_split)):
                        for g in range(G):
                            c = (i * G + g) * P
                            last = nc.tensor.transpose(dst[:, c:c + P],
                                                       sp_t[b, t % 2][:, 4 * g:4 * g + 4, :, :].rearrange("p a b c -> p (a b c)"),
                                                       eye_h[:, :])
                    last.then_inc(q[f"qkT_mm_{b}"], 1)

            steps = [(g, kt, hp) for g in range(G) for kt in range(TB) for hp in range(2)]

            def scores(b, i):
                g, kt, hp = steps[i]
                n = b * NS + i
                if i == 0:
                    pe.wait_ge(q["ada_s"], B)
                    pe.wait_ge(q[f"qkT_{b}"], 2 * TB)
                    pe.wait_ge(kpad_s[b], 64)
                    pe.wait_ge(q[f"v_{b}"], TB)
                if n >= 2:
                    pe.wait_ge(q["probs_s"], n - 1)
                for i in range(2):
                    j = 2 * hp + i
                    last = nc.tensor.matmul(bk(2 * (n % 2) + i), k_pad[:, b, g, j, kt * P:(kt + 1) * P],
                                            q_T[:, g, b * S:(b + 1) * S], start=True, stop=True)
                last.then_inc(q["scores_mm"], 1)

            def weigh(b, i):
                g, kt, hp = steps[i]
                n = b * NS + i
                bg = b * G + g
                pe.wait_ge(q["probs_s"], n + 1)
                if kt == 0 and hp == 0 and bg >= 2:
                    pe.wait_ge(q["oT_s"], bg - 1)
                for i in range(2):
                    j = 2 * hp + i
                    last = nc.tensor.matmul(bank[32 * j:32 * j + 32, 4 + bg % 2, :],
                                            v_aug[:, b * TB + kt, 4 * g + j, :], probs[:, n % 3, i, :],
                                            start=(kt == 0), stop=(kt == TB - 1), skip_group_check=True)
                last.then_inc(q["pv_mm"], 1)

            def att(b):
                per = TB * 2
                for i in range(NS + 5):
                    yield i
                    if i < NS:
                        scores(b, i)
                    if 2 <= i < NS + 2:
                        weigh(b, i - 2)
                    if i >= per + 4 and (i - 4) % per == 0:
                        bg = b * G + (i - 4) // per - 1
                        pe.wait_ge(q["oraw_s"], bg + 1)
                        nc.tensor.matmul(bk(4 + bg % 2), pick_f[:, :], o_raw[:, :], start=True, stop=True).then_inc(q["den_mm"], 1)

            def post(b):
                lo = post_bank(b)
                for t in range(TB):
                    yield t
                    if t == 0:
                        for c in range(B):
                            pe.wait_ge(q[f"qkT_{c}"], 2 * TB)
                        pe.wait_ge(q["oT_s"], G * (b + 1))
                        pe.wait_ge(q["ffw_in"], 16 * 9)
                    for g in range(G):
                        last = nc.tensor.matmul(bank[:, lo, t * P:(t + 1) * P], o_T[:, g, t * P:(t + 1) * P],
                                                w_o_sb[:, g, :], start=(g == 0), stop=(g == G - 1))
                last.then_inc(q["wo_mm"], 1)
                yield 28
                pe.wait_ge(q["h2_s"], b + 1)
                transpose_mod(b, lo + 1).then_inc(q["h2T_mm"], 1)
                for c in range(FC):
                    yield 29 + 1.25 * c
                    n = b * FC + c
                    if c == 0:
                        pe.wait_ge(q["h2T_s"], b + 1)
                    if c >= 2:
                        pe.wait_ge(q["z_s"], 2 * (n - 1))
                    nc.tensor.matmul(bk(lo + c % 2), w_f1_sb[:, c * P:(c + 1) * P], hT[:, b * S:(b + 1) * S],
                                     start=True, stop=True).then_inc(q["z_mm"], 1)
                yield Z
                pe.wait_ge(q["z_s"], 2 * FC * (b + 1))
                pe.wait_ge(q["zsum"], (FC - 1) * (b + 1))
                for t in range(TB):
                    last = nc.tensor.matmul(bank[:, lo, t:t + 1], z_sq[b][:, 0, t * P:(t + 1) * P], ones_col[:, :],
                                            start=True, stop=True)
                last.then_inc(q["zsq_mm"], 1)
                for t in range(TB):
                    yield Z + 1 + 0.8 * t
                    for c in range(FC):
                        last = nc.tensor.matmul(bank[:, lo + 1, t * P:(t + 1) * P], z_T[b][:, c, t * P:(t + 1) * P],
                                                w_f2_sb[:, c, :], start=(c == 0), stop=(c == FC - 1))
                last.then_inc(q["z2_mm"], 1)

            def rope_part(l, b):
                m = l * B + b
                yield 0
                if m == 0:
                    pe.wait_ge(q["lwt"], 16 * (DEPTH + 3))
                else:
                    pe.wait_ge(q["lqkT_s"], m * TB)
                    pe.wait_ge(q["lv_s"], m * TB)
                if b == 0:
                    pe.wait_ge(q["lw_qkv"], 16 * (l + 1))
                pe.wait_ge(q["x2_s"], b + 1) if l == 0 else pe.wait_ge(q["lx2_s"], m - B + 1)
                for t in range(TB):
                    last = nc.tensor.transpose(bank[:, 7, t * P:(t + 1) * P], xr[:, b * TB + t, :], eye_f[:, :])
                last.then_inc(q["lT_mm"], 1)
                for t in range(TB + 3):
                    i = m * TB + t
                    if t < TB:
                        for k in range(2):
                            yield 1 + t + 0.333 * k
                            if t == 0 and k == 0:
                                pe.wait_ge(q["lT_s"], m + 1)
                            if i >= 1:
                                pe.wait_ge(q["lsq_s"], 2 * i + k - 1)
                            if t >= 4:
                                pe.wait_ge(q["lqkT_s"], i - 3)
                            nc.tensor.matmul(bk(5 + k), hs_T[:, b, t * P:(t + 1) * P],
                                             wqkv_sb[:, k * INNER:(k + 1) * INNER], start=True, stop=True).then_inc(q["lqk_mm"], 1)
                        yield 1 + t + 0.587
                        if i >= 1:
                            pe.wait_ge(q["lv_s"], i)
                        nc.tensor.matmul(bk(7), hs_T[:, b, t * P:(t + 1) * P], wqkv_sb[:, 2 * INNER:],
                                         start=True, stop=True).then_inc(q["lv_mm"], 1)
                    if t >= 3:
                        yield 1 + t + 0.9
                        i = m * TB + t - 3
                        pe.wait_ge(q["lrot_s"], i + 1)
                        pe.wait_ge(q["lsq_s"], 2 * (m * TB + min(t, TB - 1) + 1))
                        if i >= 1:
                            pe.wait_ge(q["lqkT_s"], i)
                        for c in range(2 * PAIRS):
                            last = nc.tensor.transpose(bank[:, 5 + c // PAIRS, (c % PAIRS) * P:(c % PAIRS + 1) * P],
                                                       qk_rot[:, i % 4, c * P:(c + 1) * P], eye_f[:, :])
                        last.then_inc(q["lqkT_mm"], 1)

            def windows(l, b):
                m = l * B + b
                for w in range(NB + 5):
                    yield w
                    if w == 0:
                        pe.wait_ge(q["lqkT_s"], (m + 1) * TB)
                        pe.wait_ge(q["lv_s"], (m + 1) * TB)
                        if m == 0:
                            pe.wait_ge(q["z2_used"], B)
                    if w < NB:
                        j = m * NB + w
                        if j >= 2:
                            pe.wait_ge(q["lrel_s"], j - 1)
                        nc.tensor.matmul(bk(j % 2), eye_b[:, :], mask_b[:, int(w == 0), :].unsqueeze(1).to_broadcast([P, PAIRS, P]),
                                         start=True, stop=False)
                        for r in range(PAIRS):
                            last = nc.tensor.matmul(bank[:, j % 2, r * P:(r + 1) * P], q_blk[:, b, r, w, :],
                                                    k_loc[:, b, r, w * WIN:w * WIN + P], start=False, stop=(r == PAIRS - 1))
                        last.then_inc(q["ls_mm"], 1)
                    if w >= 6 and w % 2 == 0:
                        i = m * TB + (w - 6) // 2
                        if b == 0 and w == 6:
                            pe.wait_ge(q["lw_wo"], 64 * (l + 1))
                        pe.wait_ge(q["loT_s"], min(2 * i + 3, NB * (m + 1)))
                        for c in range(4):
                            last = nc.tensor.matmul(bank[:, 4, 2 * P:3 * P], oT_loc[:, i % 2, c // 2, c % 2, :],
                                                    wo_sb[:, c // 2, c % 2, :], start=(c == 0), stop=(c == 3), skip_group_check=True)
                        last.then_inc(q["lwo_mm"], 1)
                    yield w + 0.34
                    if 1 <= w <= NB:
                        j = m * NB + w - 1
                        pe.wait_ge(q["lp_s"], j + 1)
                        if j >= 1:
                            pe.wait_ge(q["lpT_s"], j)
                        for r in range(PAIRS):
                            last = nc.tensor.transpose(bank[:, 2, r * P:(r + 1) * P], p_loc[:, j % 2, r, :], eye_f[:, :])
                        last.then_inc(q["lpT_mm"], 1)
                    if 2 <= w <= NB + 1:
                        yield w + 0.64
                        j = m * NB + w - 2
                        pe.wait_ge(q["lpT_s"], j + 1)
                        if j >= 1:
                            pe.wait_ge(q["lo_s"], j)
                        for r in range(PAIRS):
                            for a in range(2):
                                last = nc.tensor.matmul(bank[WIN * a:WIN * a + WIN, 3, r * (LD + 1):(r + 1) * (LD + 1)],
                                                        pT_loc[:, j % 2, r, WIN * a:WIN * a + WIN],
                                                        v_loc[:, b, (w - 2) % 2, (w - 2) // 2, 2 * r + a, :],
                                                        start=True, stop=True, skip_group_check=True)
                        last.then_inc(q["lpv_mm"], 1)
                    if 3 <= w <= NB + 2:
                        yield w + 0.65
                        j = m * NB + w - 3
                        pe.wait_ge(q["lo_s"], j + 1)
                        if j >= 1:
                            pe.wait_ge(q["loT_s"], j)
                        if w >= 6 or m:
                            pe.wait_ge(q["lx1_s"], m * TB + max(0, (w - 4) // 2))
                        for r in range(2):
                            last = nc.tensor.transpose(bank[:, 4, r * P:(r + 1) * P],
                                                       o_loc[:, j % 2, 2 * r:2 * r + 2, :].rearrange("p r d -> p (r d)"), eye_f[:, :])
                        last.then_inc(q["loT_mm"], 1)

            def feed(l, b):
                m = l * B + b
                yield 0
                before = min((m + 2) * TB, DEPTH * T)
                pe.wait_ge(q["lqkT_s"], before)
                pe.wait_ge(q["lv_s"], before)
                if m:
                    pe.wait_ge(q["lx2_s"], m)
                for t in range(TB):
                    n = b * TB + t
                    pe.wait_ge(q["lx1_s"], l * T + n + 1)
                    last = nc.tensor.matmul(bank[:, 5, t * 64:t * 64 + 64], shift_f[:, 0, :], xr[:, n, 64:128],
                                            start=True, stop=(t == 0), skip_group_check=True)
                    if t:
                        last = nc.tensor.matmul(bank[:, 5, t * 64:t * 64 + 64], shift_f[:, 1, :], xr[:, n - 1, 64:128],
                                                start=False, stop=True, skip_group_check=True)
                last.then_inc(q["lsh_mm"], 1)
                yield 3
                pe.wait_ge(q["lhn_s"], m + 1)
                for t in range(TB):
                    last = nc.tensor.transpose(bank[:, 6, t * P:(t + 1) * P], h_mod[:, b * TB + t, :], eye_f[:, :])
                last.then_inc(q["lhT_mm"], 1)
                for c, (c0, cn) in enumerate(HC):
                    yield 3 + 1 + 0.3 * c
                    if c == 0:
                        pe.wait_ge(q["lhT_s"], m + 1)
                        if b == 0:
                            pe.wait_ge(q["lw_ff"], 16 * (1 + NH) * (l + 1))
                    nc.tensor.matmul(bank[0:cn, 5 + c, :], w1_sb[:, HID + c0:HID + c0 + cn], hT[:, b * S:(b + 1) * S],
                                     start=True, stop=True).then_inc(q["lg_mm"], 1)
                for c, (c0, cn) in enumerate(HC):
                    yield 3 + 2.3 + 0.5 * c
                    pe.wait_ge(q["lgate_s"], m * NH + c + 1)
                    nc.tensor.matmul(bank[0:cn, 5 + c, :], w1_sb[:, c0:c0 + cn], hT[:, b * S:(b + 1) * S],
                                     start=True, stop=True).then_inc(q["la_mm"], 1)
                for t in range(TB):
                    yield 7 + t / TB
                    if t == 0:
                        pe.wait_ge(q["lff_s"], (m + 1) * NH)
                    for c, (c0, cn) in enumerate(HC):
                        last = nc.tensor.matmul(bank[:, 5, t * P:(t + 1) * P], ff_T[0:cn, b, c, t * P:(t + 1) * P],
                                                w2_sb[0:cn, c, :], start=(c == 0), stop=(c == NH - 1), skip_group_check=True)
                last.then_inc(q["lf2_mm"], 1)

            schedule(pre, att, post, rope_part, windows, feed)

        @block.scalar
        def _(act):
            Hf = P // 2

            def logs(which, tiles):
                act.wait_ge(q[f"ln_num_{which}"], 1)
                nc.scalar.activation(sml[:, 2, tiles], sml[:, 0, tiles], ACT.Ln, bias=ones_col[:, 0:1], scale=1.0)
                nc.scalar.activation(sml[:, 3, tiles], sml[:, 0, tiles], ACT.Ln, bias=ones_col[:, 0:1],
                                     scale=-1.0).then_inc(q[f"ln_den_{which}"], 1)

            def tanh(b, step):
                tiles = slice(b * TB, (b + 1) * TB)
                act.wait_ge(q[f"tanh_in_{b}"], step)
                nc.scalar.activation(sml[:, 9, tiles], sml[:, 8, tiles], ACT.Tanh).then_inc(q[f"tanh_s_{b}"], 1)

            def pre(b):
                if b == 0:
                    yield 0
                    logs("all", slice(0, T))
                lo = pre_bank(b)
                yield 4
                act.wait_ge(q[f"hT_mm_{b}"], 1)
                nc.scalar.activation(hT[:, b * S:(b + 1) * S], bk(lo), ACT.Copy).then_inc(q[f"hT_{b}"], 1)
                for t in range(TB):
                    yield 5 + t
                    act.wait_ge(q[f"u_{b}"], t + 1)
                    if t >= 2:
                        act.wait_ge(q[f"usum_{b}"], t - 1)
                    nc.scalar.activation(sq[:, b, t % 2, :], u_qkv[:, b, t, :, :].rearrange("p h d -> p (h d)"),
                                         ACT.Square).then_inc(q[f"usq_{b}"], 1)
                twice = lambda a: a.unsqueeze(2).to_broadcast([P, H, 2, HD])
                for t in range(TB + 1):
                    if t < TB:
                        yield 13.5 + 2 * t
                        act.wait_ge(q[f"qk_f_{b}"], t + 1)
                        nc.scalar.activation(q_split[b, t % 2][:, :, 0:2, :], twice(qk_f[b, t % 2][:, 0:H, :]), ACT.Copy).then_inc(q[f"high_{b}"], 1)
                        nc.scalar.activation(k_split[b, t % 2][:, :, 0:3:2, :], twice(qk_f[b, t % 2][:, H:2 * H, :]), ACT.Copy).then_inc(q[f"high_{b}"], 1)
                    if t >= 1:
                        yield 13.9 + 2 * t
                        n = b * TB + t - 1
                        act.wait_ge(q[f"qkT_mm_{b}"], t)
                        src = bank[:, lo + (t - 1) % 2, :].bitcast(F16).rearrange("p (i g t) -> p i g t", i=2, g=G)
                        nc.scalar.activation(q_T[:, :, n * P:(n + 1) * P], src[:, 0, :, :], ACT.Copy).then_inc(q[f"qkT_{b}"], 1)
                        nc.scalar.activation(k_T[:, :, n * P:(n + 1) * P], src[:, 1, :, :], ACT.Copy).then_inc(q[f"qkT_{b}"], 1)

            def att(b):
                for i in range(NS):
                    yield i
                    n = b * NS + i
                    act.wait_ge(q["scores_mm"], n + 1)
                    if n >= 3:
                        act.wait_ge(q["pv_mm"], n - 2)
                    nc.scalar.activation(probs[:, n % 3, :, :], bank[:, 2 * (n % 2):2 * (n % 2) + 2, :], ACT.Exp,
                                         scale=2.0 ** (-2 * EXP_SCALE_BITS) / math.sqrt(HD)).then_inc(q["probs_s"], 1)

            def post(b):
                yield 5
                act.wait_ge(q["wo_mm"], b + 1)
                nc.scalar.activation(a_sb[:, b, :, :].rearrange("p t d -> p (t d)"), bk(post_bank(b)), ACT.Copy).then_inc(q["a_s"], 1)
                yield 11
                tanh(b, 1)
                yield 19.15
                logs(b, slice(b * TB, (b + 1) * TB))
                yield 28
                act.wait_ge(q["h2T_mm"], b + 1)
                nc.scalar.activation(hT[:, b * S:(b + 1) * S], bk(post_bank(b) + 1), ACT.Copy).then_inc(q["h2T_s"], 1)
                for c in range(FC):
                    yield 29 + 1.25 * c
                    n = b * FC + c
                    act.wait_ge(q["z_mm"], n + 1)
                    nc.scalar.activation(z_T[b][:, c, :], bk(post_bank(b) + c % 2), ACT.Identity, bias=b_f1_sb[:, c:c + 1]).then_inc(q["z_s"], 1)
                    nc.scalar.activation(z_sq[b][:, c, :], bk(post_bank(b) + c % 2), ACT.Square, bias=b_f1_sb[:, c:c + 1]).then_inc(q["z_s"], 1)
                yield Z + 11.98
                tanh(b, 2)

            def rope_part(l, b):
                m = l * B + b
                yield 0
                if l == 0:
                    act.wait_ge(q[f"room_{b}"], 5)
                act.wait_ge(q["lT_mm"], m + 1)
                nc.scalar.activation(hs_T[0:Hf, b, 0:S], bank[0:Hf, 7, :], ACT.Copy)
                nc.scalar.activation(hs_T[Hf:P, b, 1:S + 1], bank[Hf:P, 7, :], ACT.Copy).then_inc(q["lT_s"], 1)
                for t in range(TB + 3):
                    i = m * TB + t
                    if t < TB:
                        for k in range(2):
                            yield 1 + t + 0.333 * k
                            if i >= 2 and k == 0:
                                act.wait_ge(q["lx_s"], i - 1)
                                act.wait_ge(q["lred_s"], i - 1)
                            act.wait_ge(q["lqk_mm"], 2 * i + k + 1)
                            part = slice(k * INNER, (k + 1) * INNER)
                            nc.scalar.activation(qk_raw[:, i % 2, part], bk(5 + k), ACT.Copy).then_inc(q["lqk_s"], 1)
                            nc.scalar.activation(qk_sq[:, i % 2, part], bk(5 + k), ACT.Square).then_inc(q["lsq_s"], 1)
                        yield 1 + t + 0.587
                        act.wait_ge(q["lv_mm"], i + 1)
                        vs = bk(7).rearrange("p (h d) -> p h d", d=LD)
                        nc.scalar.activation(v_loc[:, b, 1, t, :, 0:LD], vs, ACT.Copy)
                        if t < TB - 1:
                            nc.scalar.activation(v_loc[WIN:P, b, 0, t + 1, :, 0:LD], vs[WIN:P], ACT.Copy)
                        nc.scalar.activation(v_loc[0:WIN, b, 0, t, :, 0:LD], vs[0:WIN], ACT.Copy).then_inc(q["lv_s"], 1)
                    if t >= 3:
                        yield 1 + t + 0.9
                        i, t3 = i - 3, t - 3
                        act.wait_ge(q["lqkT_mm"], i + 1)
                        qs = bk(5).rearrange("p (r w c) -> p r w c", r=PAIRS, w=2)
                        nc.scalar.activation(q_blk[0:Hf, b, :, 2 * t3:2 * t3 + 2, 0:WIN], qs[0:Hf], ACT.Copy)
                        nc.scalar.activation(q_blk[Hf:P, b, :, 2 * t3:2 * t3 + 2, WIN:P], qs[Hf:P], ACT.Copy)
                        nc.scalar.activation(k_loc[:, b, :, WIN + t3 * P:WIN + (t3 + 1) * P],
                                             bk(6).rearrange("p (r c) -> p r c", r=PAIRS), ACT.Copy).then_inc(q["lqkT_s"], 1)

            def windows(l, b):
                m = l * B + b
                for w in range(NB + 3):
                    if w < NB:
                        yield w
                        j = m * NB + w
                        act.wait_ge(q["lrel_s"], j + 1)
                        if j >= 2:
                            act.wait_ge(q["lpT_mm"], j - 1)
                        to = p_loc[:, j % 2, :, :].rearrange("p r (k c) -> p r k c", k=2)
                        if w % 2 == 0:
                            to = to[:, :, ::-1, :]
                        nc.scalar.activation(to, s_rel[:, j % 2, :, :].rearrange("p r (k c) -> p r k c", k=2), ACT.Exp,
                                             scale=QK_SCALE).then_inc(q["lp_s"], 1)
                    if 1 <= w <= NB:
                        yield w + 0.34
                        j = m * NB + w - 1
                        act.wait_ge(q["lpT_mm"], j + 1)
                        if j >= 2:
                            act.wait_ge(q["lpv_mm"], j - 1)
                        nc.scalar.activation(pT_loc[:, j % 2, :, :].rearrange("p r c -> p (r c)"), bk(2), ACT.Copy).then_inc(q["lpT_s"], 1)
                    if 3 <= w:
                        yield w + 0.65
                        j = m * NB + w - 3
                        i = j // 2
                        act.wait_ge(q["loT_mm"], j + 1)
                        if i >= 2:
                            act.wait_ge(q["lwo_mm"], i - 1)
                        nc.scalar.activation(oT_loc[:, i % 2, :, :, (j % 2) * WIN:(j % 2 + 1) * WIN],
                                             bk(4, 2 * P).rearrange("p (r a c) -> p r a c", r=2, a=2), ACT.Copy).then_inc(q["loT_s"], 1)

            def feed(l, b):
                m = l * B + b
                yield 3
                act.wait_ge(q["lhT_mm"], m + 1)
                nc.scalar.activation(hT[:, b * S:(b + 1) * S], bk(6), ACT.Identity, scale=ln_gb[:, 0, l:l + 1],
                                     bias=ln_gb[:, 1, l:l + 1]).then_inc(q["lhT_s"], 1)
                yield 3 + 2
                if m:
                    act.wait_ge(q["lff_s"], m * NH)
                for c, (c0, cn) in enumerate(HC):
                    act.wait_ge(q["lg_mm"], m * NH + c + 1)
                    nc.scalar.activation(gate_T[0:cn, c, :], bank[0:cn, 5 + c, :], ACT.Gelu,
                                         bias=b1_sb[0:cn, l, 1, c:c + 1]).then_inc(q["lgate_s"], 1)

            schedule(pre, att, post, rope_part, windows, feed)

        @block.vector
        def _(dve):
            chain = [0]
            v = nc.vector

            def link(ins):
                chain[0] += 1
                here = chain[0]
                ins.then_inc(q["dve_step"], 1)
                yield
                dve.wait_ge(q["dve_step"], here)

            def publish(ins, sem, value):
                ins.then_inc(sem, 1)
                yield
                dve.wait_ge(sem, value)

            def tt(o, a, b, op):
                yield from link(v.tensor_tensor(o, a, b, op))

            def ts(o, a, s1, op0, s2=None, op1=ALU.bypass):
                yield from link(v.tensor_scalar(o, a, s1, s2, op0, op1))

            def stt(o, a, sc, b, op0, op1):
                yield from link(v.scalar_tensor_tensor(o, a, sc, b, op0, op1))

            def rsqrt(*roots):
                for o, a, f in roots:
                    last = v.tensor_scalar(o.bitcast(I32), a.bitcast(I32), -0.5, float(RSQRT_MAGIC), ALU.mult, ALU.add)
                yield from link(last)
                for add in (RSQRT_ADD, None):
                    for o, a, f in roots:
                        last = v.tensor_tensor(f, o, o, ALU.mult)
                    yield from link(last)
                    for o, a, f in roots:
                        if add:
                            last = v.scalar_tensor_tensor(f, f, RSQRT_MUL, a, ALU.mult, ALU.mult)
                        else:
                            last = v.tensor_tensor(f, f, a, ALU.mult)
                    yield from link(last)
                    if add is None:
                        for o, a, f in roots:
                            last = v.scalar_tensor_tensor(f, f, -10 / 3 * RSQRT_C ** 2, f, ALU.add, ALU.mult)
                        yield from link(last)
                    for o, a, f in roots:
                        last = v.scalar_tensor_tensor(o, f, add or 5 * RSQRT_C ** 4, o, ALU.add, ALU.mult)
                    yield from link(last)

            dve.wait_ge(q["consts"], 80)
            v.tensor_copy(eye_h[:, :], eye_f[:, :])
            v.tensor_copy(eye_b[:, :], eye_f[:, :])
            v.tensor_copy(mask_b[:, :, :], mask_f[:, :, :])
            v.memset(ones_col[:, :], 1.0).then_inc(q["eyes"], 1)
            dve.wait_ge(q["eyes"], 1)
            for b in range(B):
                v.tensor_copy(cond_rep[:, b, :], cond_T[:, b:b + 1].to_broadcast([P, P])).then_inc(q["cond_rep_s"], 1)

            def moments(src, t0, n):
                for t in range(t0, t0 + n):
                    last = v.bn_stats(bn6[:, t, 0:6], src[:, t, :])
                yield from link(last)
                for t in range(t0, t0 + n):
                    last = v.bn_aggr(mean_var[:, t, :], bn6[:, t, 0:6])
                yield from link(last)

            def inverse_std(which, t0, n, half=0, end=0):
                mean, var = mean_var[:, t0:t0 + n, 0], mean_var[:, t0:t0 + n, 1]
                r = lambda k: sml[:, k, t0:t0 + n]
                f = root_f[:, t0 // TB, 0:n]
                yield from tt(r(1), mean, mean, ALU.mult)
                yield from tt(r(1), r(1), var, ALU.add)
                yield from ts(r(1), r(1), float(D), ALU.mult, EPS * EPS, ALU.max)
                yield from rsqrt((r(4), r(1), f))
                yield from stt(r(5), r(1), 1.0, r(4), ALU.mult, ALU.mult)
                yield half, end, 20
                v.tensor_scalar(r(0), r(5), SMALL_NORM, MAX_TANH, ALU.max, ALU.min).then_inc(q[f"ln_num_{which}"], 1)
                dve.wait_ge(q[f"ln_num_{which}"], 1)
                yield from ts(r(6), r(1), SMALL_NORM ** 2, ALU.min)
                yield from stt(r(6), r(6), 3.75, r(6), ALU.add, ALU.mult)
                K = 2 * SMALL_RATIO
                yield from ts(r(6), r(6), -4 / 45 * K, ALU.mult, K, ALU.add)
                yield from tt(r(6), r(6), r(0), ALU.mult)
                dve.wait_ge(q[f"ln_den_{which}"], 1)
                yield from tt(r(5), r(2), r(3), ALU.subtract)
                yield from link(v.reciprocal(r(4), r(5)))
                yield from tt(r(6), r(6), r(4), ALU.mult)
                yield from stt(r(6), r(6), 1e-6, r(6), ALU.mult, ALU.mult)
                yield from tt(r(6), r(6), var, ALU.add)
                yield from rsqrt((r(5), r(6), f))

            def modulate(src, b, k_scale_row, k_shift_row, done=None):
                for t in range(TB):
                    last = v.tensor_scalar(h_mod[:, b * TB + t, :], src[:, b * TB + t, :], mean_var[:, b * TB + t, 0:1],
                                           sml[:, 5, b * TB + t:b * TB + t + 1], ALU.subtract, ALU.mult)
                yield from link(last)
                hb = h_mod[:, b * TB:(b + 1) * TB, :]
                wide = lambda k: ada[:, b, k, :].unsqueeze(1).to_broadcast([P, TB, D])
                yield from tt(hb, hb, wide(k_scale_row), ALU.mult)
                yield from link(v.tensor_tensor(hb, hb, wide(k_shift_row), ALU.add))
                tiles = slice(b * TB, (b + 1) * TB)
                for t in range(b * TB, (b + 1) * TB):
                    last = v.tensor_tensor_reduce(out=junk[:, b, t % TB, :], in0=h_mod[:, t, :], in1=h_mod[:, t, :],
                                                  scale=1.0, scalar=0.0, op0=ALU.mult, op1=ALU.add,
                                                  accum_out=sml[:, 6, t:t + 1])
                yield from link(last)
                yield from ts(sml[:, 6, tiles], sml[:, 6, tiles], EPS * EPS, ALU.max)
                yield from rsqrt((sml[:, 7, tiles], sml[:, 6, tiles], root_f[:, b, 0:TB]))
                last = v.tensor_scalar(sml[:, 7, tiles], sml[:, 7, tiles], MAX_ARTANH, 1.0, ALU.mult, ALU.min)
                if done is None:
                    yield from link(last)
                else:
                    yield from publish(last, done, 1)

            def sum_squares(b, t):
                dve.wait_ge(q[f"usq_{b}"], t + 1)
                v.tensor_reduce(head_sq[:, b, t, :], sq[:, b, t % 2, :].rearrange("p (h d) -> p h d", d=HD),
                                AXX, ALU.add).then_inc(q[f"usum_{b}"], 1)

            def pre(b):
                if b == 0:
                    yield 0
                    dve.wait_ge(q["x_in_s"], 16)
                    yield from moments(x_in, 0, T)
                    yield from inverse_std("all", 0, T)
                    dve.wait_ge(q["w_a_in"], 16 * 8)
                    for c in range(B):
                        dve.wait_ge(q["ada_mm"], c + 1)
                        for half in range(2):
                            last = v.tensor_tensor(ada[:, c, 3 * half:3 * half + 3, :].rearrange("p k d -> p (k d)"),
                                                   bk(2 * c + half, 3 * D), b_ada_sb[:, half * 3 * D:(half + 1) * 3 * D], ALU.add)
                        yield from link(last)
                        for k in (1, 4):
                            last = v.tensor_scalar(ada[:, c, k, :], ada[:, c, k, :], 1.0, None, ALU.add)
                        last.then_inc(q["ada_s"], 1)
                    dve.wait_ge(q["ada_s"], B)
                yield 0, 4, 20
                yield from modulate(x_in, b, 1, 0, q[f"hmod_{b}"])
                for t in range(TB):
                    yield 5 + t
                    dve.wait_ge(q[f"qkv_mm_{b}"], t + 1)
                    v.scalar_tensor_tensor(u_qkv[:, b, t, :, :].rearrange("p h d -> p (h d)"), bk(pre_bank(b) + 1 - t % 2, 3 * D),
                                           sml[:, 7, b * TB + t:b * TB + t + 1], b_qkv_sb[:, :], ALU.mult, ALU.add).then_inc(q[f"u_{b}"], 1)
                    if t:
                        yield
                        sum_squares(b, t - 1)
                yield 5 + TB, 14, 20
                sum_squares(b, TB - 1)
                dve.wait_ge(q[f"usum_{b}"], TB)
                flat = lambda a: a[:, b, :, :].rearrange("p t h -> p (t h)")
                yield from link(v.tensor_reduce(all_sq[:, b, :, :].rearrange("p t i -> p (t i)"),
                                     head_sq[:, b, :, :].rearrange("p t (i h) -> p (t i) h", h=H), AXX, ALU.add))
                v.tensor_scalar(flat(head_sq), flat(head_sq), EPS * EPS, None, ALU.max)
                yield from ts(flat(all_sq), flat(all_sq), EPS * EPS, ALU.max)
                yield from rsqrt((flat(head_f), flat(head_sq), root_f[:, b, 0:TB * 3 * H]),
                                 (flat(all_f), flat(all_sq), root_f[:, b, TB * 3 * H:]))
                v.tensor_scalar(flat(all_f), flat(all_f), RATIO * MAX_ARTANH, RATIO, ALU.mult, ALU.min)
                yield from ts(flat(head_f), flat(head_f), MAX_ARTANH, ALU.mult)
                hf = head_f[:, b, :, :].rearrange("p t (i h) -> p (t i) h", h=H)
                yield from tt(hf, hf, all_f[:, b, :, :].rearrange("p t i -> p (t i)").unsqueeze(2).to_broadcast([P, TB * 3, H]), ALU.min)
                v.tensor_scalar(head_f[:, b, :, 0:2 * H], head_f[:, b, :, 0:2 * H], 2.0 ** EXP_SCALE_BITS, None, ALU.mult)
                yield from publish(v.tensor_scalar(head_f[:, b, :, 2 * H:3 * H], head_f[:, b, :, 2 * H:3 * H], 1.0 / RATIO, None, ALU.mult),
                                   q[f"head_{b}"], 1)
                for t in range(TB + 1):
                    if t < TB:
                        yield 13 + 2 * t
                        if t >= 2:
                            dve.wait_ge(q[f"qkT_mm_{b}"], t - 1)
                        v.tensor_tensor(qk_f[b, t % 2], u_qkv[:, b, t, 0:2 * H, :],
                                        head_f[:, b, t, 0:2 * H].unsqueeze(2).to_broadcast([P, 2 * H, HD]), ALU.mult).then_inc(q[f"qk_f_{b}"], 1)
                    if t >= 1:
                        yield 13.6 + 2 * t
                        k = (t - 1) % 2
                        dve.wait_ge(q[f"high_{b}"], 2 * t)
                        twice = lambda a: a.unsqueeze(2).to_broadcast([P, H, 2, HD])
                        v.tensor_tensor(q_split[b, k][:, :, 2:4, :], twice(qk_f[b, k][:, 0:H, :]), q_split[b, k][:, :, 0:2, :], ALU.subtract)
                        v.tensor_tensor(k_split[b, k][:, :, 1:4:2, :], twice(qk_f[b, k][:, H:2 * H, :]), k_split[b, k][:, :, 0:3:2, :],
                                        ALU.subtract).then_inc(q[f"split_{b}"], 1)

            def att(b):
                per = TB * 2
                for g in range(G):
                    bg = b * G + g
                    yield per * (g + 1) + 1
                    dve.wait_ge(q["pv_mm"], (bg + 1) * per)
                    v.tensor_copy(o_raw[:, :], bk(4 + bg % 2)).then_inc(q["oraw_s"], 1)
                    yield per * (g + 1) + 4
                    dve.wait_ge(q["den_mm"], bg + 1)
                    yield from link(v.reciprocal(den_r[:, :], bk(4 + bg % 2)))
                    if b >= 1 and g == 0:
                        dve.wait_ge(q["wo_mm"], b)
                    yield from publish(v.tensor_tensor(o_T[:, g, :], o_raw[:, :], den_r[:, :], ALU.mult), q["oT_s"], bg + 1)

            def mobius_step(b, k_gate, x_old, x_new, step, half, end, done=None):
                r = lambda k: sml[:, k, b * TB:(b + 1) * TB]
                w = w_sb[b]
                gate = ada[:, b, k_gate, :].unsqueeze(1).to_broadcast([P, TB, D])
                yield from tt(w[:, :, :], a_sb[:, b, :, :], gate, ALU.mult)
                for t in range(TB):
                    xt = x_old[:, b * TB + t, :]
                    for i, (k, l, m) in enumerate(((10, a_sb[:, b, t, :], a_sb[:, b, t, :]), (11, w[:, t, :], w[:, t, :]),
                                    (12, xt, w[:, t, :]), (13, xt, xt))):
                        last = v.tensor_tensor_reduce(out=junk[:, b, 4 * t + i, :], in0=l, in1=m, scale=1.0, scalar=0.0,
                                                      op0=ALU.mult, op1=ALU.add, accum_out=sml[:, k, b * TB + t:b * TB + t + 1])
                yield from link(last)
                two = lambda k: sml[:, k:k + 2, b * TB:(b + 1) * TB]
                yield from ts(two(14), two(10), EPS * EPS, ALU.max)
                yield from rsqrt((two(16), two(14), root_f[:, b, 0:2 * TB].rearrange("p (k t) -> p k t", k=2)))
                v.tensor_scalar(r(19), r(13), -1.0, 1.0, ALU.mult, ALU.add)
                v.tensor_scalar(r(18), r(16), MAX_ARTANH, 1.0, ALU.mult, ALU.min)
                yield from tt(r(11), r(15), r(17), ALU.mult)
                yield half
                v.tensor_tensor(r(8), r(11), r(18), ALU.mult).then_inc(q[f"tanh_in_{b}"], 1)
                yield half, end, 9
                dve.wait_ge(q[f"tanh_s_{b}"], step)
                v.tensor_tensor(r(15), r(9), r(17), ALU.mult)
                yield from tt(r(11), r(9), r(9), ALU.mult)
                v.scalar_tensor_tensor(r(12), r(12), 2.0, r(15), ALU.mult, ALU.mult)
                yield from tt(r(17), r(13), r(11), ALU.mult)
                v.scalar_tensor_tensor(r(17), r(12), 1.0, r(17), ALU.add, ALU.add)
                v.scalar_tensor_tensor(r(16), r(12), 1.0, r(11), ALU.add, ALU.add)
                yield from tt(r(13), r(19), r(15), ALU.mult)
                yield from ts(r(14), r(17), EPS, ALU.max)
                yield from link(v.reciprocal(r(18), r(14)))
                v.tensor_tensor(r(12), r(16), r(18), ALU.mult)
                yield from tt(r(13), r(13), r(18), ALU.mult)
                for t in range(TB):
                    last = v.tensor_scalar(w[:, t, :], w[:, t, :], sml[:, 13, b * TB + t:b * TB + t + 1], None, ALU.mult)
                yield from link(last)
                for t in range(TB):
                    last = v.scalar_tensor_tensor(x_new[:, b * TB + t, :], x_old[:, b * TB + t, :], sml[:, 12, b * TB + t:b * TB + t + 1],
                                                  w[:, t, :], ALU.mult, ALU.add)
                if done is None:
                    yield from link(last)
                else:
                    yield from publish(last, done, b + 1)

            def post(b):
                yield 5, 11, 13
                dve.wait_ge(q["rope_s"], 4 * DEPTH)
                dve.wait_ge(q["a_s"], b + 1)
                yield from mobius_step(b, 2, x_in, x_mid, 1, 11, 15)
                yield 15, 19.15, 14
                yield from moments(x_mid, b * TB, TB)
                yield from inverse_std(b, b * TB, TB, 19.15, 28)
                yield from modulate(x_mid, b, 4, 3)
                for t in range(TB):
                    last = v.tensor_scalar(h_mod[:, b * TB + t, :], h_mod[:, b * TB + t, :], sml[:, 7, b * TB + t:b * TB + t + 1], None, ALU.mult)
                last.then_inc(q["h2_s"], 1)

                yield Z, Z + 4, 10
                dve.wait_ge(q["ffw_in"], 16 * 9)
                dve.wait_ge(q["zsq_mm"], b + 1)
                tiles = slice(b * TB, (b + 1) * TB)
                yield from ts(sml[:, 6, tiles], bank[:, post_bank(b), 0:TB], EPS * EPS, ALU.max)
                yield from rsqrt((sml[:, 7, tiles], sml[:, 6, tiles], root_f[:, b, 0:TB]))
                yield from ts(sml[:, 7, tiles], sml[:, 7, tiles], MAX_ARTANH, ALU.mult, 1.0, ALU.min)
                yield Z + 4, Z + 11.98, 14
                dve.wait_ge(q["z2_mm"], b + 1)
                for t in range(TB):
                    last = v.scalar_tensor_tensor(a_sb[:, b, t, :], bank[:, post_bank(b) + 1, t * P:(t + 1) * P], sml[:, 7, b * TB + t:b * TB + t + 1],
                                                  b_f2_sb[:, :], ALU.mult, ALU.add)
                yield from publish(last, q["z2_used"], b + 1)
                yield from mobius_step(b, 5, x_mid, xr, 2, Z + 11.98, Z + 16, q["x2_s"])

            def rope_part(l, b):
                m = l * B + b
                for u in range(TB // 2):
                    for t in (2 * u, 2 * u + 1):
                        yield 1 + t + 0.333, 1 + t + 2.9 - 2, 4
                        n = b * TB + t
                        i = m * TB + t
                        if m == 0 and t == 0:
                            dve.wait_ge(q["x2_s"], 1)
                        dve.wait_ge(q["lsq_s"], 2 * (i + 1))
                        v.tensor_reduce(norm_sq[:, n, :], qk_sq[:, i % 2, :].rearrange("p (h d) -> p h d", d=LD),
                                        AXX, ALU.add).then_inc(q["lred_s"], 1)
                        yield
                        if i >= 4:
                            dve.wait_ge(q["lqkT_mm"], i - 3)
                        for k in range(2):
                            last = v.tensor_tensor(qk_rot[:, i % 4, k * INNER:(k + 1) * INNER].rearrange("p (h d) -> p h d", d=LD),
                                                   qk_raw[:, i % 2, k * INNER:(k + 1) * INNER].rearrange("p (h d) -> p h d", d=LD),
                                                   rope_l[:, l, k, t, :].unsqueeze(1).to_broadcast([P, LH, LD]), ALU.mult)
                        yield from link(last)
                        dve.wait_ge(q["lc_s"], i + 1)
                        yield from publish(v.tensor_tensor(qk_rot[:, i % 4, :], qk_rot[:, i % 4, :], qk_cross[:, i % 2, :], ALU.add), q["lx_s"], i + 1)
                    yield 2 * u + 3, 2 * u + 3.96, 13
                    dve.wait_ge(q["lred_s"], m * TB + 2 * u + 2)
                    pair = lambda a: a[:, b * TB + 2 * u:b * TB + 2 * u + 2, :].rearrange("p t h -> p (t h)")
                    yield from ts(pair(norm_sq), pair(norm_sq), 1e-24, ALU.max)
                    yield from rsqrt((pair(norm_r), pair(norm_sq), root_l[:, :]))
                    for t in (2 * u, 2 * u + 1):
                        i = m * TB + t
                        to = qk_rot[:, i % 4, :].rearrange("p (h d) -> p h d", d=LD)
                        yield from publish(v.tensor_tensor(to, to, norm_r[:, b * TB + t, :].unsqueeze(2).to_broadcast([P, 2 * LH, LD]), ALU.mult),
                                           q["lrot_s"], i + 1)

            def windows(l, b):
                m = l * B + b
                for w in range(NB + 5):
                    if w < NB:
                        yield w
                        j = m * NB + w
                        dve.wait_ge(q["ls_mm"], j + 1)
                        S4 = bk(j % 2).rearrange("p (r c) -> p r c", r=PAIRS)
                        yield from link(v.tensor_reduce(row_max[:, j % 2, :], S4, AXX, ALU.max))
                        if j >= 2:
                            dve.wait_ge(q["lp_s"], j - 1)
                        v.tensor_tensor(s_rel[:, j % 2, :, :], S4, row_max[:, j % 2, :].unsqueeze(2).to_broadcast([P, PAIRS, P]),
                                        ALU.subtract).then_inc(q["lrel_s"], 1)
                    if w >= 6 and w % 2 == 0:
                        yield w
                        i = m * TB + (w - 6) // 2
                        n = b * TB + (w - 6) // 2
                        dve.wait_ge(q["lwo_mm"], i + 1)
                        v.tensor_tensor(xr[:, n, :], xr[:, n, :], bank[:, 4, 2 * P:3 * P], ALU.add).then_inc(q["lx1_s"], 1)
                    if 3 <= w <= NB + 2:
                        yield w + 0.31
                        j = m * NB + w - 3
                        dve.wait_ge(q["lpv_mm"], j + 1)
                        O4 = bk(3, PAIRS * (LD + 1)).rearrange("p (r d) -> p r d", r=PAIRS)
                        if j >= 2:
                            dve.wait_ge(q["loT_mm"], j - 1)
                        yield from link(v.reciprocal(o_den[:, j % 2, :], O4[:, :, LD]))
                        v.tensor_tensor(o_loc[:, j % 2, :, :], O4[:, :, 0:LD], o_den[:, j % 2, :].unsqueeze(2).to_broadcast([P, PAIRS, LD]),
                                        ALU.mult).then_inc(q["lo_s"], 1)

            def feed(l, b):
                m = l * B + b
                ns = range(b * TB, (b + 1) * TB)
                yield 0, 3, 16
                dve.wait_ge(q["lx1_s"], (m + 1) * TB)
                dve.wait_ge(q["lsh_mm"], m + 1)
                up = lambda n: bank[:, 5, n % TB * 64:n % TB * 64 + 64]
                for n in ns:
                    v.bn_stats(bn6[:, n, 0:6], xr[:, n, 0:64])
                    last = v.bn_stats(bn6[:, n, 6:12], up(n))
                yield from link(last)
                for n in ns:
                    last = v.bn_aggr(mean_var[:, n, :], bn6[:, n, :])
                yield from link(last)
                yield from ts(sml[:, 1, 0:TB], mean_var[:, b * TB:(b + 1) * TB, 1], 1e-5, ALU.add)
                yield from rsqrt((sml[:, 5, 0:TB], sml[:, 1, 0:TB], root_f[:, 0, 0:TB]))
                for n in ns:
                    r = sml[:, 5, n % TB:n % TB + 1]
                    v.tensor_scalar(h_mod[:, n, 0:64], xr[:, n, 0:64], mean_var[:, n, 0:1], r, ALU.subtract, ALU.mult)
                    last = v.tensor_scalar(h_mod[:, n, 64:128], up(n), mean_var[:, n, 0:1], r, ALU.subtract, ALU.mult)
                yield from publish(last, q["lhn_s"], m + 1)
                for c, (c0, cn) in enumerate(HC):
                    yield 3 + 2.5 + 0.5 * c
                    i = m * NH + c
                    if c == 0:
                        dve.wait_ge(q["lqkT_mm"], min((m + 2) * TB, DEPTH * T))
                    dve.wait_ge(q["lgate_s"], i + 1)
                    dve.wait_ge(q["la_mm"], i + 1)
                    v.scalar_tensor_tensor(ff_T[0:cn, b, c, :], bank[0:cn, 5 + c, :], b1_sb[0:cn, l, 0, c:c + 1],
                                           gate_T[0:cn, c, :], ALU.add, ALU.mult).then_inc(q["lff_s"], 1)
                yield 7
                xb = xr[:, b * TB:(b + 1) * TB, :]
                yield from tt(xb, xb, b2_sb[:, l, :].unsqueeze(1).to_broadcast([P, TB, D]), ALU.add)
                yield 7 + 1
                dve.wait_ge(q["lf2_mm"], m + 1)
                yield from publish(v.tensor_tensor(xb, xb, bk(5).rearrange("p (t d) -> p t d", d=D), ALU.add), q["lx2_s"], m + 1)
                if m == DEPTH * B - 1:
                    v.tensor_tensor(xr[:, :, :], xr[:, :, :], x_in[:, :, :], ALU.add).then_inc(q["lx2_s"], 1)

            schedule(pre, att, post, rope_part, windows, feed)


_INS = ['x', 'cond_1024', 'L0_cond_w_q', 'L0_cond_b_q', 'L0_cond_w_k', 'L0_cond_b_k', 'L0_cond_w_v', 'L0_cond_b_v',
        'L0_cond_w_o', 'L0_cond_b_o', 'L0_cond_w_f1', 'L0_cond_b_f1', 'L0_cond_w_f2', 'L0_cond_b_f2', 'L0_cond_w_ada',
        'L0_cond_b_ada', 'L0_ffn_wqkv', 'L0_ffn_q_scale', 'L0_ffn_k_scale', 'L0_ffn_wo', 'L0_ffn_ln_g', 'L0_ffn_ln_b',
        'L0_ffn_w1', 'L0_ffn_b1', 'L0_ffn_w2', 'L0_ffn_b2']


def _constants(S, depth_head, window):
    import numpy as np
    f = np.float32
    half = np.arange(0, depth_head, 2, dtype=f)
    inv = (f(1.0) / f(10000.0) ** (half / f(depth_head))).astype(f)
    t = np.arange(S, dtype=f)
    fr = (t[:, None] * inv[None, :]).astype(f)
    fr = np.concatenate([fr, fr], -1)
    base = (half + f(0.4 * depth_head)) / f(1.4 * depth_head)
    power = (t - S // 2) / f(window // 2)
    sc = (base[None, :] ** power[:, None]).astype(f)
    sc = np.concatenate([sc, sc], -1)
    cos, sin = np.cos(fr).astype(f), np.sin(fr).astype(f)
    sign = np.concatenate([-np.ones(depth_head // 2, f), np.ones(depth_head // 2, f)])
    rope = np.stack([cos * sc, cos / sc, sign * sin * sc, sign * sin / sc]).astype(f)
    i = np.arange(128)[:, None] % window
    j = np.arange(2 * window)[None, :]
    band = np.where((j >= i) & (j <= i + window), f(0), f(-1e30)).astype(f)
    first = np.where(j >= window, band, f(-1e30)).astype(f)
    masks = np.stack([band, first])
    eye = np.eye(128, dtype=f)
    shift = np.zeros((2, 128, 128), f)
    shift[0, np.arange(127), np.arange(1, 128)] = 1
    shift[1, 127, 0] = 1
    pick = np.zeros((128, 128), f)
    for r in range(128):
        pick[32 * (r // 32) + 8, r] = 1
    return {'rope': rope, 'masks': masks, 'eye': eye, 'shift': shift, 'denom_pick': pick}


def kernel(**inputs):
    import numpy as _np
    import concourse.bacc as _bacc
    from concourse import mybir as _mybir
    from concourse.bass_utils import run_bass_kernel_spmd as _run

    nc = _bacc.Bacc("TRN2", target_bir_lowering=False, num_devices=1)
    arrays, args = {}, []
    values = {n: inputs[n] for n in _INS}
    shape = values['x'].shape
    values['cond_1024'] = _np.asarray(values['cond_1024']).T
    values['L0_cond_b_f1'] = _np.asarray(values['L0_cond_b_f1']).reshape(-1, 128).T
    values['L0_ffn_ln_g'] = _np.asarray(values['L0_ffn_ln_g']).T
    values['L0_ffn_ln_b'] = _np.asarray(values['L0_ffn_ln_b']).T
    b1 = _np.asarray(values['L0_ffn_b1'])
    depth, hid = b1.shape[0], b1.shape[1] // 2
    b1 = _np.pad(b1.reshape(depth, 2, hid), ((0, 0), (0, 0), (0, -hid % 128)))
    values['L0_ffn_b1'] = b1.reshape(depth * 2 * (b1.shape[2] // 128), 128).T
    values.update(_constants(shape[1], values['L0_ffn_q_scale'].shape[1], 64))
    for name, a in values.items():
        a = _np.ascontiguousarray(a)
        arrays[f"in_{name}"] = a
        args.append(nc.dram_tensor(f"in_{name}", a.shape, _mybir.dt.from_np(a.dtype), kind="ExternalInput").ap())
    args.append(nc.dram_tensor("out_0", shape, _mybir.dt.float32, kind="ExternalOutput").ap())
    adaln_ffn_kernel(nc, *args)
    r = _run(nc, [arrays], core_ids=[0])
    return r.results[0]["out_0"]
```
